# Optimizing a Trainium2 kernel written in Bass

```python
import numpy as np
import jax
import jax.numpy as jnp

def _softmax(x, axis=-1):
    return jax.nn.softmax(x, axis=axis)

def _gelu(x):
    return jax.nn.gelu(x, approximate=True)

def _silu(x):
    return jax.nn.silu(x)

def _sigmoid(x):
    return jax.nn.sigmoid(x)

def _layernorm(x, axis=-1, eps=1e-05):
    m = jnp.mean(x, axis=axis, keepdims=True)
    v = jnp.var(x, axis=axis, keepdims=True)
    return (x - m) / jnp.sqrt(v + eps)

def _scatter_add(tgt, idx, src, axis=0):
    return tgt.at[idx].add(src)

def _segment_sum(src, seg, n):
    return jax.ops.segment_sum(src, seg, n)
kernel_name = 'mk_seq_preln_d2_jaxref_r4_8d7461'

def setup_inputs(seed: int=0):
    np.random.seed(seed)
    _w = jnp.asarray

    def _L0_attn_setup():
        import jax, jax.numpy as jnp
        import numpy as np
        N, T, D = (2, 1024, 256)
        H, E, L = (8, 4, 32)
        DK, DV = (64, 64)

        def _pscan(A, Xv, Y0):
            Ae = jnp.broadcast_to(A[..., None], Xv.shape)
            Xv = Xv.at[..., 0, :].add(A[..., 0, None] * Y0)

            def op(c1, c2):
                a1, x1 = c1
                a2, x2 = c2
                return (a1 * a2, a2 * x1 + x2)
            _, Y = jax.lax.associative_scan(op, (Ae, Xv), axis=3)
            return Y
        key = jax.random.key(seed)
        ks = jax.random.split(key, 8)

        def randw(k, *d):
            return jax.random.normal(k, d, dtype=jnp.float32) / np.float32(np.sqrt(d[-1]))
        return {'X': jax.random.normal(ks[0], (N, T, D), dtype=jnp.float32), 'w_G': randw(ks[1], H, E, D), 'b_G': jnp.full((H, E), -float(H) ** 0.5, dtype=jnp.float32), 'w_K': randw(ks[2], H, DK, D), 'w_V': randw(ks[3], H, DV, D), 'w_Q': randw(ks[4], H, DK, D), 'w_O': randw(ks[5], DV * H, D), 'init_K_rec': randw(ks[6], E, L, DK), 'init_V_rec': randw(ks[7], E, L, DV)}
    _L0_attn_in = _L0_attn_setup()

    def _L0_ffn_setup():
        import jax, jax.numpy as jnp
        import numpy as np
        NH, NKV, E, K = (16, 4, 8, 2)
        CAP_FACTOR = 1.25
        LN_EPS = 1e-05

        def _layer_norm(x, w, b):
            mu = jnp.mean(x, axis=-1, keepdims=True)
            var = jnp.mean(jnp.square(x - mu), axis=-1, keepdims=True)
            return (x - mu) * jax.lax.rsqrt(var + LN_EPS) * w + b
        key = jax.random.key(seed)
        ks = jax.random.split(key, 6)
        S, B, H, F = (512, 1, 256, 512)
        HD = H // NH
        qkv_out = NKV * (NH // NKV + 2) * HD
        f32 = jnp.float32
        return {'hidden_states': jax.random.normal(ks[0], (S, B, H), f32), 'ln1_weight': jnp.ones((H,), f32), 'ln1_bias': jnp.zeros((H,), f32), 'ln2_weight': jnp.ones((H,), f32), 'ln2_bias': jnp.zeros((H,), f32), 'qkv_weight': jax.random.normal(ks[1], (qkv_out, H), f32) * 0.02, 'proj_weight': jax.random.normal(ks[2], (H, H), f32) * 0.02, 'router_weight': jax.random.normal(ks[3], (H, E), f32) * 0.02, 'moe_w1': jax.random.normal(ks[4], (E, H, F), f32) * 0.02, 'moe_w2': jax.random.normal(ks[5], (F and E, F, H), f32)[:E] * 0.02 if False else jax.random.normal(ks[5], (E, F, H), f32) * 0.02}
    _L0_ffn_in = _L0_ffn_setup()

    def _L1_attn_setup():
        import jax, jax.numpy as jnp
        import numpy as np
        EPS = 1e-05

        def xpos_rotate(x, offset=0, conjugate=False):
            b, s, h, dh = x.shape
            expoent = jnp.arange(0, dh, 2, dtype=jnp.float32) / dh
            angle = 10.0 ** (-4.0 * expoent)
            if conjugate:
                angle = -angle
            pos = jnp.arange(offset, s + offset, dtype=jnp.float32)
            nangle = pos[:, None] * angle[None, :]
            sin = jnp.sin(nangle)[None, :, None, :]
            cos = jnp.cos(nangle)[None, :, None, :]
            x0 = x[..., 0::2]
            x1 = x[..., 1::2]
            rot = jnp.stack([x0 * cos - x1 * sin, x0 * sin + x1 * cos], axis=-1)
            return rot.reshape(b, s, h, dh)

        def decay_mask(nseq, scale):
            idx = jnp.arange(nseq)
            diff = idx[:, None] - idx[None, :]
            mask = (diff >= 0).astype(scale.dtype)
            diff_c = jnp.maximum(diff, 0).astype(scale.dtype)
            logd = diff_c[None, :, :] * jnp.log(scale)[:, None, None]
            return jnp.exp(logd) * mask[None, :, :]

        def group_norm(R, gamma, beta, nheads):
            b, s, d = R.shape
            dh = d // nheads
            Rg = R.reshape(b, s, nheads, dh)
            mu = jnp.mean(Rg, axis=-1, keepdims=True)
            var = jnp.var(Rg, axis=-1, keepdims=True)
            Rn = (Rg - mu) * jax.lax.rsqrt(var + EPS)
            Rn = Rn * gamma.reshape(1, 1, nheads, dh) + beta.reshape(1, 1, nheads, dh)
            return Rn.reshape(b, s, d)
        key = jax.random.key(seed)
        ks = jax.random.split(key, 7)
        b, s, d, h = (2, 512, 256, 16)
        dh = d // h
        x = jax.random.normal(ks[0], (b, s, d), dtype=jnp.float32)
        std_qkv = float(np.sqrt(2.0 / (dh + d)))
        std_o = float(np.sqrt(2.0 / (d + d)))
        WQ = jax.random.normal(ks[1], (h, dh, d), dtype=jnp.float32) * std_qkv
        WK = jax.random.normal(ks[2], (h, dh, d), dtype=jnp.float32) * std_qkv
        WV = jax.random.normal(ks[3], (h, dh, d), dtype=jnp.float32) * std_qkv
        WO = jax.random.normal(ks[4], (d, d), dtype=jnp.float32) * std_o
        gamma = jnp.ones((d,), dtype=jnp.float32)
        beta = jnp.zeros((d,), dtype=jnp.float32)
        return {'x': x, 'WQ': WQ, 'WK': WK, 'WV': WV, 'WO': WO, 'gamma': gamma, 'beta': beta}
    _L1_attn_in = _L1_attn_setup()

    def _L1_ffn_setup():
        import jax, jax.numpy as jnp
        import numpy as np
        DIM = 256
        HIDDEN = 768
        SCALE = 1.0 / 127.0

        def _dequant(w_int, dtype):
            return w_int.astype(dtype) * jnp.asarray(SCALE, dtype)
        key = jax.random.key(seed)
        k_x, k_g, k_u, k_d = jax.random.split(key, 4)
        x = jax.random.normal(k_x, (4, 512, DIM), dtype=jnp.float32)
        w_gate = jax.random.randint(k_g, (HIDDEN, DIM), -127, 128, dtype=jnp.int32)
        w_up = jax.random.randint(k_u, (HIDDEN, DIM), -127, 128, dtype=jnp.int32)
        w_down = jax.random.randint(k_d, (DIM, HIDDEN), -127, 128, dtype=jnp.int32)
        return {'x': x, 'w_gate': w_gate, 'w_up': w_up, 'w_down': w_down}
    _L1_ffn_in = _L1_ffn_setup()
    _d = {'L0_attn_X': _L0_attn_in['X'], 'L0_attn_w_G': _L0_attn_in['w_G'], 'L0_attn_b_G': _L0_attn_in['b_G'], 'L0_attn_w_K': _L0_attn_in['w_K'], 'L0_attn_w_V': _L0_attn_in['w_V'], 'L0_attn_w_Q': _L0_attn_in['w_Q'], 'L0_attn_w_O': _L0_attn_in['w_O'], 'L0_attn_init_K_rec': _L0_attn_in['init_K_rec'], 'L0_attn_init_V_rec': _L0_attn_in['init_V_rec'], 'L0_ffn_ln1_weight': _L0_ffn_in['ln1_weight'], 'L0_ffn_ln1_bias': _L0_ffn_in['ln1_bias'], 'L0_ffn_ln2_weight': _L0_ffn_in['ln2_weight'], 'L0_ffn_ln2_bias': _L0_ffn_in['ln2_bias'], 'L0_ffn_qkv_weight': _L0_ffn_in['qkv_weight'], 'L0_ffn_proj_weight': _L0_ffn_in['proj_weight'], 'L0_ffn_router_weight': _L0_ffn_in['router_weight'], 'L0_ffn_moe_w1': _L0_ffn_in['moe_w1'], 'L0_ffn_moe_w2': _L0_ffn_in['moe_w2'], 'L1_attn_WQ': _L1_attn_in['WQ'], 'L1_attn_WK': _L1_attn_in['WK'], 'L1_attn_WV': _L1_attn_in['WV'], 'L1_attn_WO': _L1_attn_in['WO'], 'L1_attn_gamma': _L1_attn_in['gamma'], 'L1_attn_beta': _L1_attn_in['beta'], 'L1_ffn_w_gate': _L1_ffn_in['w_gate'], 'L1_ffn_w_up': _L1_ffn_in['w_up'], 'L1_ffn_w_down': _L1_ffn_in['w_down']}
    _x0 = _d['L0_attn_X']
    _d['L0_attn_X'] = jax.random.normal(jax.random.fold_in(jax.random.key(seed), 1), (8, 512, 256), dtype=_x0.dtype)
    del _x0
    return _d

def reference(L0_attn_X, L0_attn_w_G, L0_attn_b_G, L0_attn_w_K, L0_attn_w_V, L0_attn_w_Q, L0_attn_w_O, L0_attn_init_K_rec, L0_attn_init_V_rec, L0_ffn_ln1_weight, L0_ffn_ln1_bias, L0_ffn_ln2_weight, L0_ffn_ln2_bias, L0_ffn_qkv_weight, L0_ffn_proj_weight, L0_ffn_router_weight, L0_ffn_moe_w1, L0_ffn_moe_w2, L1_attn_WQ, L1_attn_WK, L1_attn_WV, L1_attn_WO, L1_attn_gamma, L1_attn_beta, L1_ffn_w_gate, L1_ffn_w_up, L1_ffn_w_down):

    def _L0_attn_ref(X, w_G, b_G, w_K, w_V, w_Q, w_O, init_K_rec, init_V_rec):
        import jax, jax.numpy as jnp
        import numpy as np
        N, T, D = (2, 1024, 256)
        H, E, L = (8, 4, 32)
        DK, DV = (64, 64)

        def _pscan(A, Xv, Y0):
            Ae = jnp.broadcast_to(A[..., None], Xv.shape)
            Xv = Xv.at[..., 0, :].add(A[..., 0, None] * Y0)

            def op(c1, c2):
                a1, x1 = c1
                a2, x2 = c2
                return (a1 * a2, a2 * x1 + x2)
            _, Y = jax.lax.associative_scan(op, (Ae, Xv), axis=3)
            return Y
        n, t, _ = X.shape
        t_pad = ((t - 1) // L + 1) * L
        Xp = jnp.pad(X, ((0, 0), (0, t_pad - t), (0, 0)))
        G = jax.nn.sigmoid(jnp.einsum('ntd,hed->nhet', Xp, w_G) + b_G[None, :, :, None])
        K = jnp.einsum('ntc,hdc->nhtd', Xp, w_K)
        V = jnp.einsum('ntc,hdc->nhtd', Xp, w_V)
        A = 1.0 - jnp.minimum(G.sum(axis=1), 1.0)
        gK = jnp.einsum('nhet,nhtd->netd', G, K)
        gV = jnp.einsum('nhet,nhtd->netd', G, V)
        tc = t_pad // L
        A = A.reshape(n, E, L, tc)
        gK = gK.reshape(n, E, L, tc, DK)
        gV = gV.reshape(n, E, L, tc, DV)
        iK = jnp.broadcast_to(init_K_rec[None], (n, E, L, DK))
        iV = jnp.broadcast_to(init_V_rec[None], (n, E, L, DV))
        nK = _pscan(A, gK, iK).reshape(n, E, t_pad, DK)
        nV = _pscan(A, gV, iV).reshape(n, E, t_pad, DV)
        recK = jnp.concatenate([iK, nK], axis=2)
        recV = jnp.concatenate([iV, nV], axis=2)
        idx = 1 + jnp.arange(t_pad)[:, None] + jnp.arange(L)[None, :]
        uk = recK[:, :, idx]
        uv = recV[:, :, idx]
        Q = jnp.einsum('ntc,hdc->nhtd', Xp, w_Q)
        scores = jnp.einsum('nhtd,netld->nhtel', Q, uk) / jnp.float32(np.sqrt(DK))
        probs = jax.nn.softmax(scores.reshape(n, H, t_pad, E * L), axis=-1).reshape(scores.shape)
        Y = jnp.einsum('nhtel,netld->nthd', probs, uv).reshape(n, t_pad, H * DV)
        return (Y @ w_O)[:, :t]

    def _L0_ffn_ref(hidden_states, ln1_weight, ln1_bias, ln2_weight, ln2_bias, qkv_weight, proj_weight, router_weight, moe_w1, moe_w2):
        import jax, jax.numpy as jnp
        import numpy as np
        NH, NKV, E, K = (16, 4, 8, 2)
        CAP_FACTOR = 1.25
        LN_EPS = 1e-05

        def _layer_norm(x, w, b):
            mu = jnp.mean(x, axis=-1, keepdims=True)
            var = jnp.mean(jnp.square(x - mu), axis=-1, keepdims=True)
            return (x - mu) * jax.lax.rsqrt(var + LN_EPS) * w + b
        S, B, H = hidden_states.shape
        HD = H // NH
        q_per_kv = NH // NKV
        ln1 = _layer_norm(hidden_states, ln1_weight, ln1_bias)
        qkv = jnp.einsum('sbh,oh->sbo', ln1, qkv_weight)
        qkv = qkv.reshape(S, B, NKV, (q_per_kv + 2) * HD)
        q = qkv[..., :q_per_kv * HD].reshape(S, B, NH, HD)
        k = qkv[..., q_per_kv * HD:(q_per_kv + 1) * HD]
        v = qkv[..., (q_per_kv + 1) * HD:]
        qb = jnp.transpose(q, (1, 2, 0, 3)).reshape(B, NKV, q_per_kv, S, HD)
        kb = jnp.transpose(k, (1, 2, 0, 3))
        vb = jnp.transpose(v, (1, 2, 0, 3))
        scale = 1.0 / np.sqrt(HD).astype(np.float32)
        scores = jnp.einsum('bgqsd,bgtd->bgqst', qb, kb) * scale
        causal = jnp.tril(jnp.ones((S, S), bool))
        scores = jnp.where(causal, scores, jnp.finfo(scores.dtype).min)
        attn = jax.nn.softmax(scores, axis=-1)
        ao = jnp.einsum('bgqst,bgtd->bgqsd', attn, vb)
        ao = ao.reshape(B, NH, S, HD)
        ao = jnp.transpose(ao, (2, 0, 1, 3)).reshape(S, B, H)
        proj = jnp.einsum('sbh,oh->sbo', ao, proj_weight)
        h1 = hidden_states + proj
        ln2 = _layer_norm(h1, ln2_weight, ln2_bias)
        x = ln2.reshape(-1, H)
        N = x.shape[0]
        logits = x @ router_weight
        probs = jax.nn.softmax(logits, axis=-1)
        top_p, top_i = jax.lax.top_k(probs, K)
        top_p = top_p / jnp.sum(top_p, axis=-1, keepdims=True)
        exp_idx = top_i.reshape(-1)
        exp_p = top_p.reshape(-1)
        order = jnp.argsort(exp_idx, stable=True)
        sorted_exp = exp_idx[order]
        counts = jnp.bincount(exp_idx, length=E)
        offsets = jnp.concatenate([jnp.zeros((1,), counts.dtype), jnp.cumsum(counts)[:-1]])
        within = jnp.arange(N * K) - offsets[sorted_exp]
        cap = int(np.ceil(N * K / E * CAP_FACTOR))
        T = E * cap
        valid = within < cap
        dst = jnp.where(valid, sorted_exp * cap + within, T)
        padded_tokens = jnp.zeros((T, H), x.dtype).at[dst].set(x[order // K], mode='drop')
        padded_probs = jnp.zeros((T,), exp_p.dtype).at[dst].set(exp_p[order], mode='drop')
        padded_tid = jnp.zeros((T,), jnp.int32).at[dst].set((order // K).astype(jnp.int32), mode='drop')
        xt = padded_tokens.reshape(E, cap, H)
        fc1 = jax.nn.gelu(jnp.einsum('ech,ehf->ecf', xt, moe_w1))
        fc2 = jnp.einsum('ecf,efh->ech', fc1, moe_w2).reshape(T, H)
        weighted = fc2 * padded_probs[:, None]
        moe_out = jnp.zeros((N, H), hidden_states.dtype).at[padded_tid].add(weighted)
        return h1 + moe_out.reshape(S, B, H)

    def _L1_attn_ref(x, WQ, WK, WV, WO, gamma, beta):
        import jax, jax.numpy as jnp
        import numpy as np
        EPS = 1e-05

        def xpos_rotate(x, offset=0, conjugate=False):
            b, s, h, dh = x.shape
            expoent = jnp.arange(0, dh, 2, dtype=jnp.float32) / dh
            angle = 10.0 ** (-4.0 * expoent)
            if conjugate:
                angle = -angle
            pos = jnp.arange(offset, s + offset, dtype=jnp.float32)
            nangle = pos[:, None] * angle[None, :]
            sin = jnp.sin(nangle)[None, :, None, :]
            cos = jnp.cos(nangle)[None, :, None, :]
            x0 = x[..., 0::2]
            x1 = x[..., 1::2]
            rot = jnp.stack([x0 * cos - x1 * sin, x0 * sin + x1 * cos], axis=-1)
            return rot.reshape(b, s, h, dh)

        def decay_mask(nseq, scale):
            idx = jnp.arange(nseq)
            diff = idx[:, None] - idx[None, :]
            mask = (diff >= 0).astype(scale.dtype)
            diff_c = jnp.maximum(diff, 0).astype(scale.dtype)
            logd = diff_c[None, :, :] * jnp.log(scale)[:, None, None]
            return jnp.exp(logd) * mask[None, :, :]

        def group_norm(R, gamma, beta, nheads):
            b, s, d = R.shape
            dh = d // nheads
            Rg = R.reshape(b, s, nheads, dh)
            mu = jnp.mean(Rg, axis=-1, keepdims=True)
            var = jnp.var(Rg, axis=-1, keepdims=True)
            Rn = (Rg - mu) * jax.lax.rsqrt(var + EPS)
            Rn = Rn * gamma.reshape(1, 1, nheads, dh) + beta.reshape(1, 1, nheads, dh)
            return Rn.reshape(b, s, d)
        b, s, d = x.shape
        h, dh, _ = WQ.shape
        Q = jnp.einsum('bsd,hud->bshu', x, WQ)
        K = jnp.einsum('bsd,hud->bshu', x, WK)
        V = jnp.einsum('bsd,hud->bshu', x, WV)
        Q = xpos_rotate(Q)
        K = xpos_rotate(K)
        QK = jnp.einsum('bihd,bjhd->bhij', Q, K)
        scale = 1.0 - 2.0 ** (-5.0 - jnp.arange(h, dtype=jnp.float32))
        D = decay_mask(s, scale)
        QKD = QK * D[None]
        R = jnp.einsum('bhij,bjhd->bihd', QKD, V)
        R = R.reshape(b, s, d)
        R = group_norm(R, gamma, beta, h)
        y = R @ WO
        return y

    def _L1_ffn_ref(x, w_gate, w_up, w_down):
        import jax, jax.numpy as jnp
        import numpy as np
        DIM = 256
        HIDDEN = 768
        SCALE = 1.0 / 127.0

        def _dequant(w_int, dtype):
            return w_int.astype(dtype) * jnp.asarray(SCALE, dtype)
        wg = _dequant(w_gate, x.dtype)
        wu = _dequant(w_up, x.dtype)
        wd = _dequant(w_down, x.dtype)
        gate = jnp.einsum('bsd,hd->bsh', x, wg)
        up = jnp.einsum('bsd,hd->bsh', x, wu)
        h = jax.nn.silu(gate) * up
        return jnp.einsum('bsh,dh->bsd', h, wd)
    x = L0_attn_X
    x = x + _L0_attn_ref(_layernorm(x, axis=-1), L0_attn_w_G, L0_attn_b_G, L0_attn_w_K, L0_attn_w_V, L0_attn_w_Q, L0_attn_w_O, L0_attn_init_K_rec, L0_attn_init_V_rec)
    x = x + _L0_ffn_ref(_layernorm(x, axis=-1), L0_ffn_ln1_weight, L0_ffn_ln1_bias, L0_ffn_ln2_weight, L0_ffn_ln2_bias, L0_ffn_qkv_weight, L0_ffn_proj_weight, L0_ffn_router_weight, L0_ffn_moe_w1, L0_ffn_moe_w2)
    x = x + _L1_attn_ref(_layernorm(x, axis=-1), L1_attn_WQ, L1_attn_WK, L1_attn_WV, L1_attn_WO, L1_attn_gamma, L1_attn_beta)
    x = x + _L1_ffn_ref(_layernorm(x, axis=-1), L1_ffn_w_gate, L1_ffn_w_up, L1_ffn_w_down)
    return x

_drawn_inputs = setup_inputs


def setup_inputs(seed=0):
    import zlib

    import numpy as np

    out = dict(_drawn_inputs(seed))
    spreads = {'L0_attn_b_G': (-2.8284270763397217, 0.2),
     'L0_ffn_ln1_weight': (1.0, 0.6),
     'L0_ffn_ln1_bias': (0.0, 0.763),
     'L0_ffn_ln2_weight': (1.0, 0.6),
     'L0_ffn_ln2_bias': (0.0, 0.426),
     'L1_attn_gamma': (1.0, 0.2),
     'L1_attn_beta': (0.0, 0.1)}
    factors = {'L0_attn_init_K_rec': 8.0, 'L0_attn_init_V_rec': 5.735}
    for name, (base, spread) in spreads.items():
        noise = np.random.default_rng([zlib.crc32(name.encode()), seed]).standard_normal(out[name].shape)
        drawn = base * np.exp(spread * noise) if base else spread * noise
        out[name] = jnp.asarray(drawn.astype(out[name].dtype))
    for name, factor in factors.items():
        out[name] = (out[name] * factor).astype(out[name].dtype)
    return out
```

```python
from contextlib import ExitStack

import numpy as np

import concourse.bass as bass
from concourse import mybir

F32 = mybir.dt.float32
BF16 = mybir.dt.bfloat16
I32 = mybir.dt.int32
U32 = mybir.dt.uint32
ALU = mybir.AluOpType
ACT = mybir.ActivationFunctionType
AX = mybir.AxisListType

P = 128
NB, T, D = 8, 512, 256
NT = NB * T // P
TS = T // P
KC = D // P
EPS = 1e-5
H0, E0, L0, DK = 8, 4, 32, 64
WIN = L0 + T
NH, NKV, HD = 16, 4, 16
QG = NH // NKV
QKVW = NKV * (QG + 2) * HD
NE, FE = 8, 512
CAP = 1280
SLOTS = NE * CAP
H1, DH = 16, 16
FF = 768
QSCALE = 1.0 / 127.0
NEG = -1e30


def bc(ap, shape):
    return ap.broadcast_to(shape)


class Chain:

    def __init__(self, eng, sem, base=0):
        self.eng, self.sem, self.base, self.n = eng, sem, base, 0

    def step(self, ins):
        self.n += 1
        ins.then_inc(self.sem, 1)
        self.eng.wait_ge(self.sem, self.base + self.n)

    def mark(self, ins):
        self.n += 1
        ins.then_inc(self.sem, 1)
        return self.n

    def after(self, n):
        self.eng.wait_ge(self.sem, self.base + n)


def pass_gate(k, eng):
    eng.sem_inc(k.gates_passed, 1)


class Kernel:
    def __init__(self, nc, a, out, upto):
        self.nc, self.a, self.out, self.upto = nc, a, out, upto
        self.n = 0

    def sb(self, ctx, name, shape, dt=F32):
        return ctx.enter_context(self.nc.sbuf_tensor(name, shape, dt))

    def ps(self, ctx, name, shape, dt=F32):
        return ctx.enter_context(self.nc.psum_tensor(name, shape, dt))

    def sem(self, ctx, name):
        return ctx.enter_context(self.nc.semaphore(name))


def build(nc, a, out, upto=4):
    k = Kernel(nc, a, out, upto)
    with ExitStack() as ctx:
        k.X = k.sb(ctx, "X", [P, NT, D])
        k.BST = k.sb(ctx, "BST", [P, NT, 6])
        k.mean = k.sb(ctx, "mean", [P, NT])
        k.rstd = k.sb(ctx, "rstd", [P, NT])
        k.ident = k.sb(ctx, "ident", [P, P])
        k.ones = k.sb(ctx, "ones", [P, P])
        k.mhalf = k.sb(ctx, "mhalf", [P, NT])
        k.stored = k.sem(ctx, "out_stored")
        k.gates_passed = k.sem(ctx, "gates_passed")
        k.xt_dram = nc.dram_tensor("expert_in", (SLOTS + P, D), F32, kind="Internal").ap()
        k.y_dram = nc.dram_tensor("expert_out", (SLOTS + P, D), F32, kind="Internal").ap()
        setup(k)
        if upto >= 1:
            with ExitStack() as c1:
                k.Rec = k.sb(c1, "Rec", [P, NB, E0, WIN])
                k.XTall = k.sb(c1, "XTall", [P, KC, NB * T])
                ln_stats(k, "s1")
                recurrence(k)
                window_attention(k)
        if upto >= 2:
            with ExitStack() as c2:
                k.HS = k.sb(c2, "HS", [P, NT, D])
                k.slots = k.sb(c2, "slots", [P, NT, 2], U32)
                k.prob = k.sb(c2, "prob", [P, NT, 2])
                with ExitStack() as c3:
                    k.QKV = k.sb(c3, "QKV", [P, NT, QKVW])
                    k.AO = k.sb(c3, "AO", [P, NT, D])
                    ln_stats(k, "s2")
                    position_qkv(k)
                    position_attention(k)
                    route(k)
                experts(k)
                combine(k)
        if upto >= 3:
            ln_stats(k, "s3")
            retention(k)
        if upto >= 4:
            ln_stats(k, "s4")
            swiglu(k)
        else:
            store_x(k)


def setup(k):
    nc, a = k.nc, k.a
    with ExitStack() as ctx:
        parts = [k.sem(ctx, f"x_part{n}") for n in range(2)]
        const = k.sem(ctx, "const_loaded")
        stats = k.sem(ctx, "x_stats")
        ones_set = k.sem(ctx, "ones_set")
        zero = k.sb(ctx, "zero_rows", [P, 10, D])
        zero_set = k.sem(ctx, "zero_set")
        zero_stored = k.sem(ctx, "zero_stored")
        block = ctx.enter_context(nc.Block())

        @block.sync
        def _(sp):
            for n in range(NB):
                sp.dma_start(k.X[:, n * TS:(n + 1) * TS, :],
                             a["x"][n * T:(n + 1) * T, :].rearrange("(i p) c -> p i c", p=P)).then_inc(parts[n // 4], 16)
            sp.dma_start(k.ident[:, :], a["ident"]).then_inc(const, 16)
            sp.wait_ge(const, 16)

        @block.scalar
        def _(act):
            act.wait_ge(zero_set, 1)
            for e in range(NE):
                act.dma_start(k.xt_dram[e * CAP:(e + 1) * CAP, :].rearrange("(i p) c -> p i c", p=P),
                              zero[:, :, :]).then_inc(zero_stored, 16)
            act.dma_start(k.y_dram[SLOTS:SLOTS + P, :], zero[:, 0, :]).then_inc(zero_stored, 16)
            act.wait_ge(zero_stored, 16 * (NE + 1))

        @block.gpsimd
        def _(pool):
            nc.gpsimd.memset(k.mhalf[:, :], -0.5).then_inc(ones_set, 1)
            nc.gpsimd.memset(k.ones[:, :], 1.0).then_inc(ones_set, 1)

        @block.vector
        def _(dve):
            nc.vector.memset(zero[:, :, :], 0.0).then_inc(zero_set, 1)
            for n in range(2):
                dve.wait_ge(parts[n], 64)
                for t in range(n * NT // 2, (n + 1) * NT // 2):
                    nc.vector.bn_stats(k.BST[:, t, :], k.X[:, t, :]).then_inc(stats, 1)


def stats_steps(nc, chain, bst, mean, var, tmp, ready):
    me, mo, ve, vo = bst[:, :, 1], bst[:, :, 4], bst[:, :, 2], bst[:, :, 5]
    m1 = chain.mark(nc.vector.tensor_tensor(mean, me, mo, ALU.add))
    m2 = chain.mark(nc.vector.tensor_tensor(tmp, me, mo, ALU.subtract))
    m3 = chain.mark(nc.vector.tensor_tensor(var, ve, vo, ALU.add))
    chain.after(m1)
    chain.mark(nc.vector.tensor_scalar(mean, mean, 0.5, None, ALU.mult))
    chain.after(m2)
    chain.step(nc.vector.tensor_tensor(tmp, tmp, tmp, ALU.mult))
    chain.after(m3)
    chain.step(nc.vector.scalar_tensor_tensor(var, tmp, D / 4.0, var, ALU.mult, ALU.add))
    nc.vector.tensor_scalar(var, var, 1.0 / D, EPS, ALU.mult, ALU.add).then_inc(ready, 1)


def ln_stats(k, tag):
    nc = k.nc
    with ExitStack() as ctx:
        tmp = k.sb(ctx, tag + "tmp", [P, NT])
        var = k.sb(ctx, tag + "var", [P, NT])
        steps = k.sem(ctx, tag + "_steps")
        var_ready = k.sem(ctx, tag + "_var")
        root = k.sem(ctx, tag + "_root")
        block = ctx.enter_context(nc.Block())

        @block.vector
        def _(dve):
            chain = Chain(dve, steps)
            stats_steps(nc, chain, k.BST[:, :, :], k.mean[:, :], var[:, :], tmp[:, :], var_ready)

        @block.gpsimd
        def _(pool):
            pool.wait_ge(var_ready, 1)
            nc.gpsimd.tensor_tensor(k.rstd[:, :], var[:, :], k.mhalf[:, :], ALU.pow).then_inc(root, 1)


def store_x(k):
    nc = k.nc
    with ExitStack() as ctx:
        block = ctx.enter_context(nc.Block())

        @block.sync
        def _(sp):
            sp.dma_start(k.out.rearrange("(i p) c -> p i c", p=P), k.X[:, :, :]).then_inc(k.stored, 16)
            sp.wait_ge(k.stored, 16)


def normalise(k, dst, tile):
    return k.nc.vector.tensor_scalar(dst, k.X[:, bass.ds(tile, 1), :], k.mean[:, bass.ds(tile, 1)],
                                     k.rstd[:, bass.ds(tile, 1)], ALU.subtract, ALU.mult)


def recurrence(k):
    nc, a = k.nc, k.a
    HE = H0 * E0
    with ExitStack() as ctx:
        wg = k.sb(ctx, "wg", [P, KC, HE])
        bg = k.sb(ctx, "bg", [1, HE])
        wkv = k.sb(ctx, "wkv", [P, KC, H0 * P])
        ikv = k.sb(ctx, "ikv", [P, E0, L0])
        XN = k.sb(ctx, "XN1", [P, TS, D])
        XT = k.sb(ctx, "XT1", [P, KC, T])
        eg = k.sb(ctx, "eg", [P, TS, HE])
        G = k.sb(ctx, "G", [P, TS, HE])
        A = k.sb(ctx, "A", [P, TS, E0])
        acc = k.sb(ctx, "acc", [P, TS, E0, P])
        gT = k.sb(ctx, "gT", [P, E0, T])
        AT = k.sb(ctx, "AT", [P, E0, T])
        seed = k.sb(ctx, "seed", [P, E0, L0])
        psT = k.ps(ctx, "psT", [P, KC, 2 * P])
        psG = k.ps(ctx, "psG", [P, 512])
        psKV = [[k.ps(ctx, f"psKV{s}{h}", [P, 4, P]) for h in range(2)] for s in range(2)]
        psR = k.ps(ctx, "psR", [P, T])
        psA = k.ps(ctx, "psA", [P, T])
        weights = k.sem(ctx, "r_weights")
        xn_ready, xn_free = k.sem(ctx, "r_xn_ready"), k.sem(ctx, "r_xn_free")
        t_ready, t_evac = k.sem(ctx, "r_t_ready"), k.sem(ctx, "r_t_evac")
        g_ready, g_exp, g_gate = k.sem(ctx, "r_g_ready"), k.sem(ctx, "r_g_exp"), k.sem(ctx, "r_g_gate")
        kv_ready, acc_step = k.sem(ctx, "r_kv_ready"), k.sem(ctx, "r_acc_step")
        ra_ready, ra_evac = k.sem(ctx, "r_ra_ready"), k.sem(ctx, "r_ra_evac")
        acc_free, scan_done = k.sem(ctx, "r_acc_free"), k.sem(ctx, "r_scan_done")
        xt_copied = k.sem(ctx, "r_xt_copied")
        dstep = k.sem(ctx, "r_dstep")
        init_set = k.sem(ctx, "r_init_set")
        block = ctx.enter_context(nc.Block())

        @block.sync
        def _(sp):
            sp.dma_start(wg[:, :, :], a["wg"].rearrange("(k p) n -> p k n", p=P)).then_inc(weights, 16)
            sp.dma_start(bg[:, :], a["bg"]).then_inc(weights, 16)
            sp.dma_start(wkv[:, :, :], a["wkv"].rearrange("(k p) n -> p k n", p=P)).then_inc(weights, 16)
            sp.dma_start(ikv[:, :, :], a["ikv"]).then_inc(weights, 16)

        @block.gpsimd
        def _(pool):
            pool.wait_ge(weights, 64)
            for n in range(NB):
                nc.gpsimd.tensor_copy(k.Rec[:, n, :, 0:L0], ikv[:, :, :]).then_inc(init_set, 1)
            pool.sem_inc(xt_copied, 1)
            with pool.Fori(0, NB) as i:
                pool.wait_ge(t_evac, i * 2 + 3)
                nc.gpsimd.tensor_copy(k.XTall[:, :, bass.ds(i * T, T)], XT[:, :, :]).then_inc(xt_copied, 1)

        @block.tensor
        def _(pe):
            pe.sem_inc(xn_free, TS)
            pe.sem_inc(kv_ready, 4)
            pe.sem_inc(acc_free, 1)
            pe.wait_ge(weights, 64)
            with pe.Fori(0, NB) as i:
                for v in range(2):
                    pe.wait_ge(t_evac, i * 2 + v + 1)
                    for u in (2 * v, 2 * v + 1):
                        pe.wait_ge(xn_ready, i * TS + u + 1)
                        for c in range(KC):
                            mm = pe.transpose(psT[:, c, (u % 2) * P:(u % 2 + 1) * P],
                                              XN[:, u, c * P:(c + 1) * P], k.ident[:, :])
                        mm.then_inc(xn_free, 1)
                    pe.wait_ge(xn_free, TS + i * TS + 2 * v + 2)
                    pe.sem_inc(t_ready, 1)
                pe.wait_ge(t_evac, i * 2 + 3)
                pe.wait_ge(g_exp, i + 1)
                for u in range(TS):
                    for c in range(KC):
                        pe.matmul(psG[:, u * HE:(u + 1) * HE], XT[:, c, u * P:(u + 1) * P], wg[:, c, :],
                                  start=(c == 0 and u == 0), stop=False, skip_group_check=True)
                    mm = pe.matmul(psG[:, u * HE:(u + 1) * HE], k.ones[0:1, :], bg[0:1, :],
                                   start=False, stop=(u == TS - 1), skip_group_check=True)
                mm.then_inc(g_ready, 1)
                for u in range(TS):
                    pe.wait_ge(acc_step, i * P + u * 32 + 32)
                    for half in range(2):
                        for c in range(KC):
                            mm = pe.matmul(psKV[u % 2][half][:, :, :], XT[:, c, u * P:(u + 1) * P],
                                           wkv[:, c, half * 512:(half + 1) * 512], start=(c == 0), stop=(c == KC - 1))
                    mm.then_inc(kv_ready, 1)
                pe.wait_ge(acc_step, i * P + P + 64)
                pe.wait_ge(g_gate, i + 2)
                for e in range(E0):
                    pe.wait_ge(ra_evac, (i * E0 + e) * 2 + 1)
                    for u in range(TS):
                        mm = pe.transpose(psR[:, u * P:(u + 1) * P], acc[:, u, e, :], k.ident[:, :])
                    mm.then_inc(ra_ready, 1)
                    pe.wait_ge(ra_evac, (i * E0 + e) * 2 + 2)
                    for u in range(TS):
                        mm = pe.transpose(psA[:, u * P:(u + 1) * P], bc(A[:, u, e:e + 1], [P, P]), k.ident[:, :])
                    mm.then_inc(ra_ready, 1)
                pe.wait_ge(ra_ready, (i * E0 + E0) * 2)
                pe.sem_inc(acc_free, 1)

        @block.scalar
        def _(act):
            act.sem_inc(t_evac, 1)
            act.sem_inc(g_exp, 1)
            act.sem_inc(ra_evac, 2)
            with act.Fori(0, NB) as i:
                for v in range(2):
                    act.wait_ge(t_ready, i * 2 + v + 1)
                    act.wait_ge(kv_ready, i * 4 + 2 * v + 2)
                    act.wait_ge(xt_copied, i + 1)
                    nc.scalar.copy(XT[:, :, v * 2 * P:(v + 1) * 2 * P], psT[:, :, :]).then_inc(t_evac, 1)
                act.wait_ge(g_ready, i + 1)
                act.wait_ge(g_gate, i + 1)
                nc.scalar.activation(eg[:, :, :], psG[:, 0:TS * HE].rearrange("p (u n) -> p u n", u=TS), ACT.Exp, scale=-1.0).then_inc(g_exp, 1)
                act.wait_ge(scan_done, i + 1)
                for e in range(E0):
                    act.wait_ge(ra_ready, (i * E0 + e) * 2 + 1)
                    nc.scalar.copy(gT[:, e, :], psR[:, :]).then_inc(ra_evac, 1)
                    act.wait_ge(ra_ready, (i * E0 + e) * 2 + 2)
                    nc.scalar.copy(AT[:, e, :], psA[:, :]).then_inc(ra_evac, 1)

        @block.vector
        def _(dve):
            dve.sem_inc(g_gate, 1)
            dve.sem_inc(acc_step, 64)
            dve.sem_inc(scan_done, 1)
            dve.wait_ge(weights, 64)
            NST = 7
            with dve.Fori(0, NB) as i:
                for u in range(TS):
                    dve.wait_ge(xn_free, i * TS + u + 1)
                    normalise(k, XN[:, u, :], i * TS + u).then_inc(xn_ready, 1)
                ch = Chain(dve, dstep, i * NST)
                dve.wait_ge(g_exp, i + 2)
                ch.step(nc.vector.tensor_scalar(G[:, :, :], eg[:, :, :], 1.0, None, ALU.add))
                ch.step(nc.vector.reciprocal(G[:, :, :], G[:, :, :]))
                dve.wait_ge(acc_free, i + 1)
                ch.step(nc.vector.tensor_reduce(A[:, :, :], G[:, :, :].rearrange("p u (h e) -> p u e h", e=E0),
                                                AX.X, ALU.add))
                ch.step(nc.vector.tensor_scalar(A[:, :, :], A[:, :, :], 1.0, -1.0, ALU.min, ALU.mult))
                nc.vector.tensor_scalar(A[:, :, :], A[:, :, :], 1.0, None, ALU.add).then_inc(g_gate, 1)
                for u in range(TS):
                    dve.wait_ge(kv_ready, 4 + i * TS + u + 1)
                    for h in range(H0):
                        for e in range(E0):
                            g = G[:, u, h * E0 + e:h * E0 + e + 1]
                            kv = psKV[u % 2][h // 4][:, h % 4, :]
                            if h == 0:
                                ins = nc.vector.tensor_scalar(acc[:, u, e, :], kv, g, None, ALU.mult)
                            else:
                                dve.wait_ge(acc_step, i * P + (u * 32 + h * E0 + e - 3 + 64))
                                ins = nc.vector.scalar_tensor_tensor(acc[:, u, e, :], kv, g, acc[:, u, e, :],
                                                                     ALU.mult, ALU.add)
                            ins.then_inc(acc_step, 1)
                dve.wait_ge(ra_evac, i * 8 + 10)
                gs = gT[:, :, :].rearrange("p e (l c) -> p e l c", c=T // L0)[:, :, :, 0]
                As = AT[:, :, :].rearrange("p e (l c) -> p e l c", c=T // L0)[:, :, :, 0]
                ch.step(nc.vector.tensor_tensor(seed[:, :, :], As, ikv[:, :, :], ALU.mult))
                ch.step(nc.vector.tensor_tensor(gs, gs, seed[:, :, :], ALU.add))
                ch.step(nc.vector.memset(As, 0.0))
                for e in range(E0):
                    n = nc.vector.tensor_tensor_scan(k.Rec[:, bass.ds(i, 1), e, L0:WIN].rearrange("p a t -> p (a t)"), AT[:, e, :], gT[:, e, :], 0.0,
                                                     ALU.mult, ALU.add)
                n.then_inc(scan_done, 1)
                assert ch.n == NST


def window_attention(k):
    nc, a = k.nc, k.a
    QB = 32
    NQ = T // QB
    KW = 2 * L0
    scale = 1.0 / 8.0
    NG = (NQ + 1 + 3) // 4
    with ExitStack() as ctx:
        wq = k.sb(ctx, "wq", [P, KC, H0 * DK])
        wo = k.sb(ctx, "wo", [P, 4, D])
        mask_f = k.sb(ctx, "mask_f", [QB, E0 * KW])
        mask = k.sb(ctx, "mask", [QB, E0 * KW], BF16)
        sel_f = k.sb(ctx, "sel_f", [QB, P])
        sel = k.sb(ctx, "sel", [QB, P], BF16)
        R = k.sb(ctx, "R", [P, WIN, E0])
        QT = k.sb(ctx, "QT", [DK, 2, NQ, 4, QB])
        V = k.sb(ctx, "V", [P, NQ + 1, DK])
        mx = k.sb(ctx, "mx", [P, 2, 2])
        nm = k.sb(ctx, "nm", [P, 2, 2])
        sums = k.sb(ctx, "sums", [P, 4, 2])
        rs = k.sb(ctx, "rs", [P, 2])
        probs = k.sb(ctx, "probs", [P, 2, 2, E0 * KW])
        PT = k.sb(ctx, "PT", [P, 2, 2, 2, P])
        Y = k.sb(ctx, "Y", [P, 2, 2, DK])
        YT = k.sb(ctx, "YT", [P, 4, T])
        psS = [k.ps(ctx, f"psS{s}", [P, 2, E0 * KW]) for s in range(2)]
        psP = [k.ps(ctx, f"psP{s}", [P, 2, 2, P]) for s in range(2)]
        psO = k.ps(ctx, "psO", [P, 2, DK])
        psY = k.ps(ctx, "psY", [P, 4, QB])
        psQ = k.ps(ctx, "psQ", [P, T])
        psV = k.ps(ctx, "psV", [P, 4, P])
        weights, casts = k.sem(ctx, "w_weights"), k.sem(ctx, "w_casts")
        r_ready, r_free = k.sem(ctx, "w_r_ready"), k.sem(ctx, "w_r_free")
        q_ready, q_evac = k.sem(ctx, "w_q_ready"), k.sem(ctx, "w_q_evac")
        v_ready, v_evac = k.sem(ctx, "w_v_ready"), k.sem(ctx, "w_v_evac")
        s_ready, m_ready, e_done = k.sem(ctx, "w_s_ready"), k.sem(ctx, "w_m_ready"), k.sem(ctx, "w_e_done")
        p_ready, p_evac = k.sem(ctx, "w_p_ready"), k.sem(ctx, "w_p_evac")
        o_ready, o_evac = k.sem(ctx, "w_o_ready"), k.sem(ctx, "w_o_evac")
        y_ready, y_evac = k.sem(ctx, "w_y_ready"), k.sem(ctx, "w_y_evac")
        z_ready, z_added = k.sem(ctx, "w_z_ready"), k.sem(ctx, "w_z_added")
        dstep = k.sem(ctx, "w_dstep")
        block = ctx.enter_context(nc.Block())

        @block.sync
        def _(sp):
            sp.dma_start(wq[:, :, :], a["wq"].rearrange("(k p) n -> p k n", p=P)).then_inc(weights, 16)
            sp.dma_start(wo[:, :, :], a["wo"].rearrange("(k p) n -> p k n", p=P)).then_inc(weights, 16)
            sp.dma_start(mask_f[:, :], a["mask"]).then_inc(weights, 16)
            sp.dma_start(sel_f[:, :], a["sel"]).then_inc(weights, 16)

        @block.gpsimd
        def _(pool):
            with pool.Fori(0, NB) as i:
                pool.wait_ge(r_free, i + 1)
                nc.gpsimd.tensor_copy(R[:, :, :].rearrange("p t e -> p e t"),
                                      k.Rec[:, bass.ds(i, 1), :, :].rearrange("p a e t -> p (a e) t")).then_inc(r_ready, 1)

        @block.tensor
        def _(pe):
            pe.sem_inc(r_free, 1)
            pe.sem_inc(p_ready, 2)
            pe.sem_inc(o_ready, 2)
            pe.sem_inc(y_ready, 2)
            pe.sem_inc(z_ready, 4)
            pe.wait_ge(weights, 64)
            pe.wait_ge(casts, 2)

            def scores(i, q):
                pe.wait_ge(e_done, (i * NQ + q) * 2 + 2)
                for hg in range(2):
                    o = psS[q % 2][:, hg, :]
                    pe.matmul(o, QT[:, hg, q, :, :].rearrange("d h t -> d (h t)"),
                              R[0:DK, q * QB:q * QB + KW, :].rearrange("d t e -> d (t e)"),
                              start=(hg == 0), stop=False, skip_group_check=True)
                    mm = pe.matmul(o, sel[:, :], mask[:, :], start=False, stop=(hg == 1), skip_group_check=True)
                mm.then_inc(s_ready, 1)

            def transposes(i, q):
                pe.wait_ge(e_done, (i * NQ + q) * 2 + 2 + 4)
                pe.wait_ge(p_evac, i * NQ + q + 1)
                for hg in range(2):
                    for kt in range(2):
                        mm = pe.transpose(psP[q % 2][:, hg, kt, :], probs[:, q % 2, hg, kt * P:(kt + 1) * P], k.ident[:, :])
                mm.then_inc(p_ready, 1)

            def values(i, q):
                pe.wait_ge(p_evac, i * NQ + q + 1 + 2)
                pe.wait_ge(o_evac, i * NQ + q + 1)
                for hg in range(2):
                    for kt in range(2):
                        mm = pe.matmul(psO[:, hg, :], PT[:, q % 2, hg, kt, :], V[:, q + kt, :],
                                       start=(hg == 0 and kt == 0), stop=(hg == 1 and kt == 1), skip_group_check=True)
                mm.then_inc(o_ready, 1)

            def turn(i, q):
                pe.wait_ge(o_evac, i * NQ + q + 1 + 1)
                pe.wait_ge(y_evac, i * NQ + q + 1)
                pe.transpose(psY[:, :, :], Y[:, q % 2, :, :].rearrange("p g d -> p (g d)"),
                             k.ident[:, :]).then_inc(y_ready, 1)

            def project(i, u):
                pe.wait_ge(y_evac, i * NQ + 4 * u + 4 + 1)
                pe.wait_ge(z_added, i * TS + u + 1)
                for c in range(4):
                    mm = pe.matmul(psQ[:, 0:D], YT[:, c, u * P:(u + 1) * P], wo[:, c, :], start=(c == 0), stop=(c == 3))
                mm.then_inc(z_ready, 1)

            with pe.Fori(0, NB) as i:
                pe.wait_ge(r_ready, i + 1)
                pe.wait_ge(z_added, i * TS + 1)
                for m in range(4):
                    pe.wait_ge(q_evac, (i * 4 + m) * 2 + 2)
                    for c in range(KC):
                        mm = pe.matmul(psQ[:, :], wq[:, c, m * P:(m + 1) * P], k.XTall[:, c, bass.ds(i * T, T)],
                                       start=(c == 0), stop=(c == KC - 1))
                    mm.then_inc(q_ready, 1)
                for g in range(NG):
                    pe.wait_ge(v_evac, i * NG + g + 1)
                    for q in range(4 * g, min(4 * g + 4, NQ + 1)):
                        mm = pe.transpose(psV[:, q % 4, :],
                                          R[:, q * QB:(q + 1) * QB, :].rearrange("d t e -> d (t e)"), k.ident[:, :])
                    mm.then_inc(v_ready, 1)
                pe.wait_ge(q_evac, i * 8 + 10)
                pe.wait_ge(v_evac, i * NG + NG + 1)
                for s in range(NQ + 3):
                    if s < NQ:
                        scores(i, s)
                    if 0 <= s - 1 < NQ:
                        transposes(i, s - 1)
                    if 0 <= s - 2 < NQ:
                        values(i, s - 2)
                    if 0 <= s - 3 < NQ:
                        turn(i, s - 3)
                    if s - 4 >= 0 and (s - 4) % 4 == 3:
                        project(i, (s - 4) // 4)
                project(i, TS - 1)
                pe.wait_ge(z_ready, i * TS + TS + 4)
                pe.sem_inc(r_free, 1)

        @block.scalar
        def _(act):
            act.sem_inc(q_evac, 2)
            act.sem_inc(v_evac, 1)
            act.sem_inc(e_done, 4)
            act.sem_inc(y_evac, 1)

            def yevac(i, q):
                act.wait_ge(y_ready, i * NQ + q + 1 + 2)
                act.wait_ge(z_ready, i * TS + q // 4 + 1)
                nc.scalar.copy(YT[:, :, q * QB:(q + 1) * QB], psY[:, :, :]).then_inc(y_evac, 1)

            with act.Fori(0, NB) as i:
                for m in range(4):
                    act.wait_ge(q_ready, i * 4 + m + 1)
                    for r in range(2):
                        nc.scalar.copy(QT[:, m // 2, :, 2 * m % 4 + r, :],
                                       psQ[r * DK:(r + 1) * DK, :].rearrange("d (b t) -> d b t", b=NQ)).then_inc(q_evac, 1)
                for g in range(NG):
                    act.wait_ge(v_ready, i * NG + g + 1)
                    w = min(4, NQ + 1 - 4 * g)
                    nc.scalar.copy(V[:, 4 * g:4 * g + w, :], psV[:, 0:w, DK:P]).then_inc(v_evac, 1)
                for s in range(NQ + 3):
                    if s < NQ:
                        q = s
                        act.wait_ge(m_ready, i * NQ + q + 1)
                        act.wait_ge(p_ready, i * NQ + q + 1)
                        for hg in range(2):
                            nc.scalar.activation(probs[:, q % 2, hg, :], psS[q % 2][:, hg, :], ACT.Exp,
                                                 bias=nm[:, q % 2, hg:hg + 1], scale=scale,
                                                 accum_out=sums[:, q % 4, hg:hg + 1]).then_inc(e_done, 1)
                    if s >= 3:
                        yevac(i, s - 3)

        @block.vector
        def _(dve):
            dve.wait_ge(weights, 64)
            nc.vector.tensor_copy(mask[:, :], mask_f[:, :]).then_inc(casts, 1)
            nc.vector.tensor_copy(sel[:, :], sel_f[:, :]).then_inc(casts, 1)
            dve.sem_inc(p_evac, 2)
            dve.sem_inc(o_evac, 1)
            dve.sem_inc(z_added, 1)
            NST = 2 * NQ + TS

            def add(i, ch, u):
                dve.wait_ge(z_ready, i * TS + u + 1 + 4)
                x = k.X[:, bass.ds(i * TS + u, 1), :].rearrange("p a c -> p (a c)")
                n = ch.mark(nc.vector.tensor_tensor(x, x, psQ[:, 0:D], ALU.add))
                ch.after(n)
                nc.vector.bn_stats(k.BST[:, bass.ds(i * TS + u, 1), :].rearrange("p a c -> p (a c)"), x).then_inc(z_added, 1)

            with dve.Fori(0, NB) as i:
                ch = Chain(dve, dstep, i * NST)
                for s in range(NQ + 2):
                    if s < NQ:
                        q = s
                        dve.wait_ge(s_ready, i * NQ + q + 1)
                        dve.wait_ge(e_done, (i * NQ + q) * 2 + 2)
                        ch.step(nc.vector.tensor_reduce(mx[:, q % 2, :], psS[q % 2][:, :, :], AX.X, ALU.max))
                        nc.vector.tensor_scalar(nm[:, q % 2, :], mx[:, q % 2, :], -scale, None, ALU.mult).then_inc(m_ready, 1)
                    if 0 <= s - 1 < NQ:
                        q = s - 1
                        dve.wait_ge(p_ready, i * NQ + q + 1 + 2)
                        dve.wait_ge(o_ready, i * NQ + q + 1)
                        nc.vector.tensor_copy(PT[:, q % 2, :, :, :], psP[q % 2][:, :, :, :]).then_inc(p_evac, 1)
                    if 0 <= s - 2 < NQ:
                        q = s - 2
                        dve.wait_ge(o_ready, i * NQ + q + 1 + 2)
                        dve.wait_ge(y_ready, i * NQ + q + 1)
                        ch.step(nc.vector.reciprocal(rs[:, :], sums[:, q % 4, :]))
                        nc.vector.tensor_tensor(Y[:, q % 2, :, :], psO[:, :, :], bc(rs[:, :].unsqueeze(2), [P, 2, DK]),
                                                ALU.mult).then_inc(o_evac, 1)
                    if s >= 5 and (s - 5) % 4 == 3:
                        add(i, ch, (s - 5) // 4)
                for u in range((NQ + 1 - 5 - 3) // 4 + 1, TS):
                    add(i, ch, u)
                assert ch.n == NST


def position_qkv(k):
    nc, a = k.nc, k.a
    with ExitStack() as ctx:
        wqkv = k.sb(ctx, "wqkv", [P, KC, QKVW])
        lnw, lnb = k.sb(ctx, "ln1w", [P, KC]), k.sb(ctx, "ln1b", [P, KC])
        bst = k.sb(ctx, "p_bst", [P, TS, 6])
        mean, var = k.sb(ctx, "p_mean", [P, TS]), k.sb(ctx, "p_var", [P, TS])
        tmp, rstd = k.sb(ctx, "p_tmp", [P, TS]), k.sb(ctx, "p_rstd", [P, TS])
        XN = k.sb(ctx, "p_XN", [P, TS, D])
        XT = k.sb(ctx, "p_XT", [P, KC, T])
        psT = [k.ps(ctx, f"p_psT{c}", [P, T]) for c in range(KC)]
        psQ = [k.ps(ctx, f"p_psQ{s}", [P, QKVW]) for s in range(4)]
        weights = k.sem(ctx, "p_weights")
        steps, var_ready, root = k.sem(ctx, "p_steps"), k.sem(ctx, "p_var_ready"), k.sem(ctx, "p_root")
        xn_ready, t_ready, t_evac = k.sem(ctx, "p_xn_ready"), k.sem(ctx, "p_t_ready"), k.sem(ctx, "p_t_evac")
        q_ready, q_evac = k.sem(ctx, "p_q_ready"), k.sem(ctx, "p_q_evac")
        block = ctx.enter_context(nc.Block())

        @block.sync
        def _(sp):
            sp.dma_start(wqkv[:, :, :], a["qkv1"].rearrange("(k p) n -> p k n", p=P)).then_inc(weights, 16)
            sp.dma_start(lnw[:, :], a["ln1w"]).then_inc(weights, 16)
            sp.dma_start(lnb[:, :], a["ln1b"]).then_inc(weights, 16)

        @block.gpsimd
        def _(pool):
            with pool.Fori(0, NB) as i:
                pool.wait_ge(var_ready, i + 1)
                nc.gpsimd.tensor_tensor(rstd[:, :], var[:, :], k.mhalf[:, 0:TS], ALU.pow).then_inc(root, 1)

        @block.vector
        def _(dve):
            NST = TS * 2 + 6
            with dve.Fori(0, NB) as i:
                ch = Chain(dve, steps, i * NST)
                for u in range(TS):
                    hs = k.HS[:, bass.ds(i * TS + u, 1), :].rearrange("p a c -> p (a c)")
                    n = ch.mark(normalise(k, hs, i * TS + u))
                    ch.after(n)
                    pass_gate(k, dve)
                    n = ch.mark(nc.vector.bn_stats(bst[:, u, :], hs))
                ch.after(n)
                stats_steps(nc, ch, bst[:, :, :], mean[:, :], var[:, :], tmp[:, :], var_ready)
                dve.wait_ge(root, i + 1)
                dve.wait_ge(t_ready, i + 1)
                for u in range(TS):
                    hs = k.HS[:, bass.ds(i * TS + u, 1), :].rearrange("p a c -> p (a c)")
                    nc.vector.tensor_scalar(XN[:, u, :], hs, mean[:, u:u + 1], rstd[:, u:u + 1],
                                            ALU.subtract, ALU.mult).then_inc(xn_ready, 1)
                assert ch.n == NST

        @block.tensor
        def _(pe):
            pe.sem_inc(t_ready, 1)
            pe.sem_inc(q_ready, 4)
            pe.wait_ge(weights, 48)
            with pe.Fori(0, NB) as i:
                pe.wait_ge(t_evac, i * 2 + 2)
                for u in range(TS):
                    pe.wait_ge(xn_ready, i * TS + u + 1)
                    for c in range(KC):
                        mm = pe.transpose(psT[c][:, u * P:(u + 1) * P], XN[:, u, c * P:(c + 1) * P], k.ident[:, :])
                mm.then_inc(t_ready, 1)
                pe.wait_ge(t_evac, i * 2 + 4)
                for u in range(TS):
                    pe.wait_ge(q_evac, i * TS + u + 1)
                    for c in range(KC):
                        mm = pe.matmul(psQ[u][:, :], XT[:, c, u * P:(u + 1) * P], wqkv[:, c, :],
                                       start=(c == 0), stop=(c == KC - 1))
                    mm.then_inc(q_ready, 1)

        @block.scalar
        def _(act):
            act.sem_inc(t_evac, 2)
            act.sem_inc(q_evac, 4)
            act.wait_ge(weights, 48)
            with act.Fori(0, NB) as i:
                act.wait_ge(t_ready, i + 2)
                act.wait_ge(q_ready, i * TS + 4)
                for c in range(KC):
                    nc.scalar.activation(XT[:, c, :], psT[c][:, :], ACT.Identity, bias=lnb[:, c:c + 1],
                                         scale=lnw[:, c:c + 1]).then_inc(t_evac, 1)
                for u in range(TS):
                    act.wait_ge(q_ready, i * TS + u + 1 + 4)
                    nc.scalar.copy(k.QKV[:, bass.ds(i * TS + u, 1), :].rearrange("p a c -> p (a c)"),
                                   psQ[u][:, :]).then_inc(q_evac, 1)


def position_attention(k):
    nc = k.nc
    S = NB
    with ExitStack() as ctx:
        sc = k.sb(ctx, "sc", [P, S, S, NH])
        mx = k.sb(ctx, "a_mx", [P, S, NH])
        prod = k.sb(ctx, "prod", [P, 2, S, D])
        steps, made, summed = k.sem(ctx, "a_steps"), k.sem(ctx, "a_made"), k.sem(ctx, "a_summed")
        sub_ready, exp_ready, p_ready = k.sem(ctx, "a_sub"), k.sem(ctx, "a_exp"), k.sem(ctx, "a_p")
        block = ctx.enter_context(nc.Block())

        def row(s, bt):
            return k.QKV[:, bass.ds(bt + s * TS, 1), :].rearrange("p a (g c) -> p (a g) c", g=NKV)

        def fwd(x):
            return x.rearrange("p (g j d) -> p g j d", g=NKV, j=QG)

        @block.gpsimd
        def _(pool):
            with pool.Fori(0, TS) as bt:
                for s in range(S):
                    pool.wait_ge(summed, bt * 16 + s + 1)
                    pass_gate(k, pool)
                    q = row(s, bt)[:, :, 0:QG * HD].rearrange("p g (j d) -> p g j d", j=QG)
                    for t in range(s + 1):
                        kk = row(t, bt)[:, :, QG * HD:QG * HD + HD].unsqueeze(2)
                        ins = nc.gpsimd.tensor_tensor(fwd(prod[:, s % 2, t, :]), q, bc(kk, [P, NKV, QG, HD]), ALU.mult)
                    ins.then_inc(made, 1)
                pool.wait_ge(p_ready, bt + 1)
                for s in range(S):
                    pool.wait_ge(summed, bt * 16 + 8 + s + 1)
                    pass_gate(k, pool)
                    for t in range(s + 1):
                        v = row(t, bt)[:, :, QG * HD + HD:].unsqueeze(2)
                        p = sc[:, s, t, :].rearrange("p (g j) -> p g j", g=NKV).unsqueeze(3)
                        ins = nc.gpsimd.tensor_tensor(fwd(prod[:, s % 2, t, :]), bc(p, [P, NKV, QG, HD]),
                                                      bc(v, [P, NKV, QG, HD]), ALU.mult)
                    ins.then_inc(made, 1)

        @block.scalar
        def _(act):
            with act.Fori(0, TS) as bt:
                act.wait_ge(sub_ready, bt + 1)
                nc.scalar.activation(sc[:, :, :, :], sc[:, :, :, :], ACT.Exp, scale=0.25).then_inc(exp_ready, 1)

        @block.vector
        def _(dve):
            dve.sem_inc(summed, 2)
            NST = 4
            with dve.Fori(0, TS) as bt:
                ch = Chain(dve, steps, bt * NST)
                ch.step(nc.vector.memset(sc[:, :, :, :], NEG))
                for s in range(S):
                    dve.wait_ge(made, bt * 16 + s + 1)
                    nc.vector.tensor_reduce(sc[:, s, 0:s + 1, :], prod[:, s % 2, 0:s + 1, :].rearrange(
                        "p t (h d) -> p t h d", d=HD), AX.X, ALU.add).then_inc(summed, 1)
                dve.wait_ge(summed, bt * 16 + 8 + 2)
                by_t = sc[:, :, :, :].rearrange("p s t h -> p s h t")
                ch.step(nc.vector.tensor_reduce(mx[:, :, :], by_t, AX.X, ALU.max))
                nc.vector.tensor_tensor(by_t, by_t, bc(mx[:, :, :].unsqueeze(3), [P, S, NH, S]),
                                        ALU.subtract).then_inc(sub_ready, 1)
                dve.wait_ge(exp_ready, bt + 1)
                ch.step(nc.vector.tensor_reduce(mx[:, :, :], by_t, AX.X, ALU.add))
                ch.step(nc.vector.reciprocal(mx[:, :, :], mx[:, :, :]))
                nc.vector.tensor_tensor(by_t, by_t, bc(mx[:, :, :].unsqueeze(3), [P, S, NH, S]),
                                        ALU.mult).then_inc(p_ready, 1)
                for s in range(S):
                    dve.wait_ge(made, bt * 16 + 8 + s + 1)
                    nc.vector.tensor_reduce(k.AO[:, bass.ds(bt + s * TS, 1), :].rearrange("p a c -> p (a c)"),
                                            prod[:, s % 2, 0:s + 1, :].rearrange("p t c -> p c t"),
                                            AX.X, ALU.add).then_inc(summed, 1)
                assert ch.n == NST


def route(k):
    nc, a = k.nc, k.a
    with ExitStack() as ctx:
        wp = k.sb(ctx, "wp", [P, KC, D])
        wr = k.sb(ctx, "wr", [P, KC, NE])
        lnw, lnb = k.sb(ctx, "rl_w", [P, KC]), k.sb(ctx, "rl_b", [P, KC])
        before = k.sb(ctx, "before", [P, P])
        iota8 = k.sb(ctx, "iota8", [P, NE])
        AT = k.sb(ctx, "o_AT", [P, KC, T])
        bst = k.sb(ctx, "o_bst", [P, TS, 6])
        mean, var = k.sb(ctx, "o_mean", [P, TS]), k.sb(ctx, "o_var", [P, TS])
        tmp, rstd = k.sb(ctx, "o_tmp", [P, TS]), k.sb(ctx, "o_rstd", [P, TS])
        XN = k.sb(ctx, "o_XN", [P, TS, D])
        XT = k.sb(ctx, "o_XT", [P, KC, T])
        LG = k.sb(ctx, "LG", [P, TS, NE])
        best = k.sb(ctx, "best", [P, TS, 8])
        bidx = k.sb(ctx, "bidx", [P, TS, 8], U32)
        idxf = k.sb(ctx, "idxf", [P, TS, 2])
        oh = k.sb(ctx, "oh", [P, 2, TS, NE])
        both = k.sb(ctx, "both", [P, TS, NE])
        seen = k.sb(ctx, "seen", [P, TS + 1, NE])
        pick = k.sb(ctx, "pick", [P, 2, TS, NE])
        rank = k.sb(ctx, "rank", [P, TS, 2])
        fits = k.sb(ctx, "fits", [P, TS, 2])
        ed = k.sb(ctx, "ed", [P, TS])
        slot = k.sb(ctx, "slot", [P, TS, 2])
        sidx = k.sb(ctx, "sidx", [P, TS, 2], U32)
        psT = [k.ps(ctx, f"o_psT{c}", [P, T]) for c in range(KC)]
        psH = [k.ps(ctx, f"o_psH{s}", [P, D]) for s in range(2)]
        psL = k.ps(ctx, "o_psL", [P, TS, NE])
        psR = k.ps(ctx, "o_psR", [P, TS, NE])
        weights = k.sem(ctx, "o_weights")
        steps, var_ready, root = k.sem(ctx, "o_steps"), k.sem(ctx, "o_var_ready"), k.sem(ctx, "o_root")
        a_ready, a_evac = k.sem(ctx, "o_a_ready"), k.sem(ctx, "o_a_evac")
        h_ready, h_added = k.sem(ctx, "o_h_ready"), k.sem(ctx, "o_h_added")
        xn_ready, t_ready, t_evac = k.sem(ctx, "o_xn_ready"), k.sem(ctx, "o_t_ready"), k.sem(ctx, "o_t_evac")
        l_ready, l_copied = k.sem(ctx, "o_l_ready"), k.sem(ctx, "o_l_copied")
        d_ready, d_exp = k.sem(ctx, "o_d_ready"), k.sem(ctx, "o_d_exp")
        m_ready, r_ready, s_ready = k.sem(ctx, "o_m_ready"), k.sem(ctx, "o_r_ready"), k.sem(ctx, "o_s_ready")
        rows_sent = k.sem(ctx, "o_rows_sent")
        sent = k.sem(ctx, "o_sent")
        block = ctx.enter_context(nc.Block())

        @block.sync
        def _(sp):
            sp.dma_start(wp[:, :, :], a["proj"].rearrange("(k p) n -> p k n", p=P)).then_inc(weights, 16)
            sp.dma_start(wr[:, :, :], a["router"].rearrange("(k p) n -> p k n", p=P)).then_inc(weights, 16)
            sp.dma_start(lnw[:, :], a["ln2w"]).then_inc(weights, 16)
            sp.dma_start(lnb[:, :], a["ln2b"]).then_inc(weights, 16)
            sp.dma_start(before[:, :], a["before"]).then_inc(weights, 16)
            sp.dma_start(iota8[:, :], a["iota8"]).then_inc(weights, 16)

        @block.gpsimd
        def _(pool):
            pool.sem_inc(rows_sent, 1)
            with pool.Fori(0, NB) as i:
                pool.wait_ge(var_ready, i + 1)
                nc.gpsimd.tensor_tensor(rstd[:, :], var[:, :], k.mhalf[:, 0:TS], ALU.pow).then_inc(root, 1)
                pool.wait_ge(s_ready, i + 1)
                pass_gate(k, pool)
                for u in range(TS):
                    for j in range(2):
                        pool.indirect_dma_start(
                            k.xt_dram[:, :], bass.IndirectOffsetOnAxis(ap=sidx[:, u, j:j + 1], axis=0),
                            XN[:, u, :], None, bounds_check=SLOTS - 1, oob_is_err=False,
                        ).then_inc(sent, 16)
                pool.wait_ge(sent, i * (2 * TS * 16) + 2 * TS * 16)
                pool.sem_inc(rows_sent, 1)

        @block.tensor
        def _(pe):
            pe.sem_inc(t_ready, 1)
            pe.wait_ge(weights, 96)
            with pe.Fori(0, NB) as i:
                pe.wait_ge(t_evac, i * 4 + 2)
                for u in range(TS):
                    for c in range(KC):
                        if c == 0:
                            pe.wait_ge(a_ready, i * TS + u + 1)
                        mm = pe.transpose(psT[c][:, u * P:(u + 1) * P], XN[:, u, c * P:(c + 1) * P], k.ident[:, :])
                mm.then_inc(t_ready, 1)
                pe.wait_ge(t_evac, i * 4 + 4)
                for u in range(TS):
                    pe.wait_ge(h_added, i * TS + u + 1)
                    for c in range(KC):
                        mm = pe.matmul(psH[u % 2][:, :], AT[:, c, u * P:(u + 1) * P], wp[:, c, :],
                                       start=(c == 0), stop=(c == KC - 1))
                    mm.then_inc(h_ready, 1)
                for u in range(TS):
                    pe.wait_ge(xn_ready, i * TS + u + 1)
                    for c in range(KC):
                        mm = pe.transpose(psT[c][:, u * P:(u + 1) * P], XN[:, u, c * P:(c + 1) * P], k.ident[:, :])
                mm.then_inc(t_ready, 1)
                pe.wait_ge(t_evac, i * 4 + 6)
                for u in range(TS):
                    for c in range(KC):
                        mm = pe.matmul(psL[:, u, :], XT[:, c, u * P:(u + 1) * P], wr[:, c, :],
                                       start=(u == 0 and c == 0), stop=(u == TS - 1 and c == KC - 1), skip_group_check=True)
                mm.then_inc(l_ready, 1)
                pe.wait_ge(m_ready, i + 1)
                for u in range(TS):
                    pe.matmul(psR[:, u, :], before[:, :], both[:, u, :], start=(u == 0), stop=False, skip_group_check=True)
                    mm = pe.matmul(psR[:, u, :], k.ones[:, :], seen[:, u, :], start=False, stop=(u == TS - 1),
                                   skip_group_check=True)
                mm.then_inc(r_ready, 1)

        @block.scalar
        def _(act):
            act.sem_inc(t_evac, 2)
            act.wait_ge(weights, 96)
            with act.Fori(0, NB) as i:
                for u in range(TS):
                    if u == 0:
                        act.wait_ge(rows_sent, i + 1)
                        act.wait_ge(t_ready, i * 2 + 1)
                    nc.scalar.copy(XN[:, u, :], k.AO[:, bass.ds(i * TS + u, 1), :].rearrange("p a c -> p (a c)")).then_inc(a_ready, 1)
                act.wait_ge(t_ready, i * 2 + 2)
                for c in range(KC):
                    nc.scalar.copy(AT[:, c, :], psT[c][:, :]).then_inc(t_evac, 1)
                act.wait_ge(t_ready, i * 2 + 3)
                for c in range(KC):
                    nc.scalar.activation(XT[:, c, :], psT[c][:, :], ACT.Identity, bias=lnb[:, c:c + 1],
                                         scale=lnw[:, c:c + 1]).then_inc(t_evac, 1)
                act.wait_ge(d_ready, i + 1)
                nc.scalar.activation(ed[:, :], ed[:, :], ACT.Exp).then_inc(d_exp, 1)

        @block.vector
        def _(dve):
            dve.sem_inc(h_added, 2)
            nc.vector.memset(seen[:, :, :], 0.0).then_inc(l_copied, 1)
            dve.wait_ge(l_copied, 1)
            dve.wait_ge(weights, 96)
            NST = 41
            with dve.Fori(0, NB) as i:
                ch = Chain(dve, steps, i * NST)
                for u in range(TS):
                    dve.wait_ge(h_ready, i * TS + u + 1)
                    hs = k.HS[:, bass.ds(i * TS + u, 1), :].rearrange("p a c -> p (a c)")
                    ch.step(nc.vector.tensor_tensor(hs, hs, psH[u % 2][:, :], ALU.add))
                    pass_gate(k, dve)
                    nc.vector.bn_stats(bst[:, u, :], hs).then_inc(h_added, 1)
                dve.wait_ge(h_added, i * TS + TS + 2)
                stats_steps(nc, ch, bst[:, :, :], mean[:, :], var[:, :], tmp[:, :], var_ready)
                dve.wait_ge(root, i + 1)
                dve.wait_ge(t_ready, i * 2 + 2)
                for u in range(TS):
                    hs = k.HS[:, bass.ds(i * TS + u, 1), :].rearrange("p a c -> p (a c)")
                    nc.vector.tensor_scalar(XN[:, u, :], hs, mean[:, u:u + 1], rstd[:, u:u + 1],
                                            ALU.subtract, ALU.mult).then_inc(xn_ready, 1)
                dve.wait_ge(l_ready, i + 1)
                ch.step(nc.vector.tensor_copy(LG[:, :, :], psL[:, :, :]))
                pass_gate(k, dve)
                for u in range(TS):
                    n = ch.mark(nc.vector.max(best[:, u, :], LG[:, u, :]))
                ch.after(n)
                pass_gate(k, dve)
                for u in range(TS):
                    n = ch.mark(nc.vector.max_index(bidx[:, u, :], best[:, u, :], LG[:, u, :]))
                nc.vector.tensor_tensor(ed[:, :], best[:, :, 1], best[:, :, 0], ALU.subtract).then_inc(d_ready, 1)
                ch.after(n)
                ch.step(nc.vector.tensor_copy(idxf[:, :, :], bidx[:, :, 0:2]))
                for j in range(2):
                    n = ch.mark(nc.vector.tensor_tensor(oh[:, j, :, :], bc(iota8[:, :].unsqueeze(1), [P, TS, NE]),
                                                        bc(idxf[:, :, j:j + 1], [P, TS, NE]), ALU.is_equal))
                ch.after(n)
                ch.step(nc.vector.tensor_tensor(both[:, :, :], oh[:, 0, :, :], oh[:, 1, :, :], ALU.add))
                for u in range(TS):
                    ch.step(nc.vector.tensor_tensor(seen[:, u + 1, :], seen[:, u, :], both[:, u, :], ALU.add))
                nc.vector.tensor_copy(idxf[:, :, 0:1], idxf[:, :, 0:1]).then_inc(m_ready, 1)
                dve.wait_ge(d_exp, i + 1)
                ch.step(nc.vector.tensor_scalar(tmp[:, :], ed[:, :], 1.0, None, ALU.add))
                ch.step(nc.vector.reciprocal(tmp[:, :], tmp[:, :]))
                dve.wait_ge(r_ready, i + 1)
                for j in range(2):
                    n = ch.mark(nc.vector.tensor_tensor(pick[:, j, :, :], oh[:, j, :, :], psR[:, :, :], ALU.mult))
                ch.after(n)
                for j in range(2):
                    n = ch.mark(nc.vector.tensor_reduce(rank[:, :, j], pick[:, j, :, :], AX.X, ALU.add))
                ch.after(n)
                ch.mark(nc.vector.tensor_copy(seen[:, 0, :], seen[:, TS, :]))
                ch.step(nc.vector.tensor_scalar(fits[:, :, :], rank[:, :, :], float(CAP), None, ALU.is_lt))
                pr = k.prob[:, bass.ds(i * TS, TS), :]
                ch.step(nc.vector.tensor_tensor(pr[:, :, 0], tmp[:, :], fits[:, :, 0], ALU.mult))
                ch.step(nc.vector.tensor_tensor(tmp[:, :], tmp[:, :], ed[:, :], ALU.mult))
                ch.mark(nc.vector.tensor_tensor(pr[:, :, 1], tmp[:, :], fits[:, :, 1], ALU.mult))
                ch.step(nc.vector.scalar_tensor_tensor(slot[:, :, :], idxf[:, :, :], float(CAP), rank[:, :, :], ALU.mult, ALU.add))
                ch.step(nc.vector.scalar_tensor_tensor(slot[:, :, :], slot[:, :, :], -float(SLOTS), fits[:, :, :], ALU.add, ALU.mult))
                ch.step(nc.vector.tensor_scalar(slot[:, :, :], slot[:, :, :], float(SLOTS), None, ALU.add))
                nc.vector.tensor_copy(k.slots[:, bass.ds(i * TS, TS), :], slot[:, :, :]).then_inc(l_copied, 1)
                nc.vector.tensor_copy(sidx[:, :, :], slot[:, :, :]).then_inc(s_ready, 1)
                assert ch.n == NST, ch.n


def experts(k):
    nc, a = k.nc, k.a
    CH = 2 * P
    NCH = CAP // CH
    with ExitStack() as ctx:
        w1 = k.sb(ctx, "w1", [P, 2, KC, FE])
        w2 = k.sb(ctx, "w2", [P, 2, FE // P, D])
        lnw, lnb = k.sb(ctx, "e_w", [P, KC]), k.sb(ctx, "e_b", [P, KC])
        XE = k.sb(ctx, "XE", [P, 4, 2, D])
        XT = k.sb(ctx, "e_XT", [P, 2, KC, CH])
        HT = k.sb(ctx, "e_HT", [P, 2, FE // P, CH])
        YE = k.sb(ctx, "YE", [P, 2, 2, D])
        psX = k.ps(ctx, "e_psX", [P, KC, CH])
        psH = [[k.ps(ctx, f"e_psH{s}{h}", [P, 2, CH]) for h in range(2)] for s in range(2)]
        psY = [k.ps(ctx, f"e_psY{s}", [P, 2, D]) for s in range(2)]
        consts = k.sem(ctx, "e_consts")
        w_loaded = [k.sem(ctx, f"e_w_loaded{s}") for s in range(2)]
        x_loaded = [k.sem(ctx, f"e_x_loaded{s}") for s in range(2)]
        y_stored = [k.sem(ctx, f"e_y_stored{s}") for s in range(2)]
        x_ready, x_evac = k.sem(ctx, "e_x_ready"), k.sem(ctx, "e_x_evac")
        h_ready, h_done = k.sem(ctx, "e_h_ready"), k.sem(ctx, "e_h_done")
        y_ready, y_evac = k.sem(ctx, "e_y_ready"), k.sem(ctx, "e_y_evac")
        block = ctx.enter_context(nc.Block())
        N = 2 * NCH
        assert N % 2 == 0

        @block.sync
        def _(sp):
            sp.dma_start(lnw[:, :], a["ln2w"]).then_inc(consts, 16)
            sp.dma_start(lnb[:, :], a["ln2b"]).then_inc(consts, 16)
            with sp.Fori(0, NE // 2) as i:
                for s in range(2):
                    sp.wait_ge(y_ready, i * N + (s + 1) * NCH)
                    sp.dma_start(w1[:, s, :, :], a["w1"][bass.ds(i * 2 + s, 1), :, :].rearrange("a (k p) n -> p (a k) n", p=P)).then_inc(w_loaded[s], 16)
                    sp.dma_start(w2[:, s, :, :], a["w2"][bass.ds(i * 2 + s, 1), :, :].rearrange("a (k p) n -> p (a k) n", p=P)).then_inc(w_loaded[s], 16)
                    for c in range(s * NCH, (s + 1) * NCH):
                        sp.wait_ge(x_ready, i * N + c + 1)
                        sp.dma_start(XE[:, c % 2, :, :], k.xt_dram[bass.ds((i * N + c) * CH, CH), :].rearrange(
                            "(j p) n -> p j n", p=P)).then_inc(x_loaded[c % 2], 16)

        @block.tensor
        def _(pe):
            pe.sem_inc(y_ready, N)
            pe.sem_inc(x_ready, 2)

            def turn(i, c):
                pe.wait_ge(x_loaded[c % 2], i * (16 * N // 2) + 16 * (c // 2 + 1))
                pe.wait_ge(x_evac, (i * N + c) * 2 + 2)
                for j in range(2):
                    for kc in range(KC):
                        mm = pe.transpose(psX[:, kc, j * P:(j + 1) * P], XE[:, c % 2, j, kc * P:(kc + 1) * P], k.ident[:, :])
                mm.then_inc(x_ready, 1)

            def hidden(i, c):
                s = c // NCH
                if c % NCH == 0:
                    pe.wait_ge(w_loaded[s], i * 32 + 32)
                pe.wait_ge(x_evac, (i * N + c) * 2 + 4)
                for half in range(2):
                    pe.wait_ge(h_done, (i * N + c) * 2 + half + 1)
                    for m in range(2):
                        for kc in range(KC):
                            f = (half * 2 + m) * P
                            mm = pe.matmul(psH[c % 2][half][:, m, :], w1[:, s, kc, f:f + P], XT[:, c % 2, kc, :],
                                           start=(m == 0 and kc == 0), stop=(m == 1 and kc == KC - 1), skip_group_check=True)
                    mm.then_inc(h_ready, 1)

            def rows(i, c):
                s = c // NCH
                pe.wait_ge(h_done, (i * N + c) * 2 + 2 + 4)
                pe.wait_ge(y_evac, i * N + c + 1)
                for j in range(2):
                    for m in range(FE // P):
                        mm = pe.matmul(psY[c % 2][:, j, :], HT[:, c % 2, m, j * P:(j + 1) * P], w2[:, s, m, :],
                                       start=(j == 0 and m == 0), stop=(j == 1 and m == FE // P - 1), skip_group_check=True)
                mm.then_inc(y_ready, 1)

            with pe.Fori(0, NE // 2) as i:
                turn(i, 0)
                for c in range(N):
                    if c + 1 < N:
                        turn(i, c + 1)
                    hidden(i, c)
                    if c >= 1:
                        rows(i, c - 1)
                rows(i, N - 1)

        @block.scalar
        def _(act):
            act.sem_inc(h_done, 4)
            act.sem_inc(y_stored[0], 16)
            act.sem_inc(y_stored[1], 16)

            def store(i, c):
                act.wait_ge(y_evac, i * N + c + 1 + 2)
                act.dma_start(k.y_dram[bass.ds((i * N + c) * CH, CH), :].rearrange("(j p) n -> p j n", p=P),
                              YE[:, c % 2, :, :]).then_inc(y_stored[c % 2], 16)

            with act.Fori(0, NE // 2) as i:
                for c in range(N):
                    act.wait_ge(y_ready, i * N + c + 1 + N - 2)
                    for half in range(2):
                        act.wait_ge(h_ready, (i * N + c) * 2 + half + 1)
                        nc.scalar.activation(HT[:, c % 2, 2 * half:2 * half + 2, :], psH[c % 2][half][:, :, :],
                                             ACT.Gelu_apprx_tanh).then_inc(h_done, 1)
                    if c >= 2:
                        store(i, c - 2)
                store(i, N - 2)
                store(i, N - 1)
            for s in range(2):
                act.wait_ge(y_stored[s], 16 + 16 * (NE // 2) * (N // 2))

        @block.vector
        def _(dve):
            dve.sem_inc(x_evac, 2)
            dve.sem_inc(y_evac, 2)
            dve.wait_ge(consts, 32)

            def evac_x(i, c):
                dve.wait_ge(x_ready, i * N + c + 1 + 2)
                for kc in range(KC):
                    nc.vector.tensor_scalar(XT[:, c % 2, kc, :], psX[:, kc, :], lnw[:, kc:kc + 1], lnb[:, kc:kc + 1],
                                            ALU.mult, ALU.add).then_inc(x_evac, 1)

            def evac_y(i, c):
                dve.wait_ge(y_ready, i * N + c + 1 + N)
                dve.wait_ge(y_stored[c % 2], i * (16 * N // 2) + 16 * (c // 2 + 1))
                nc.vector.tensor_copy(YE[:, c % 2, :, :], psY[c % 2][:, :, :]).then_inc(y_evac, 1)

            with dve.Fori(0, NE // 2) as i:
                evac_x(i, 0)
                for c in range(N):
                    if c >= 2:
                        evac_y(i, c - 2)
                    if c + 1 < N:
                        evac_x(i, c + 1)
                evac_y(i, N - 2)
                evac_y(i, N - 1)


def combine(k):
    nc = k.nc
    U = 4
    with ExitStack() as ctx:
        cidx = k.sb(ctx, "cidx", [P, U, 2], U32)
        YG = k.sb(ctx, "YG", [P, U, 2, D])
        steps, i_ready, used = k.sem(ctx, "c_steps"), k.sem(ctx, "c_i_ready"), k.sem(ctx, "c_used")
        got = [k.sem(ctx, f"c_got{u}") for u in range(U)]
        block = ctx.enter_context(nc.Block())

        @block.gpsimd
        def _(pool):
            with pool.Fori(0, NT // U) as i:
                for u in range(U):
                    pool.wait_ge(used, i * U + u + 1)
                    nc.gpsimd.tensor_copy(cidx[:, u, :], k.slots[:, bass.ds(i * U + u, 1), :].rearrange("p a j -> p (a j)")).then_inc(i_ready, 1)
                    pool.wait_ge(i_ready, i * U + u + 1)
                    pass_gate(k, pool)
                    for j in range(2):
                        pool.indirect_dma_start(YG[:, u, j, :], None, k.y_dram[:, :],
                                                bass.IndirectOffsetOnAxis(ap=cidx[:, u, j:j + 1], axis=0)).then_inc(got[u], 16)

        @block.vector
        def _(dve):
            dve.sem_inc(used, U)
            with dve.Fori(0, NT // U) as i:
                ch = Chain(dve, steps, i * 3 * U)
                for u in range(U):
                    x = k.X[:, bass.ds(i * U + u, 1), :].rearrange("p a c -> p (a c)")
                    h = k.HS[:, bass.ds(i * U + u, 1), :].rearrange("p a c -> p (a c)")
                    pr = k.prob[:, bass.ds(i * U + u, 1), :].rearrange("p a j -> p (a j)")
                    ch.step(nc.vector.tensor_tensor(x, x, h, ALU.add))
                    dve.wait_ge(got[u], i * 32 + 32)
                    for j in range(2):
                        ch.step(nc.vector.scalar_tensor_tensor(x, YG[:, u, j, :], pr[:, j:j + 1], x, ALU.mult, ALU.add))
                    pass_gate(k, dve)
                    nc.vector.bn_stats(k.BST[:, bass.ds(i * U + u, 1), :].rearrange("p a c -> p (a c)"), x).then_inc(used, 1)


def retention(k):
    nc, a = k.nc, k.a
    t_order = [("x", 0), ("x", 1), ("x", 2), ("r", 0), ("x", 3), ("r", 1), ("r", 2), ("r", 3)]
    with ExitStack() as ctx:
        wqkv = k.sb(ctx, "n_wqkv", [P, KC, 3 * D])
        wo = k.sb(ctx, "n_wo", [P, KC, D])
        gam, bet = k.sb(ctx, "n_gam", [P, KC]), k.sb(ctx, "n_bet", [P, KC])
        rotC, rotS = k.sb(ctx, "rotC", [P, TS, 2 * D]), k.sb(ctx, "rotS", [P, TS, 2 * D])
        causal = k.sb(ctx, "causal", [P, P])
        carry = k.sb(ctx, "carry", [P, KC, P])
        XN = k.sb(ctx, "n_XN", [P, 2, D])
        XT = k.sb(ctx, "n_XT", [P, KC, P])
        m1, m2 = k.sb(ctx, "rot1", [P, 2 * D]), k.sb(ctx, "rot2", [P, 2 * D])
        Qr = k.sb(ctx, "Qr", [P, D])
        Kr = k.sb(ctx, "Kr", [P, 2, D])
        Kpar = [k.sb(ctx, f"Kpar{par}", [P, KC, P]) for par in range(2)]
        V = k.sb(ctx, "n_V", [P, 2, D])
        KT = k.sb(ctx, "n_KT", [P, 2, KC, P])
        QT = k.sb(ctx, "n_QT", [P, KC, P])
        ST = k.sb(ctx, "n_ST", [P, 4, KC, 2, P])
        state = k.sb(ctx, "state", [P, KC, P])
        snew = k.sb(ctx, "snew", [P, KC, P])
        hm, hv = k.sb(ctx, "hm", [P, H1]), k.sb(ctx, "hv", [P, H1])
        hr = k.sb(ctx, "hr", [P, H1])
        cen, sq = k.sb(ctx, "cen", [P, H1, DH]), k.sb(ctx, "sq", [P, H1, DH])
        RN = k.sb(ctx, "RN", [P, H1, DH])
        RT = k.sb(ctx, "n_RT", [P, KC, P])
        psT = k.ps(ctx, "n_psT", [P, KC, P])
        psQK = k.ps(ctx, "n_psQK", [P, 2 * D])
        psV = k.ps(ctx, "n_psV", [P, D])
        psK = k.ps(ctx, "n_psK", [P, 2, KC, P])
        psX = k.ps(ctx, "n_psX", [P, 2, KC, P])
        psS = [k.ps(ctx, f"n_psS{s}", [P, KC, 2, P]) for s in range(2)]
        psR = k.ps(ctx, "n_psR", [P, D])
        weights, zeroed = k.sem(ctx, "n_weights"), k.sem(ctx, "n_zeroed")
        xn_ready, t_ready, t_evac = k.sem(ctx, "n_xn_ready"), k.sem(ctx, "n_t_ready"), k.sem(ctx, "n_t_evac")
        qk_ready, v_ready, v_evac = k.sem(ctx, "n_qk_ready"), k.sem(ctx, "n_v_ready"), k.sem(ctx, "n_v_evac")
        rot_done, rot_ready = k.sem(ctx, "n_rot_done"), k.sem(ctx, "n_rot_ready")
        x_ready, x_evac = k.sem(ctx, "n_x_ready"), k.sem(ctx, "n_x_evac")
        s_ready, s_masked = k.sem(ctx, "n_s_ready"), k.sem(ctx, "n_s_masked")
        r_ready, r_read = k.sem(ctx, "n_r_ready"), k.sem(ctx, "n_r_read")
        st_ready, st_done = k.sem(ctx, "n_st_ready"), k.sem(ctx, "n_st_done")
        var_ready, root, rn_ready = k.sem(ctx, "n_var_ready"), k.sem(ctx, "n_root"), k.sem(ctx, "n_rn_ready")
        z_ready, z_added = k.sem(ctx, "n_z_ready"), k.sem(ctx, "n_z_added")
        dstep = k.sem(ctx, "n_dstep")
        block = ctx.enter_context(nc.Block())

        @block.sync
        def _(sp):
            sp.dma_start(wqkv[:, :, :], a["wqkv1"].rearrange("(k p) n -> p k n", p=P)).then_inc(weights, 16)
            sp.dma_start(rotC[:, :, :], a["rotC"]).then_inc(weights, 16)
            sp.dma_start(rotS[:, :, :], a["rotS"]).then_inc(weights, 16)
            sp.dma_start(causal[:, :], a["causal"]).then_inc(weights, 16)
            sp.dma_start(carry[:, :, :], a["carry"]).then_inc(weights, 16)
            sp.dma_start(wo[:, :, :], a["wo1"].rearrange("(k p) n -> p k n", p=P)).then_inc(weights, 16)
            sp.dma_start(gam[:, :], a["gamma"]).then_inc(weights, 16)
            sp.dma_start(bet[:, :], a["beta"]).then_inc(weights, 16)

        @block.tensor
        def _(pe):
            pe.sem_inc(x_ready, 1)
            pe.wait_ge(weights, 16 * 8)

            def bank_turn(i, what, u):
                return i * 8 + t_order.index((what, u))

            def project(i, u):
                n = bank_turn(i, "x", u)
                pe.wait_ge(xn_ready, i * TS + u + 1)
                pe.wait_ge(t_evac, n + 1)
                for c in range(KC):
                    mm = pe.transpose(psT[:, c, :], XN[:, u % 2, c * P:(c + 1) * P], k.ident[:, :])
                mm.then_inc(t_ready, 1)
                pe.wait_ge(t_evac, n + 2)
                pe.wait_ge(rot_done, i * TS + u + 1)
                for c in range(KC):
                    mm = pe.matmul(psQK[:, :], XT[:, c, :], wqkv[:, c, 0:2 * D], start=(c == 0), stop=(c == KC - 1))
                mm.then_inc(qk_ready, 1)
                pe.wait_ge(v_evac, i * TS + u + 1)
                pe.wait_ge(z_added, i * TS + (1 if u == 3 else 0) + 1)
                for c in range(KC):
                    mm = pe.matmul(psV[:, :], XT[:, c, :], wqkv[:, c, 2 * D:], start=(c == 0), stop=(c == KC - 1))
                mm.then_inc(v_ready, 1)

            def turn(i, u):
                pe.wait_ge(rot_ready, i * TS + u + 2)
                pe.wait_ge(x_evac, (i * TS + u) * 2 + 2)
                pe.wait_ge(st_done, i * (TS - 1) + u + 1)
                for par in range(2):
                    for c in range(KC):
                        pe.transpose(psK[:, par, c, :], Kpar[par][:, c, :], k.ident[:, :])
                for c in range(KC):
                    mm = pe.transpose(psX[:, 0, c, :], Qr[:, c * P:(c + 1) * P], k.ident[:, :])
                mm.then_inc(x_ready, 1)

            def attend(i, u):
                g = i * TS + u
                pe.wait_ge(x_evac, g * 2 + 4)
                for half in range(2):
                    pe.wait_ge(s_masked, g * 4 + 2 * half + 2)
                    for c in range(KC):
                        for par in range(2):
                            for b in range(2):
                                r = 32 * (2 * half + b)
                                mm = pe.matmul(psS[b][:, c, par, :], KT[r:r + 32, par, c, :], QT[r:r + 32, c, :],
                                               start=(c == 0 and par == 0), stop=(c == 1 and par == 1), skip_group_check=True)
                    mm.then_inc(s_ready, 1)
                pe.wait_ge(r_read, g + 1)
                if u > 0:
                    pe.wait_ge(st_done, i * (TS - 1) + u + 1)
                    for c in range(KC):
                        pe.matmul(psR[:, c * P:(c + 1) * P], QT[:, c, :], state[:, c, :], start=(c == 0), stop=False,
                                  skip_group_check=True)
                pe.wait_ge(s_masked, g * 4 + 4 + 2)
                for r in range(4):
                    for c in range(KC):
                        for par in range(2):
                            h = c * 8 + r * 2 + par
                            first = u == 0 and r == 0 and c == 0 and par == 0
                            mm = pe.matmul(psR[:, h * DH:(h + 1) * DH], ST[:, r, c, par, :], V[:, u % 2, h * DH:(h + 1) * DH],
                                           start=first, stop=(r == 3 and c == 1 and par == 1), skip_group_check=True)
                mm.then_inc(r_ready, 1)
                if u < TS - 1:
                    for c in range(KC):
                        mm = pe.matmul(psX[:, 1, c, :], Kr[:, u % 2, c * P:(c + 1) * P], V[:, u % 2, c * P:(c + 1) * P],
                                       start=(c == 0), stop=(c == KC - 1), skip_group_check=True)
                    mm.then_inc(st_ready, 1)

            def out(i, u):
                n = bank_turn(i, "r", u)
                pe.wait_ge(rn_ready, i * TS + u + 2)
                pe.wait_ge(t_evac, n + 1)
                for c in range(KC):
                    mm = pe.transpose(psT[:, c, :], RN[:, 8 * c:8 * c + 8, :].rearrange("p h d -> p (h d)"), k.ident[:, :])
                mm.then_inc(t_ready, 1)
                pe.wait_ge(t_evac, n + 2)
                pe.wait_ge(v_evac, i * TS + min(u + 3, TS) + 1)
                pe.wait_ge(z_added, i * TS + u + 1)
                for c in range(KC):
                    mm = pe.matmul(psV[:, :], RT[:, c, :], wo[:, c, :], start=(c == 0), stop=(c == KC - 1))
                mm.then_inc(z_ready, 1)

            with pe.Fori(0, NB) as i:
                for s in range(TS + 2):
                    if s < TS:
                        project(i, s)
                    if s >= 2:
                        out(i, s - 2)
                    if 1 <= s <= TS:
                        attend(i, s - 1)
                    if s < TS:
                        turn(i, s)

        @block.scalar
        def _(act):
            act.sem_inc(t_evac, 1)
            act.sem_inc(v_evac, 1)
            act.sem_inc(x_evac, 2)
            act.wait_ge(weights, 16 * 8)

            def x_turned(i, u):
                n = i * 8 + t_order.index(("x", u))
                act.wait_ge(t_ready, n + 1)
                nc.scalar.copy(XT[:, :, :], psT[:, :, :]).then_inc(t_evac, 1)

            def r_turned(i, u):
                n = i * 8 + t_order.index(("r", u))
                act.wait_ge(t_ready, n + 1)
                for c in range(KC):
                    ins = nc.scalar.activation(RT[:, c, :], psT[:, c, :], ACT.Identity, bias=bet[:, c:c + 1],
                                               scale=gam[:, c:c + 1])
                ins.then_inc(t_evac, 1)

            def values(i, u):
                act.wait_ge(v_ready, i * TS + u + 1)
                nc.scalar.copy(V[:, u % 2, :], psV[:, :]).then_inc(v_evac, 1)

            def turned(i, u):
                act.wait_ge(x_ready, i * TS + u + 2)
                nc.scalar.copy(KT[:, :, :, :], psK[:, :, :, :]).then_inc(x_evac, 1)
                nc.scalar.copy(QT[:, :, :], psX[:, 0, :, :]).then_inc(x_evac, 1)

            with act.Fori(0, NB) as i:
                for s in range(TS + 2):
                    if s < TS:
                        x_turned(i, s)
                        values(i, s)
                    if s >= 2:
                        r_turned(i, s - 2)
                    if s < TS:
                        turned(i, s)

        @block.gpsimd
        def _(pool):
            pool.sem_inc(rot_ready, 1)
            pool.sem_inc(rn_ready, 1)
            for par in range(2):
                nc.gpsimd.memset(Kpar[par][:, :, :], 0.0).then_inc(zeroed, 1)
            pool.wait_ge(zeroed, 2)

            def rotated(i, u):
                pool.wait_ge(rot_done, i * TS + u + 2)
                pool.wait_ge(x_ready, i * TS + u + 1)
                nc.gpsimd.tensor_tensor(Qr[:, :], m1[:, 0:D], m2[:, 0:D], ALU.add)
                nc.gpsimd.tensor_tensor(Kr[:, u % 2, :], m1[:, D:], m2[:, D:], ALU.add)
                for par in range(2):
                    def side(x):
                        return x.rearrange("p (g h d) -> p g h d", h=2, d=DH)[:, :, par, :]
                    dst = Kpar[par][:, :, :].rearrange("p c (g h d) -> p (c g) h d", h=2, d=DH)[:, :, par, :]
                    ins = nc.gpsimd.tensor_tensor(dst, side(m1[:, D:]), side(m2[:, D:]), ALU.add)
                ins.then_inc(rot_ready, 1)

            def normed(i, u):
                pool.wait_ge(var_ready, i * TS + u + 1)
                nc.gpsimd.tensor_tensor(hr[:, :], hv[:, :], k.mhalf[:, 0:H1], ALU.pow).then_inc(root, 1)
                pool.wait_ge(root, i * TS + u + 1)
                nc.gpsimd.tensor_tensor(RN[:, :, :], cen[:, :, :], bc(hr[:, :].unsqueeze(2), [P, H1, DH]),
                                        ALU.mult).then_inc(rn_ready, 1)

            with pool.Fori(0, NB) as i:
                for s in range(TS + 1):
                    if s < TS:
                        rotated(i, s)
                    if s >= 1:
                        normed(i, s - 1)

        @block.vector
        def _(dve):
            dve.sem_inc(rot_done, 1)
            dve.sem_inc(s_masked, 2)
            dve.sem_inc(st_done, 1)
            dve.sem_inc(r_read, 1)
            dve.sem_inc(z_added, 1)
            dve.wait_ge(weights, 16 * 8)
            NST = 4 * TS + (TS - 2) + TS

            def norm(i, u):
                normalise(k, XN[:, u % 2, :], i * TS + u).then_inc(xn_ready, 1)

            def rotate(i, u):
                dve.wait_ge(qk_ready, i * TS + u + 1)
                dve.wait_ge(rot_ready, i * TS + u + 1)
                nc.vector.tensor_tensor(m1[:, :], psQK[:, :], rotC[:, u, :], ALU.mult)
                for x in range(2):
                    def lane(y, z):
                        return y.rearrange("p (n two) -> p n two", two=2)[:, :, z]
                    ins = nc.vector.tensor_tensor(lane(m2[:, :], x), lane(psQK[:, :], 1 - x), lane(rotS[:, u, :], x), ALU.mult)
                ins.then_inc(rot_done, 1)

            def mask(i, u):
                for r in range(4):
                    if r % 2 == 0:
                        dve.wait_ge(s_ready, (i * TS + u) * 2 + r // 2 + 1)
                    nc.vector.tensor_tensor(ST[:, r, :, :, :].rearrange("p c a t -> p (c a) t"),
                                            psS[r % 2][:, :, :, :].rearrange("p c a t -> p (c a) t"),
                                            bc(causal[:, :].unsqueeze(1), [P, 4, P]), ALU.mult).then_inc(s_masked, 1)

            def carry_on(i, u, ch):
                dve.wait_ge(st_ready, i * (TS - 1) + u + 1)
                new = psX[:, 1, :, :]
                if u > 0:
                    ch.step(nc.vector.tensor_tensor(snew[:, :, :], psX[:, 1, :, :], state[:, :, :], ALU.add))
                    new = snew[:, :, :]
                nc.vector.tensor_tensor(state[:, :, :], new, carry[:, :, :], ALU.mult).then_inc(st_done, 1)

            def head_norm(i, u, ch):
                g = i * TS + u
                dve.wait_ge(r_ready, g + 1)
                R = psR[:, :].rearrange("p (h d) -> p h d", d=DH)
                ch.step(nc.vector.tensor_reduce(hm[:, :], R, AX.X, ALU.add))
                ch.step(nc.vector.tensor_scalar(hm[:, :], hm[:, :], 1.0 / DH, None, ALU.mult))
                dve.wait_ge(rn_ready, g + 1)
                nc.vector.tensor_tensor(cen[:, :, :], R, bc(hm[:, :].unsqueeze(2), [P, H1, DH]),
                                        ALU.subtract).then_inc(r_read, 1)
                dve.wait_ge(r_read, g + 2)
                ch.step(nc.vector.tensor_tensor(sq[:, :, :], cen[:, :, :], cen[:, :, :], ALU.mult))
                ch.step(nc.vector.tensor_reduce(hv[:, :], sq[:, :, :], AX.X, ALU.add))
                nc.vector.tensor_scalar(hv[:, :], hv[:, :], 1.0 / DH, EPS, ALU.mult, ALU.add).then_inc(var_ready, 1)

            def add(i, u, ch):
                dve.wait_ge(z_ready, i * TS + u + 1)
                x = k.X[:, bass.ds(i * TS + u, 1), :].rearrange("p a c -> p (a c)")
                ch.step(nc.vector.tensor_tensor(x, x, psV[:, :], ALU.add))
                pass_gate(k, dve)
                nc.vector.bn_stats(k.BST[:, bass.ds(i * TS + u, 1), :].rearrange("p a c -> p (a c)"), x).then_inc(z_added, 1)

            with dve.Fori(0, NB) as i:
                ch = Chain(dve, dstep, i * NST)
                norm(i, 0)
                for s in range(TS + 2):
                    if s < TS - 1:
                        if s >= 1:
                            dve.wait_ge(t_ready, i * 8 + t_order.index(("x", s - 1)) + 1)
                        norm(i, s + 1)
                    if s < TS:
                        rotate(i, s)
                    if s >= 2:
                        add(i, s - 2, ch)
                    if 1 <= s <= TS:
                        mask(i, s - 1)
                        if s < TS:
                            carry_on(i, s - 1, ch)
                        head_norm(i, s - 1, ch)
                assert ch.n == NST, ch.n


def swiglu(k):
    nc, a = k.nc, k.a
    M = FF // P
    with ExitStack() as ctx:
        wgu = k.sb(ctx, "wgu", [P, KC, 2 * FF])
        wd = k.sb(ctx, "wd", [P, M, D])
        XN = k.sb(ctx, "f_XN", [P, TS, D])
        XT = k.sb(ctx, "f_XT", [P, KC, T])
        SG = k.sb(ctx, "f_SG", [P, 2, T])
        HT = k.sb(ctx, "f_HT", [P, M, T])
        psT = [k.ps(ctx, f"f_psT{c}", [P, T]) for c in range(KC)]
        psG = [k.ps(ctx, f"f_psG{s}", [P, T]) for s in range(2)]
        psU = [k.ps(ctx, f"f_psU{s}", [P, T]) for s in range(2)]
        psY = [k.ps(ctx, f"f_psY{s}", [P, D]) for s in range(2)]
        casts = k.sem(ctx, "f_casts")
        xn_ready, t_ready, t_evac = k.sem(ctx, "f_xn_ready"), k.sem(ctx, "f_t_ready"), k.sem(ctx, "f_t_evac")
        g_ready, g_done, u_done = k.sem(ctx, "f_g_ready"), k.sem(ctx, "f_g_done"), k.sem(ctx, "f_u_done")
        y_ready, y_added = k.sem(ctx, "f_y_ready"), k.sem(ctx, "f_y_added")
        with ExitStack() as c2:
            raw = k.sb(c2, "w_raw", [P, KC * 2 * FF + M * D], I32)
            weights = k.sem(ctx, "f_weights")
            n1 = KC * 2 * FF
            with nc.Block() as load:
                @load.sync
                def _(sp):
                    sp.dma_start(raw[:, 0:n1].rearrange("p (k n) -> p k n", k=KC),
                                 a["wgu"].rearrange("(k p) n -> p k n", p=P)).then_inc(weights, 16)
                    sp.dma_start(raw[:, n1:].rearrange("p (m n) -> p m n", m=M),
                                 a["wd"].rearrange("(m p) n -> p m n", p=P)).then_inc(weights, 16)

                @load.vector
                def _(dve):
                    dve.wait_ge(weights, 32)
                    nc.vector.tensor_copy(wgu[:, :, :].rearrange("p k n -> p (k n)"), raw[:, 0:n1]).then_inc(casts, 1)

                @load.gpsimd
                def _(pool):
                    pool.wait_ge(weights, 32)
                    nc.gpsimd.tensor_copy(wd[:, :, :].rearrange("p m n -> p (m n)"), raw[:, n1:]).then_inc(casts, 1)
        block = ctx.enter_context(nc.Block())

        @block.tensor
        def _(pe):
            pe.sem_inc(t_ready, 1)
            pe.sem_inc(y_ready, 4)
            pe.wait_ge(casts, 2)

            def turn(i):
                pe.wait_ge(t_evac, i * 2 + 2)
                for u in range(TS):
                    pe.wait_ge(xn_ready, i * TS + u + 1)
                    for c in range(KC):
                        mm = pe.transpose(psT[c][:, u * P:(u + 1) * P], XN[:, u, c * P:(c + 1) * P], k.ident[:, :])
                mm.then_inc(t_ready, 1)

            with pe.Fori(0, NB) as i:
                turn(i)
                pe.wait_ge(t_evac, i * 2 + 4)
                for m in range(M):
                    pe.wait_ge(g_done, i * M + m + 1)
                    for c in range(KC):
                        mm = pe.matmul(psG[m % 2][:, :], wgu[:, c, m * P:(m + 1) * P], XT[:, c, :], start=(c == 0), stop=(c == KC - 1))
                    mm.then_inc(g_ready, 1)
                    pe.wait_ge(u_done, i * M + m + 1)
                    for c in range(KC):
                        mm = pe.matmul(psU[m % 2][:, :], wgu[:, c, FF + m * P:FF + (m + 1) * P], XT[:, c, :], start=(c == 0), stop=(c == KC - 1))
                    mm.then_inc(g_ready, 1)
                pe.wait_ge(u_done, i * M + M + 2)
                for u in range(TS):
                    pe.wait_ge(y_added, i * TS + u + 1)
                    for m in range(M):
                        mm = pe.matmul(psY[u % 2][:, :], HT[:, m, u * P:(u + 1) * P], wd[:, m, :], start=(m == 0), stop=(m == M - 1))
                    mm.then_inc(y_ready, 1)

        @block.scalar
        def _(act):
            act.sem_inc(t_evac, 2)
            act.sem_inc(g_done, 2)
            with act.Fori(0, NB) as i:
                act.wait_ge(t_ready, i + 2)
                for c in range(KC):
                    nc.scalar.copy(XT[:, c, :], psT[c][:, :]).then_inc(t_evac, 1)
                for m in range(M):
                    act.wait_ge(g_ready, (i * M + m) * 2 + 1)
                    act.wait_ge(u_done, i * M + m + 1)
                    nc.scalar.activation(SG[:, m % 2, :], psG[m % 2][:, :], ACT.Silu, scale=QSCALE).then_inc(g_done, 1)

        @block.sync
        def _(sp):
            with sp.Fori(0, NB) as i:
                sp.wait_ge(y_added, i * TS + TS + 2)
                sp.dma_start(k.out[bass.ds(i * T, T), :].rearrange("(j p) c -> p j c", p=P),
                             k.X[:, bass.ds(i * TS, TS), :]).then_inc(k.stored, 16)
            sp.wait_ge(k.stored, 16 * NB)

        @block.vector
        def _(dve):
            dve.sem_inc(u_done, 2)
            dve.sem_inc(y_added, 2)
            with dve.Fori(0, NB) as i:
                dve.wait_ge(t_ready, i + 1)
                for u in range(TS):
                    normalise(k, XN[:, u, :], i * TS + u).then_inc(xn_ready, 1)
                for m in range(M):
                    dve.wait_ge(g_ready, (i * M + m) * 2 + 2)
                    dve.wait_ge(g_done, i * M + m + 1 + 2)
                    dve.wait_ge(y_ready, i * TS + TS)
                    nc.vector.scalar_tensor_tensor(HT[:, m, :], psU[m % 2][:, :], QSCALE, SG[:, m % 2, :],
                                                   ALU.mult, ALU.mult).then_inc(u_done, 1)
                for u in range(TS):
                    dve.wait_ge(y_ready, i * TS + u + 1 + 4)
                    x = k.X[:, bass.ds(i * TS + u, 1), :].rearrange("p a c -> p (a c)")
                    nc.vector.scalar_tensor_tensor(x, psY[u % 2][:, :], QSCALE, x, ALU.mult, ALU.add).then_inc(y_added, 1)


def lay_out(x):
    f = np.ascontiguousarray
    c = {}
    c["x"] = f(x["L0_attn_X"]).reshape(NB * T, D)
    c["wg"] = f(x["L0_attn_w_G"].reshape(H0 * E0, D).T)
    c["bg"] = f(x["L0_attn_b_G"].reshape(1, H0 * E0))
    c["wkv"] = f(np.concatenate([x["L0_attn_w_K"], x["L0_attn_w_V"]], axis=1).reshape(H0 * P, D).T)
    c["wq"] = f(x["L0_attn_w_Q"].reshape(H0 * DK, D).T)
    c["wo"] = f(x["L0_attn_w_O"].reshape(2, 4, DK, D).transpose(1, 0, 2, 3)).reshape(H0 * DK, D)
    c["ikv"] = f(np.concatenate([x["L0_attn_init_K_rec"], x["L0_attn_init_V_rec"]], axis=2).transpose(2, 0, 1))
    c["ident"] = np.eye(P, dtype=np.float32)
    q, s = np.arange(32)[:, None], np.arange(64)[None, :]
    seen = (s > q) & (s <= q + L0)
    c["mask"] = f(np.repeat(np.where(seen, 0.0, NEG).astype(np.float32), E0, axis=1))
    c["sel"] = f(np.tile(np.eye(32, dtype=np.float32), (1, 4)))
    col = lambda v: f(v.reshape(KC, P).T)
    c["qkv1"] = f(x["L0_ffn_qkv_weight"].T)
    c["proj"] = f(x["L0_ffn_proj_weight"].T)
    c["router"] = f(x["L0_ffn_router_weight"])
    c["ln1w"], c["ln1b"] = col(x["L0_ffn_ln1_weight"]), col(x["L0_ffn_ln1_bias"])
    c["ln2w"], c["ln2b"] = col(x["L0_ffn_ln2_weight"]), col(x["L0_ffn_ln2_bias"])
    c["w1"], c["w2"] = f(x["L0_ffn_moe_w1"]), f(x["L0_ffn_moe_w2"])
    c["before"] = np.triu(np.ones((P, P), np.float32), 1)
    c["iota8"] = f(np.tile(np.arange(NE, dtype=np.float32), (P, 1)))
    flat = lambda w: w.reshape(D, D)
    c["wqkv1"] = f(np.concatenate([flat(x["L1_attn_WQ"]), flat(x["L1_attn_WK"]), flat(x["L1_attn_WV"])]).T)
    c["wo1"] = f(x["L1_attn_WO"])
    c["gamma"], c["beta"] = col(x["L1_attn_gamma"]), col(x["L1_attn_beta"])
    c["rotC"], c["rotS"], c["carry"] = decay_tables()
    c["causal"] = np.triu(np.ones((P, P), np.float32))
    c["wgu"] = f(np.concatenate([x["L1_ffn_w_gate"], x["L1_ffn_w_up"]]).T)
    c["wd"] = f(x["L1_ffn_w_down"].T)
    return c


def decay_tables():
    freq = (10.0 ** (-4.0 * (np.arange(0, DH, 2, dtype=np.float32) / np.float32(DH)))).astype(np.float32)
    angle = (np.arange(T, dtype=np.float32)[:, None] * freq[None, :]).astype(np.float64)
    gamma = 1.0 - 2.0 ** (-5.0 - np.arange(H1, dtype=np.float64))
    i = np.arange(P, dtype=np.float64)
    both = np.stack([gamma[None, :] ** i[:, None], gamma[None, :] ** -i[:, None]], axis=1)
    def spread(t):
        t = t.reshape(TS, P, 1, 1, DH).transpose(1, 0, 2, 3, 4) * both[:, None, :, :, None]
        return np.ascontiguousarray(t.reshape(P, TS, 2 * D).astype(np.float32))
    cos = np.repeat(np.cos(angle), 2, axis=1)
    sin = np.stack([-np.sin(angle), np.sin(angle)], axis=2).reshape(T, DH)
    carry = np.zeros((P, KC, P))
    for h in range(H1):
        r = slice(h % 8 * DH, h % 8 * DH + DH)
        carry[r, h // 8, r] = gamma[h] ** P
    return spread(cos), spread(sin), carry.astype(np.float32)


UPTO = 4
_SHAPE = (NB, T, D)


def kernel(**inputs):
    import numpy as _np
    import concourse.bacc as _bacc
    from concourse import mybir as _mybir
    from concourse.bass_utils import run_bass_kernel_spmd as _run

    arrays = lay_out(inputs)
    nc = _bacc.Bacc("TRN2", target_bir_lowering=False, num_devices=1)
    args = {}
    for name, v in arrays.items():
        args[name] = nc.dram_tensor("in_" + name, v.shape, _mybir.dt.from_np(v.dtype), kind="ExternalInput").ap()
    out = nc.dram_tensor("out_x", (NB * T, D), F32, kind="ExternalOutput").ap()
    build(nc, args, out, UPTO)
    r = _run(nc, [{"in_" + n: v for n, v in arrays.items()}], core_ids=[0])
    return r.results[0]["out_x"].reshape(_SHAPE)
```

```python
from contextlib import ExitStack

import numpy as np

import concourse.bass as bass
from concourse import mybir

F32 = mybir.dt.float32
BF16 = mybir.dt.bfloat16
I32 = mybir.dt.int32
U32 = mybir.dt.uint32
ALU = mybir.AluOpType
ACT = mybir.ActivationFunctionType
AX = mybir.AxisListType

P = 128
NB, T, D = 8, 512, 256
NT = NB * T // P
TS = T // P
KC = D // P
EPS = 1e-5
H0, E0, L0, DK = 8, 4, 32, 64
WIN = L0 + T
NH, NKV, HD = 16, 4, 16
QG = NH // NKV
QKVW = NKV * (QG + 2) * HD
NE, FE = 8, 512
CAP = 1280
SLOTS = NE * CAP
H1, DH = 16, 16
FF = 768
QSCALE = 1.0 / 127.0
NEG = -1e30


def bc(ap, shape):
    return ap.broadcast_to(shape)


class Chain:

    def __init__(self, eng, sem, base=0):
        self.eng, self.sem, self.base, self.n = eng, sem, base, 0

    def step(self, ins):
        self.n += 1
        ins.then_inc(self.sem, 1)
        self.eng.wait_ge(self.sem, self.base + self.n)

    def mark(self, ins):
        self.n += 1
        ins.then_inc(self.sem, 1)
        return self.n

    def after(self, n):
        self.eng.wait_ge(self.sem, self.base + n)


def pass_gate(k, eng):
    eng.sem_inc(k.gates_passed, 1)


class Kernel:
    def __init__(self, nc, a, out, upto):
        self.nc, self.a, self.out, self.upto = nc, a, out, upto
        self.n = 0

    def sb(self, ctx, name, shape, dt=F32):
        return ctx.enter_context(self.nc.sbuf_tensor(name, shape, dt))

    def ps(self, ctx, name, shape, dt=F32):
        return ctx.enter_context(self.nc.psum_tensor(name, shape, dt))

    def sem(self, ctx, name):
        return ctx.enter_context(self.nc.semaphore(name))


def build(nc, a, out, upto=4):
    k = Kernel(nc, a, out, upto)
    with ExitStack() as ctx:
        k.X = k.sb(ctx, "X", [P, NT, D])
        k.BST = k.sb(ctx, "BST", [P, NT, 6])
        k.mean = k.sb(ctx, "mean", [P, NT])
        k.rstd = k.sb(ctx, "rstd", [P, NT])
        k.ident = k.sb(ctx, "ident", [P, P])
        k.ones = k.sb(ctx, "ones", [P, P])
        k.mhalf = k.sb(ctx, "mhalf", [P, NT])
        k.stored = k.sem(ctx, "out_stored")
        k.ln_steps, k.ln_var, k.ln_root = k.sem(ctx, "ln_steps"), k.sem(ctx, "ln_var"), k.sem(ctx, "ln_root")
        k.gates_passed = k.sem(ctx, "gates_passed")
        k.xt_dram = nc.dram_tensor("expert_in", (SLOTS + P, D), F32, kind="Internal").ap()
        k.xT_dram = nc.dram_tensor("x_turned", (P, KC, NB * T), F32, kind="Internal").ap()
        k.y_dram = nc.dram_tensor("expert_out", (SLOTS + P, D), F32, kind="Internal").ap()
        setup(k)
        if upto >= 1:
            with ExitStack() as c1:
                k.Rec = k.sb(c1, "Rec", [P, NB, WIN, E0])
                ln_stats(k)
                recurrence(k)
                window_attention(k)
        if upto >= 2:
            with ExitStack() as c2:
                k.HS = k.sb(c2, "HS", [P, NT, D])
                k.slots = k.sb(c2, "slots", [P, NT, 2], U32)
                k.prob = k.sb(c2, "prob", [P, NT, 2])
                with ExitStack() as c3:
                    k.LG = k.sb(c3, "LG", [P, NB, TS, NE])
                    with ExitStack() as c4:
                        k.QKV = k.sb(c4, "QKV", [P, NT, QKVW])
                        ln_stats(k)
                        position_qkv(k)
                        position_attention(k)
                    ln_stats(k)
                    route(k)
                experts(k)
                combine(k)
        if upto >= 3:
            ln_stats(k)
            retention(k)
        if upto >= 4:
            ln_stats(k)
            swiglu(k)
        else:
            store_x(k)


def setup(k):
    nc, a = k.nc, k.a
    with ExitStack() as ctx:
        parts = [k.sem(ctx, f"x_part{n}") for n in range(2)]
        const = k.sem(ctx, "const_loaded")
        stats = k.sem(ctx, "x_stats")
        ones_set = k.sem(ctx, "ones_set")
        zero = k.sb(ctx, "zero_rows", [P, 10, D])
        zero_set = k.sem(ctx, "zero_set")
        zero_stored = k.sem(ctx, "zero_stored")
        block = ctx.enter_context(nc.Block())

        @block.sync
        def _(sp):
            for n in range(NB):
                sp.dma_start(k.X[:, n * TS:(n + 1) * TS, :],
                             a["x"][n * T:(n + 1) * T, :].rearrange("(i p) c -> p i c", p=P)).then_inc(parts[n // 4], 16)
            sp.dma_start(k.ident[:, :], a["ident"]).then_inc(const, 16)
            sp.wait_ge(const, 16)

        @block.scalar
        def _(act):
            act.wait_ge(zero_set, 1)
            for e in range(NE):
                act.dma_start(k.xt_dram[e * CAP:(e + 1) * CAP, :].rearrange("(i p) c -> p i c", p=P),
                              zero[:, :, :]).then_inc(zero_stored, 16)
            act.dma_start(k.y_dram[SLOTS:SLOTS + P, :], zero[:, 0, :]).then_inc(zero_stored, 16)
            act.wait_ge(zero_stored, 16 * (NE + 1))

        @block.gpsimd
        def _(pool):
            nc.gpsimd.memset(k.mhalf[:, :], -0.5).then_inc(ones_set, 1)
            nc.gpsimd.memset(k.ones[:, :], 1.0).then_inc(ones_set, 1)

        @block.vector
        def _(dve):
            nc.vector.memset(zero[:, :, :], 0.0).then_inc(zero_set, 1)
            for n in range(2):
                dve.wait_ge(parts[n], 64)
                for t in range(n * NT // 2, (n + 1) * NT // 2):
                    nc.vector.bn_stats(k.BST[:, t, :], k.X[:, t, :]).then_inc(stats, 1)


def stats_steps(nc, chain, bst, mean, var, tmp, ready):
    me, mo, ve, vo = bst[:, :, 1], bst[:, :, 4], bst[:, :, 2], bst[:, :, 5]
    m1 = chain.mark(nc.vector.tensor_tensor(mean, me, mo, ALU.add))
    m2 = chain.mark(nc.vector.tensor_tensor(tmp, me, mo, ALU.subtract))
    m3 = chain.mark(nc.vector.tensor_tensor(var, ve, vo, ALU.add))
    chain.after(m1)
    chain.mark(nc.vector.tensor_scalar(mean, mean, 0.5, None, ALU.mult))
    chain.after(m2)
    chain.step(nc.vector.tensor_tensor(tmp, tmp, tmp, ALU.mult))
    chain.after(m3)
    chain.step(nc.vector.scalar_tensor_tensor(var, tmp, D / 4.0, var, ALU.mult, ALU.add))
    nc.vector.tensor_scalar(var, var, 1.0 / D, EPS, ALU.mult, ALU.add).then_inc(ready, 1)


def ln_stats(k):
    nc = k.nc
    with ExitStack() as ctx:
        tmp = k.sb(ctx, f"ln{k.n}_tmp", [P, NT])
        var = k.sb(ctx, f"ln{k.n}_var", [P, NT])
        block = ctx.enter_context(nc.Block())

        @block.vector
        def _(dve):
            chain = Chain(dve, k.ln_steps, k.n * 6)
            stats_steps(nc, chain, k.BST[:, :, :], k.mean[:, :], var[:, :], tmp[:, :], k.ln_var)
            assert chain.n == 6

        @block.gpsimd
        def _(pool):
            pool.wait_ge(k.ln_var, k.n + 1)
            nc.gpsimd.tensor_tensor(k.rstd[:, :], var[:, :], k.mhalf[:, :], ALU.pow).then_inc(k.ln_root, 1)
    k.n += 1


def store_x(k):
    nc = k.nc
    with ExitStack() as ctx:
        block = ctx.enter_context(nc.Block())

        @block.sync
        def _(sp):
            sp.dma_start(k.out.rearrange("(i p) c -> p i c", p=P), k.X[:, :, :]).then_inc(k.stored, 16)
            sp.wait_ge(k.stored, 16)


def normalise(k, dst, tile):
    return k.nc.vector.tensor_scalar(dst, k.X[:, bass.ds(tile, 1), :], k.mean[:, bass.ds(tile, 1)],
                                     k.rstd[:, bass.ds(tile, 1)], ALU.subtract, ALU.mult)


def recurrence(k):
    nc, a = k.nc, k.a
    HE = H0 * E0
    EV = E0 - 1
    NV = H0 * EV
    with ExitStack() as ctx:
        wg = k.sb(ctx, "wg", [P, KC, HE])
        bg = k.sb(ctx, "bg", [1, HE])
        wkv = k.sb(ctx, "wkv", [P, KC, H0 * P])
        ikv = k.sb(ctx, "ikv", [P, E0, L0])
        XN = k.sb(ctx, "XN1", [P, 2, D])
        XT = k.sb(ctx, "XT1", [P, TS, KC, P])
        eg = k.sb(ctx, "eg", [P, TS, HE])
        G = k.sb(ctx, "G", [P, TS, HE])
        A = k.sb(ctx, "A", [P, TS, E0])
        gated = k.sb(ctx, "gated", [P, 2, H0, P])
        acc = k.sb(ctx, "acc", [P, 2, E0, P])
        gT = k.sb(ctx, "gT", [P, E0, T])
        AT = k.sb(ctx, "AT", [P, E0, T])
        seed = k.sb(ctx, "seed", [P, E0, L0])
        psT = k.ps(ctx, "psT", [P, KC, P])
        psG = k.ps(ctx, "psG", [P, TS, HE])
        psKV = [[k.ps(ctx, f"psKV{s}{h}", [P, 4, P]) for h in range(2)] for s in range(2)]
        psR = k.ps(ctx, "psR", [P, E0, P])
        psA = k.ps(ctx, "psA", [P, E0, P])
        weights = k.sem(ctx, "r_weights")
        xn_ready, t_ready, t_evac = k.sem(ctx, "r_xn_ready"), k.sem(ctx, "r_t_ready"), k.sem(ctx, "r_t_evac")
        g_ready, g_exp, g_gate = k.sem(ctx, "r_g_ready"), k.sem(ctx, "r_g_exp"), k.sem(ctx, "r_g_gate")
        kv_ready, acc_step = k.sem(ctx, "r_kv_ready"), k.sem(ctx, "r_acc_step")
        gated_ready, gated_step, gated_summed = k.sem(ctx, "r_gated"), k.sem(ctx, "r_gated_step"), k.sem(ctx, "r_gated_summed")
        ra_ready, ra_evac = k.sem(ctx, "r_ra_ready"), k.sem(ctx, "r_ra_evac")
        scan_done = k.sem(ctx, "r_scan_done")
        xt_stored = [k.sem(ctx, f"r_xt_stored{u}") for u in range(TS)]
        gate_step, scan_step = k.sem(ctx, "r_gate_step"), k.sem(ctx, "r_scan_step")
        init_set = k.sem(ctx, "r_init_set")
        block = ctx.enter_context(nc.Block())

        def stream(eng, step):
            def peeled(g):
                step(g // TS, g % TS, lambda d: 0 <= g + d < NT)
            for g in range(-TS, TS):
                peeled(g)
            with eng.Fori(1, NB - 1) as i:
                for u in range(TS):
                    step(i, u, lambda d: True)
            for g in range(NT - TS, NT + 1):
                peeled(g)

        @block.sync
        def _(sp):
            sp.dma_start(wg[:, :, :], a["wg"].rearrange("(k p) n -> p k n", p=P)).then_inc(weights, 16)
            sp.dma_start(bg[:, :], a["bg"]).then_inc(weights, 16)
            sp.dma_start(wkv[:, :, :], a["wkv"].rearrange("(k p) n -> p k n", p=P)).then_inc(weights, 16)
            sp.dma_start(ikv[:, :, :], a["ikv"]).then_inc(weights, 16)
            for u in range(TS):
                sp.sem_inc(xt_stored[u], 16)
            with sp.Fori(0, NB) as i:
                for u in range(TS):
                    sp.wait_ge(t_evac, i * TS + u + 2)
                    sp.dma_start(k.xT_dram[:, :, bass.ds(i * T + u * P, P)], XT[:, u, :, :]).then_inc(xt_stored[u], 16)
            for u in range(TS):
                sp.wait_ge(xt_stored[u], 16 * (NB + 1))

        @block.gpsimd
        def _(pool):
            pool.sem_inc(gated_summed, 2)
            pool.wait_ge(weights, 64)
            for n in range(NB):
                nc.gpsimd.tensor_copy(k.Rec[:, n, 0:L0, :].rearrange("p t e -> p e t"), ikv[:, :, :]).then_inc(init_set, 1)

            def head_sum(t, v):
                ch = Chain(pool, gated_step, t * 2)
                x = gated[:, v % 2, :, :]
                pool.wait_ge(gated_ready, t * 2 + 2 + 8)
                ch.step(nc.gpsimd.tensor_tensor(x[:, 0:4, :], x[:, 0:4, :], x[:, 4:8, :], ALU.add))
                ch.step(nc.gpsimd.tensor_tensor(x[:, 0:2, :], x[:, 0:2, :], x[:, 2:4, :], ALU.add))
                pool.wait_ge(ra_ready, t * 2 + 5)
                nc.gpsimd.tensor_tensor(acc[:, v % 2, EV, :], x[:, 0, :], x[:, 1, :], ALU.add).then_inc(gated_summed, 1)

            def step(i, u, has):
                if has(0):
                    head_sum(i * TS + u, u)

            stream(pool, step)

        @block.tensor
        def _(pe):
            pe.sem_inc(t_ready, 2)
            pe.sem_inc(kv_ready, 4)
            pe.sem_inc(ra_ready, 8)
            pe.wait_ge(weights, 64)

            def turned(t, v):
                pe.wait_ge(t_evac, t + 1)
                pe.wait_ge(xn_ready, t + 1)
                for c in range(KC):
                    mm = pe.transpose(psT[:, c, :], XN[:, v % 2, c * P:(c + 1) * P], k.ident[:, :])
                mm.then_inc(t_ready, 1)

            def gates(t, v):
                pe.wait_ge(t_evac, t + 2)
                pe.wait_ge(g_exp, t + 1)
                for c in range(KC):
                    pe.matmul(psG[:, v, :], XT[:, v, c, :], wg[:, c, :], start=(c == 0), stop=False)
                pe.matmul(psG[:, v, :], k.ones[0:1, :], bg[0:1, :], start=False, stop=True).then_inc(g_ready, 1)

            def keys_values(t, v):
                pe.wait_ge(t_evac, t + 2)
                pe.wait_ge(acc_step, t * NV + NV)
                pe.wait_ge(gated_ready, t * 2 + 6)
                for half in range(2):
                    for c in range(KC):
                        mm = pe.matmul(psKV[v % 2][half][:, :, :], XT[:, v, c, :],
                                       wkv[:, c, half * 512:(half + 1) * 512], start=(c == 0), stop=(c == KC - 1))
                mm.then_inc(kv_ready, 1)

            def sums_turned(t, v):
                pe.wait_ge(acc_step, t * NV + 3 * NV)
                pe.wait_ge(gated_summed, t + 3)
                pe.wait_ge(ra_evac, t * 2 + 1)
                for e in range(E0):
                    mm = pe.transpose(psR[:, e, :], acc[:, v % 2, e, :], k.ident[:, :])
                mm.then_inc(ra_ready, 1)
                pe.wait_ge(ra_evac, t * 2 + 2)
                for e in range(E0):
                    mm = pe.transpose(psA[:, e, :], bc(A[:, v, e:e + 1], [P, P]), k.ident[:, :])
                mm.then_inc(ra_ready, 1)

            def step(i, u, has):
                g = i * TS + u
                if has(3):
                    turned(g + 3, (u + 3) % TS)
                if has(2):
                    gates(g + 2, (u + 2) % TS)
                if has(1):
                    keys_values(g + 1, (u + 1) % TS)
                if has(-1):
                    sums_turned(g - 1, (u - 1) % TS)

            stream(pe, step)

        @block.scalar
        def _(act):
            act.sem_inc(t_evac, 1)
            act.sem_inc(g_exp, 1)
            act.sem_inc(gated_ready, 8)
            act.sem_inc(ra_evac, 2)

            def turned(t, v, i):
                act.wait_ge(t_ready, t + 3)
                act.wait_ge(kv_ready, t + 1)
                act.wait_ge(xt_stored[v], i * 16 + 16)
                nc.scalar.copy(XT[:, v, :, :], psT[:, :, :]).then_inc(t_evac, 1)

            def exponential(t, v):
                act.wait_ge(g_ready, t + 1)
                act.wait_ge(g_gate, t + 1)
                nc.scalar.activation(eg[:, v, :], psG[:, v, :], ACT.Exp, scale=-1.0).then_inc(g_exp, 1)

            def gate(t, v, half):
                if half == 1:
                    act.wait_ge(kv_ready, t + 1 + 4)
                    act.wait_ge(g_gate, t + 1 + 4)
                    act.wait_ge(gated_summed, t + 1)
                else:
                    act.wait_ge(acc_step, t * NV + (NV // 2 + 2 * NV))
                for h in range(4 * half, 4 * half + 4):
                    ins = nc.scalar.activation(gated[:, v % 2, h, :], psKV[v % 2][half][:, h % 4, :], ACT.Copy,
                                               scale=G[:, v, h * E0 + EV:h * E0 + EV + 1])
                ins.then_inc(gated_ready, 1)

            def sums_turned(t, v, i):
                if v == 0:
                    act.wait_ge(scan_done, i + 1)
                act.wait_ge(ra_ready, t * 2 + 1 + 8)
                nc.scalar.copy(gT[:, :, v * P:(v + 1) * P], psR[:, :, :]).then_inc(ra_evac, 1)
                act.wait_ge(ra_ready, t * 2 + 2 + 8)
                nc.scalar.copy(AT[:, :, v * P:(v + 1) * P], psA[:, :, :]).then_inc(ra_evac, 1)

            def step(i, u, has):
                g = i * TS + u
                if has(0):
                    gate(g, u, 1)
                if has(3):
                    turned(g + 3, (u + 3) % TS, i + (u + 3) // TS)
                if has(2):
                    exponential(g + 2, (u + 2) % TS)
                if has(-1):
                    sums_turned(g - 1, (u - 1) % TS, i)
                if has(0):
                    gate(g, u, 0)

            stream(act, step)

        @block.vector
        def _(dve):
            dve.sem_inc(g_gate, 4)
            dve.sem_inc(acc_step, 2 * NV)
            dve.sem_inc(scan_done, 1)
            dve.wait_ge(weights, 64)

            def normed(t, v):
                dve.wait_ge(t_ready, t + 1)
                normalise(k, XN[:, v % 2, :], t).then_inc(xn_ready, 1)

            def gates(t, v):
                ch = Chain(dve, gate_step, t * 4)
                dve.wait_ge(g_exp, t + 2)
                dve.wait_ge(gated_ready, t * 2 + 2)
                ch.step(nc.vector.tensor_scalar(G[:, v, :], eg[:, v, :], 1.0, None, ALU.add))
                ch.step(nc.vector.reciprocal(G[:, v, :], G[:, v, :]))
                dve.wait_ge(ra_ready, t * 2 + 2)
                ch.step(nc.vector.tensor_reduce(A[:, v, :], G[:, v, :].rearrange("p (h e) -> p e h", e=E0), AX.X, ALU.add))
                ch.step(nc.vector.tensor_scalar(A[:, v, :], A[:, v, :], 1.0, -1.0, ALU.min, ALU.mult))
                nc.vector.tensor_scalar(A[:, v, :], A[:, v, :], 1.0, None, ALU.add).then_inc(g_gate, 1)

            def head_sum(t, v):
                dve.wait_ge(kv_ready, t + 1 + 4)
                dve.wait_ge(ra_ready, t * 2 + 5)
                for h in range(H0):
                    if h == H0 // 2:
                        dve.wait_ge(gated_ready, t * 2 + 1 + 8)
                    for e in range(EV):
                        g = G[:, v, h * E0 + e:h * E0 + e + 1]
                        kv = psKV[v % 2][h // 4][:, h % 4, :]
                        if h == 0:
                            ins = nc.vector.tensor_scalar(acc[:, v % 2, e, :], kv, g, None, ALU.mult)
                        else:
                            dve.wait_ge(acc_step, t * NV + (h * EV + e - EV + 1 + 2 * NV))
                            ins = nc.vector.scalar_tensor_tensor(acc[:, v % 2, e, :], kv, g, acc[:, v % 2, e, :],
                                                                 ALU.mult, ALU.add)
                        ins.then_inc(acc_step, 1)

            def scan(i):
                ch = Chain(dve, scan_step, i * 3)
                dve.wait_ge(ra_evac, i * 2 * TS + 2 * TS + 2)
                gs = gT[:, :, :].rearrange("p e (l c) -> p e l c", c=T // L0)[:, :, :, 0]
                As = AT[:, :, :].rearrange("p e (l c) -> p e l c", c=T // L0)[:, :, :, 0]
                ch.step(nc.vector.tensor_tensor(seed[:, :, :], As, ikv[:, :, :], ALU.mult))
                ch.step(nc.vector.tensor_tensor(gs, gs, seed[:, :, :], ALU.add))
                ch.step(nc.vector.memset(As, 0.0))
                for e in range(E0):
                    n = nc.vector.tensor_tensor_scan(k.Rec[:, bass.ds(i, 1), L0:WIN, e].rearrange("p a t -> p (a t)"),
                                                     AT[:, e, :], gT[:, e, :], 0.0, ALU.mult, ALU.add)
                n.then_inc(scan_done, 1)

            def step(i, u, has):
                g = i * TS + u
                if has(4):
                    normed(g + 4, u)
                if has(1):
                    gates(g + 1, (u + 1) % TS)
                if has(0):
                    head_sum(g, u)
                if u == 0 and has(-1):
                    scan(i - 1)

            stream(dve, step)


def window_attention(k):
    nc, a = k.nc, k.a
    QB = 32
    NQ = T // QB
    KW = 2 * L0
    NG = (NQ + 1 + 3) // 4
    MADE = 4 + NG
    SP2 = 2 * NQ
    at = {1: 0, 4: 1, 7: 2, 10: 3, 11: 4, 12: 5, 13: 6, 14: 7, 15: 8}
    scale = 1.0 / 8.0
    with ExitStack() as ctx:
        wq = k.sb(ctx, "wq", [P, KC, H0 * DK])
        wo = k.sb(ctx, "wo", [P, 4, D])
        mask_f = k.sb(ctx, "mask_f", [QB, E0 * KW])
        mask = k.sb(ctx, "mask", [QB, E0 * KW], BF16)
        sel_f = k.sb(ctx, "sel_f", [QB, P])
        sel = k.sb(ctx, "sel", [QB, P], BF16)
        R = k.sb(ctx, "R", [P, WIN, E0])
        XS = k.sb(ctx, "XS", [P, KC, T])
        QT = [k.sb(ctx, f"QT{r}", [DK, 2, NQ, 4, QB]) for r in range(2)]
        V = [k.sb(ctx, f"V{r}", [P, NQ + 1, DK]) for r in range(2)]
        mx = k.sb(ctx, "mx", [P, 2, 2])
        nm = k.sb(ctx, "nm", [P, 2, 2])
        sums = k.sb(ctx, "sums", [P, 4, 2])
        rs = k.sb(ctx, "rs", [P, 2, 2])
        probs = k.sb(ctx, "probs", [P, 2, 2, E0 * KW])
        PT = k.sb(ctx, "PT", [P, 2, 2, 2, P])
        Y = k.sb(ctx, "Y", [P, 2, 2, DK])
        YT = k.sb(ctx, "YT", [P, 4, T])
        psS = [k.ps(ctx, f"psS{s}", [P, 2, E0 * KW]) for s in range(2)]
        psP = [k.ps(ctx, f"psP{s}", [P, 2, 2, P]) for s in range(2)]
        psO = k.ps(ctx, "psO", [P, 2, DK])
        psY = k.ps(ctx, "psY", [P, 4, QB])
        psZ = k.ps(ctx, "psZ", [P, D])
        psB = k.ps(ctx, "psB", [P, T])
        weights, casts = k.sem(ctx, "w_weights"), k.sem(ctx, "w_casts")
        r_ready, x_ready = k.sem(ctx, "w_r_ready"), k.sem(ctx, "w_x_ready")
        b_ready, b_evac = k.sem(ctx, "w_b_ready"), k.sem(ctx, "w_b_evac")
        s_ready, m_ready, e_done = k.sem(ctx, "w_s_ready"), k.sem(ctx, "w_m_ready"), k.sem(ctx, "w_e_done")
        p_ready, p_evac = k.sem(ctx, "w_p_ready"), k.sem(ctx, "w_p_evac")
        o_ready, o_evac = k.sem(ctx, "w_o_ready"), k.sem(ctx, "w_o_evac")
        y_ready, y_evac = k.sem(ctx, "w_y_ready"), k.sem(ctx, "w_y_evac")
        z_ready, z_added = k.sem(ctx, "w_z_ready"), k.sem(ctx, "w_z_added")
        dstep = k.sem(ctx, "w_dstep")
        block = ctx.enter_context(nc.Block())

        def turns(eng, step, ends):
            for s in range(SP2):
                step(0, s, s)
            with eng.Fori(1, NB // 2) as j:
                for s in range(SP2):
                    step(j, s, SP2)
            for s in range(ends):
                step(NB // 2, s, -1)

        class At:
            def __init__(self, j, s, lag):
                w = s - lag
                self.g = j * SP2 + w
                self.r, self.q = (w % SP2) // NQ, w % NQ
                self.t = j * 2 + w // NQ

        def lagging(j, s, late, lag):
            if late >= 0 and lag > late or late < 0 and lag <= s:
                return None
            return At(j, s, lag)

        @block.sync
        def _(sp):
            sp.dma_start(wq[:, :, :], a["wq"].rearrange("(k p) n -> p k n", p=P)).then_inc(weights, 16)
            sp.dma_start(wo[:, :, :], a["wo"].rearrange("(k p) n -> p k n", p=P)).then_inc(weights, 16)
            sp.dma_start(mask_f[:, :], a["mask"]).then_inc(weights, 16)
            sp.dma_start(sel_f[:, :], a["sel"]).then_inc(weights, 16)
            sp.dma_start(XS[:, :, :], k.xT_dram[:, :, 0:T]).then_inc(x_ready, 16)
            with sp.Fori(1, NB) as t:
                sp.wait_ge(b_ready, t * MADE - MADE + 4)
                sp.dma_start(XS[:, :, :], k.xT_dram[:, :, bass.ds(t * T, T)]).then_inc(x_ready, 16)
            sp.wait_ge(b_ready, NB * MADE - MADE + 4)
            sp.dma_start(XS[:, :, :], k.xT_dram[:, :, (NB - 1) * T:]).then_inc(x_ready, 16)

        @block.gpsimd
        def _(pool):
            def fetch(t):
                nc.gpsimd.tensor_copy(R[:, :, :].rearrange("p t e -> p (t e)"),
                                      k.Rec[:, bass.ds(t, 1), :, :].rearrange("p a t e -> p (a t e)")).then_inc(r_ready, 1)
            fetch(0)
            with pool.Fori(1, NB) as t:
                pool.wait_ge(b_ready, t * MADE)
                pass_gate(k, pool)
                fetch(t)
            pool.wait_ge(b_ready, NB * MADE)
            fetch(NB - 1)

        @block.tensor
        def _(pe):
            pe.sem_inc(p_ready, 2)
            pe.sem_inc(o_ready, 2)
            pe.sem_inc(y_ready, 2)
            pe.sem_inc(z_ready, 4)
            pe.wait_ge(weights, 64)
            pe.wait_ge(casts, 2)

            def make(t, r, n):
                pe.wait_ge(b_evac, t * MADE + n + 1)
                if n < 4:
                    pe.wait_ge(x_ready, t * 16 + 16)
                    for c in range(KC):
                        mm = pe.matmul(psB[:, :], wq[:, c, n * P:(n + 1) * P], XS[:, c, :],
                                       start=(c == 0), stop=(c == KC - 1))
                else:
                    if n == 4:
                        pe.wait_ge(r_ready, t + 1)
                    for q in range(4 * (n - 4), min(4 * (n - 4) + 4, NQ + 1)):
                        mm = pe.transpose(psB[:, q % 4 * P:(q % 4 + 1) * P],
                                          R[:, q * QB:(q + 1) * QB, :].rearrange("d t e -> d (t e)"), k.ident[:, :])
                mm.then_inc(b_ready, 1)

            def scores(b):
                if b.q == 0:
                    pe.wait_ge(b_evac, b.t * MADE + 4 + 1)
                pe.wait_ge(e_done, b.g * 2 + 2)
                pass_gate(k, pe)
                for hg in range(2):
                    o = psS[b.q % 2][:, hg, :]
                    pe.matmul(o, QT[b.r][:, hg, b.q, :, :].rearrange("d h t -> d (h t)"),
                              k.Rec[0:DK, bass.ds(b.t, 1), b.q * QB:b.q * QB + KW, :].rearrange("d a t e -> d (a t e)"),
                              start=(hg == 0), stop=False, skip_group_check=True)
                    mm = pe.matmul(o, sel[:, :], mask[:, :], start=False, stop=(hg == 1), skip_group_check=True)
                mm.then_inc(s_ready, 1)

            def transposes(b):
                pe.wait_ge(e_done, b.g * 2 + 2 + 4)
                pe.wait_ge(p_evac, b.g + 1)
                for hg in range(2):
                    for kt in range(2):
                        mm = pe.transpose(psP[b.q % 2][:, hg, kt, :], probs[:, b.q % 2, hg, kt * P:(kt + 1) * P], k.ident[:, :])
                mm.then_inc(p_ready, 1)

            def values(b):
                if b.q == 0:
                    pe.wait_ge(b_evac, b.t * MADE + MADE + 1)
                pe.wait_ge(p_evac, b.g + 1 + 2)
                pe.wait_ge(o_evac, b.g + 1)
                for hg in range(2):
                    for kt in range(2):
                        mm = pe.matmul(psO[:, hg, :], PT[:, b.q % 2, hg, kt, :], V[b.r][:, b.q + kt, :],
                                       start=(hg == 0 and kt == 0), stop=(hg == 1 and kt == 1), skip_group_check=True)
                mm.then_inc(o_ready, 1)

            def turn(b):
                pe.wait_ge(o_evac, b.g + 1 + 1)
                pe.wait_ge(y_evac, b.g + 1)
                pe.transpose(psY[:, :, :], Y[:, b.q % 2, :, :].rearrange("p g d -> p (g d)"),
                             k.ident[:, :]).then_inc(y_ready, 1)

            def project(b):
                u = b.q // 4
                pe.wait_ge(y_evac, b.g + 1 + 1)
                pe.wait_ge(z_added, b.t * TS + u + 1)
                for c in range(4):
                    mm = pe.matmul(psZ[:, :], YT[:, c, u * P:(u + 1) * P], wo[:, c, :], start=(c == 0), stop=(c == 3))
                mm.then_inc(z_ready, 1)

            def step(j, s, late):
                if late >= 0:
                    b = At(j, s, 0)
                    scores(b)
                if b1 := lagging(j, s, late, 1):
                    transposes(b1)
                if b2 := lagging(j, s, late, 2):
                    values(b2)
                if b3 := lagging(j, s, late, 3):
                    turn(b3)
                b4 = lagging(j, s, late, 4)
                if b4 and b4.q % 4 == 3:
                    project(b4)
                if late >= 0 and b.q in at:
                    make(b.t + 1, 1 - b.r, at[b.q])

            for n in range(MADE):
                make(0, 0, n)
            turns(pe, step, 5)

        @block.scalar
        def _(act):
            act.sem_inc(b_evac, 1)
            act.sem_inc(e_done, 4)
            act.sem_inc(y_evac, 1)

            def made(t, r, n):
                act.wait_ge(b_ready, t * MADE + n + 1)
                if n < 4:
                    for x in range(2):
                        ins = nc.scalar.copy(QT[r][:, n // 2, :, 2 * n % 4 + x, :],
                                             psB[x * DK:(x + 1) * DK, :].rearrange("d (b t) -> d b t", b=NQ))
                else:
                    g = n - 4
                    w = min(4, NQ + 1 - 4 * g)
                    ins = nc.scalar.copy(V[r][:, 4 * g:4 * g + w, :],
                                         psB[:, 0:w * P].rearrange("p (w c) -> p w c", c=P)[:, :, DK:P])
                ins.then_inc(b_evac, 1)

            def exponentials(b):
                act.wait_ge(m_ready, b.g + 1)
                act.wait_ge(p_ready, b.g + 1)
                for hg in range(2):
                    nc.scalar.activation(probs[:, b.q % 2, hg, :], psS[b.q % 2][:, hg, :], ACT.Exp,
                                         bias=nm[:, b.q % 2, hg:hg + 1], scale=scale,
                                         accum_out=sums[:, b.q % 4, hg:hg + 1]).then_inc(e_done, 1)

            def turned(b):
                act.wait_ge(y_ready, b.g + 1 + 2)
                act.wait_ge(z_ready, b.t * TS + b.q // 4 + 1)
                nc.scalar.copy(YT[:, :, b.q * QB:(b.q + 1) * QB], psY[:, :, :]).then_inc(y_evac, 1)

            def step(j, s, late):
                if late >= 0:
                    b = At(j, s, 0)
                    exponentials(b)
                if b3 := lagging(j, s, late, 3):
                    turned(b3)
                if late >= 0 and b.q in at:
                    made(b.t + 1, 1 - b.r, at[b.q])

            for n in range(MADE):
                made(0, 0, n)
            turns(act, step, 4)

        @block.vector
        def _(dve):
            dve.wait_ge(weights, 64)
            nc.vector.tensor_copy(mask[:, :], mask_f[:, :]).then_inc(casts, 1)
            nc.vector.tensor_copy(sel[:, :], sel_f[:, :]).then_inc(casts, 1)
            dve.sem_inc(p_evac, 2)
            dve.sem_inc(o_evac, 1)
            dve.sem_inc(z_added, 1)

            def maxima(b, ch):
                dve.wait_ge(s_ready, b.g + 1)
                dve.wait_ge(e_done, b.g * 2 + 2)
                ch.step(nc.vector.tensor_reduce(mx[:, b.q % 2, :], psS[b.q % 2][:, :, :], AX.X, ALU.max))
                nc.vector.tensor_scalar(nm[:, b.q % 2, :], mx[:, b.q % 2, :], -scale, None, ALU.mult).then_inc(m_ready, 1)

            def turned(b):
                dve.wait_ge(p_ready, b.g + 1 + 2)
                dve.wait_ge(o_ready, b.g + 1)
                nc.vector.tensor_copy(PT[:, b.q % 2, :, :, :], psP[b.q % 2][:, :, :, :]).then_inc(p_evac, 1)

            def divided(b, ch):
                ch.step(nc.vector.reciprocal(rs[:, b.q % 2, :], sums[:, b.q % 4, :]))
                dve.wait_ge(o_ready, b.g + 1 + 2)
                dve.wait_ge(y_ready, b.g + 1)
                nc.vector.tensor_tensor(Y[:, b.q % 2, :, :], psO[:, :, :], bc(rs[:, b.q % 2, :].unsqueeze(2), [P, 2, DK]),
                                        ALU.mult).then_inc(o_evac, 1)

            def add(b, ch):
                n = b.t * TS + b.q // 4
                dve.wait_ge(z_ready, n + 1 + 4)
                x = k.X[:, bass.ds(n, 1), :].rearrange("p a c -> p (a c)")
                ch.step(nc.vector.tensor_tensor(x, x, psZ[:, :], ALU.add))
                pass_gate(k, dve)
                nc.vector.bn_stats(k.BST[:, bass.ds(n, 1), :].rearrange("p a c -> p (a c)"), x).then_inc(z_added, 1)

            chains = {}

            def step(j, s, late):
                if s == 0:
                    done = chains[0].n if chains else 0
                    NST = SP2 * 2 + 2 * TS
                    chains[len(chains)] = Chain(dve, dstep, (j - 1) * NST + done if chains else 0)
                ch = chains[len(chains) - 1]
                if late >= 0:
                    maxima(At(j, s, 0), ch)
                if b1 := lagging(j, s, late, 1):
                    turned(b1)
                if b2 := lagging(j, s, late, 2):
                    divided(b2, ch)
                b5 = lagging(j, s, late, 5)
                if b5 and b5.q % 4 == 3:
                    add(b5, ch)
                if s == SP2 - 1 and len(chains) == 2:
                    assert ch.n == SP2 * 2 + 2 * TS

            turns(dve, step, 6)


def position_qkv(k):
    nc, a = k.nc, k.a
    with ExitStack() as ctx:
        wqkv = k.sb(ctx, "wqkv", [P, KC, QKVW])
        lnw, lnb = k.sb(ctx, "ln1w", [P, KC]), k.sb(ctx, "ln1b", [P, KC])
        bst = k.sb(ctx, "p_bst", [P, TS, 6])
        mean, var = k.sb(ctx, "p_mean", [P, TS]), k.sb(ctx, "p_var", [P, TS])
        tmp, rstd = k.sb(ctx, "p_tmp", [P, TS]), k.sb(ctx, "p_rstd", [P, TS])
        XN = k.sb(ctx, "p_XN", [P, TS, D])
        XT = k.sb(ctx, "p_XT", [P, KC, T])
        psT = [k.ps(ctx, f"p_psT{c}", [P, T]) for c in range(KC)]
        psQ = [k.ps(ctx, f"p_psQ{s}", [P, QKVW]) for s in range(4)]
        weights = k.sem(ctx, "p_weights")
        steps, var_ready, root = k.sem(ctx, "p_steps"), k.sem(ctx, "p_var_ready"), k.sem(ctx, "p_root")
        xn_ready, t_ready, t_evac = k.sem(ctx, "p_xn_ready"), k.sem(ctx, "p_t_ready"), k.sem(ctx, "p_t_evac")
        q_ready, q_evac = k.sem(ctx, "p_q_ready"), k.sem(ctx, "p_q_evac")
        block = ctx.enter_context(nc.Block())

        @block.sync
        def _(sp):
            sp.dma_start(wqkv[:, :, :], a["qkv1"].rearrange("(k p) n -> p k n", p=P)).then_inc(weights, 16)
            sp.dma_start(lnw[:, :], a["ln1w"]).then_inc(weights, 16)
            sp.dma_start(lnb[:, :], a["ln1b"]).then_inc(weights, 16)

        @block.gpsimd
        def _(pool):
            with pool.Fori(0, NB) as i:
                pool.wait_ge(var_ready, i + 1)
                nc.gpsimd.tensor_tensor(rstd[:, :], var[:, :], k.mhalf[:, 0:TS], ALU.pow).then_inc(root, 1)

        @block.vector
        def _(dve):
            NST = TS * 2 + 6
            with dve.Fori(0, NB) as i:
                ch = Chain(dve, steps, i * NST)
                for u in range(TS):
                    hs = k.HS[:, bass.ds(i * TS + u, 1), :].rearrange("p a c -> p (a c)")
                    n = ch.mark(normalise(k, hs, i * TS + u))
                    ch.after(n)
                    pass_gate(k, dve)
                    n = ch.mark(nc.vector.bn_stats(bst[:, u, :], hs))
                ch.after(n)
                stats_steps(nc, ch, bst[:, :, :], mean[:, :], var[:, :], tmp[:, :], var_ready)
                dve.wait_ge(root, i + 1)
                dve.wait_ge(t_ready, i + 1)
                for u in range(TS):
                    hs = k.HS[:, bass.ds(i * TS + u, 1), :].rearrange("p a c -> p (a c)")
                    nc.vector.tensor_scalar(XN[:, u, :], hs, mean[:, u:u + 1], rstd[:, u:u + 1],
                                            ALU.subtract, ALU.mult).then_inc(xn_ready, 1)
                assert ch.n == NST

        @block.tensor
        def _(pe):
            pe.sem_inc(t_ready, 1)
            pe.sem_inc(q_ready, 4)
            pe.wait_ge(weights, 48)
            with pe.Fori(0, NB) as i:
                pe.wait_ge(t_evac, i * 2 + 2)
                for u in range(TS):
                    pe.wait_ge(xn_ready, i * TS + u + 1)
                    for c in range(KC):
                        mm = pe.transpose(psT[c][:, u * P:(u + 1) * P], XN[:, u, c * P:(c + 1) * P], k.ident[:, :])
                mm.then_inc(t_ready, 1)
                pe.wait_ge(t_evac, i * 2 + 4)
                for u in range(TS):
                    pe.wait_ge(q_evac, i * TS + u + 1)
                    for c in range(KC):
                        mm = pe.matmul(psQ[u][:, :], XT[:, c, u * P:(u + 1) * P], wqkv[:, c, :],
                                       start=(c == 0), stop=(c == KC - 1))
                    mm.then_inc(q_ready, 1)

        @block.scalar
        def _(act):
            act.sem_inc(t_evac, 2)
            act.sem_inc(q_evac, 4)
            act.wait_ge(weights, 48)
            with act.Fori(0, NB) as i:
                act.wait_ge(t_ready, i + 2)
                act.wait_ge(q_ready, i * TS + 4)
                for c in range(KC):
                    nc.scalar.activation(XT[:, c, :], psT[c][:, :], ACT.Identity, bias=lnb[:, c:c + 1],
                                         scale=lnw[:, c:c + 1]).then_inc(t_evac, 1)
                for u in range(TS):
                    act.wait_ge(q_ready, i * TS + u + 1 + 4)
                    nc.scalar.copy(k.QKV[:, bass.ds(i * TS + u, 1), :].rearrange("p a c -> p (a c)"),
                                   psQ[u][:, :]).then_inc(q_evac, 1)


def position_attention(k):
    nc, a = k.nc, k.a
    S = NB
    G = 4

    def units(rows):
        return [(s, t, min(t + G, s + 1)) for s in rows for t in range(0, s + 1, G)]

    own_rows_s, own_rows_v = (1, 7), (2, 7)
    score_units = units([s for s in range(S) if s not in own_rows_s])
    value_units = units([s for s in range(S) if s not in own_rows_v])
    own_scores, own_values = units(own_rows_s), units(own_rows_v)
    NU = len(score_units)
    assert NU == len(value_units) == 9 and len(own_values) == 3
    with ExitStack() as ctx:
        wp = k.sb(ctx, "wp", [P, KC, D])
        wr = k.sb(ctx, "wr", [P, KC, NE])
        lnw, lnb = k.sb(ctx, "rl_w", [P, KC]), k.sb(ctx, "rl_b", [P, KC])
        sc = k.sb(ctx, "sc", [P, S, S, NH])
        PR = k.sb(ctx, "a_PR", [P, S, S, NH])
        mx = k.sb(ctx, "a_mx", [P, S, NH])
        prodS = k.sb(ctx, "prodS", [P, 3, G, D])
        prodV = k.sb(ctx, "prodV", [P, 3, G, D])
        ownS = k.sb(ctx, "ownS", [P, G, D])
        ownV = k.sb(ctx, "ownV", [P, 3, G, D])
        AT = k.sb(ctx, "o_AT", [P, 2, KC, P])
        mean, var = k.sb(ctx, "o_mean", [P, S]), k.sb(ctx, "o_var", [P, S])
        tmp, rstd = k.sb(ctx, "o_tmp", [P, S]), k.sb(ctx, "o_rstd", [P, S])
        XN = k.sb(ctx, "o_XN", [P, 4, D])
        XT = k.sb(ctx, "o_XT", [P, 2, KC, P])
        psA = [k.ps(ctx, f"o_psA{s}", [P, KC, P]) for s in range(2)]
        psH = [k.ps(ctx, f"o_psH{s}", [P, D]) for s in range(2)]
        psT = [k.ps(ctx, f"o_psT{s}", [P, KC, P]) for s in range(2)]
        psL = k.ps(ctx, "o_psL", [P, S, NE])
        weights, steps = k.sem(ctx, "a_weights"), k.sem(ctx, "a_steps")
        s_made, s_summed = k.sem(ctx, "a_s_made"), k.sem(ctx, "a_s_summed")
        sub_ready, exp_ready, p_ready = k.sem(ctx, "a_sub"), k.sem(ctx, "a_exp"), k.sem(ctx, "a_p")
        v_made, v_used = k.sem(ctx, "a_v_made"), k.sem(ctx, "a_v_used")
        own_made, own_used = k.sem(ctx, "a_own_made"), k.sem(ctx, "a_own_used")
        a_evac = k.sem(ctx, "a_a_evac")
        h_ready, h_added = k.sem(ctx, "a_h_ready"), k.sem(ctx, "a_h_added")
        var_ready, root = k.sem(ctx, "a_var_ready"), k.sem(ctx, "a_root")
        xn_ready, t_ready, t_evac = k.sem(ctx, "a_xn_ready"), k.sem(ctx, "a_t_ready"), k.sem(ctx, "a_t_evac")
        l_ready, l_copied = k.sem(ctx, "a_l_ready"), k.sem(ctx, "a_l_copied")
        block = ctx.enter_context(nc.Block())

        def turns(eng, turn):
            turn(0, True, False, False)
            turn(1, True, True, False)
            with eng.Fori(2, TS) as i:
                turn(i, True, True, True)
            turn(TS, False, True, True)
            turn(TS + 1, False, False, True)

        def row(s, bt):
            return k.QKV[:, bass.ds(bt + s * TS, 1), :].rearrange("p a (g c) -> p (a g) c", g=NKV)

        def fwd(x):
            return x.rearrange("p (g j d) -> p g j d", g=NKV, j=QG)

        def score_product(eng, dst, bt, s, t):
            q = row(s, bt)[:, :, 0:QG * HD].rearrange("p g (j d) -> p g j d", j=QG)
            kk = row(t, bt)[:, :, QG * HD:QG * HD + HD].unsqueeze(2)
            return eng.tensor_tensor(fwd(dst), q, bc(kk, [P, NKV, QG, HD]), ALU.mult)

        def value_product(eng, dst, bt, s, t):
            v = row(t, bt)[:, :, QG * HD + HD:].unsqueeze(2)
            p = PR[:, s, t, :].rearrange("p (g j) -> p g j", g=NKV).unsqueeze(3)
            return eng.tensor_tensor(fwd(dst), bc(p, [P, NKV, QG, HD]), bc(v, [P, NKV, QG, HD]), ALU.mult)

        @block.sync
        def _(sp):
            sp.dma_start(wp[:, :, :], a["proj"].rearrange("(k p) n -> p k n", p=P)).then_inc(weights, 16)
            sp.dma_start(wr[:, :, :], a["router"].rearrange("(k p) n -> p k n", p=P)).then_inc(weights, 16)
            sp.dma_start(lnw[:, :], a["ln2w"]).then_inc(weights, 16)
            sp.dma_start(lnb[:, :], a["ln2b"]).then_inc(weights, 16)

        @block.gpsimd
        def _(pool):
            def turn(i, entering, leaving, last):
                for m in range(NU + 3):
                    if entering and m < NU:
                        s, t0, t1 = score_units[m]
                        pool.wait_ge(s_summed, i * NU + m + 1)
                        pass_gate(k, pool)
                        for t in range(t0, t1):
                            ins = score_product(nc.gpsimd, prodS[:, m % 3, t - t0, :], i, s, t)
                        ins.then_inc(s_made, 1)
                    n = m - 3
                    if leaving and n >= 0:
                        s, t0, t1 = value_units[n]
                        if n == 0:
                            pool.wait_ge(p_ready, i)
                        pool.wait_ge(v_used, i * NU - NU + n + 1)
                        pass_gate(k, pool)
                        for t in range(t0, t1):
                            ins = value_product(nc.gpsimd, prodV[:, n % 3, t - t0, :], i - 1, s, t)
                        ins.then_inc(v_made, 1)

            turns(pool, turn)

        @block.tensor
        def _(pe):
            pe.sem_inc(v_used, 3)
            pe.sem_inc(own_used, 3)
            pe.wait_ge(weights, 64)

            def attended(j, s):
                pe.wait_ge(a_evac, j * S + s + 1)
                own = s in own_rows_v
                us = own_values if own else value_units
                for n, (s_, t0, t1) in enumerate(us):
                    if s_ != s:
                        continue
                    pe.wait_ge(own_made if own else v_made, j * len(us) + n + 1)
                    src = ownV[:, n, :, :] if own else prodV[:, n % 3, :, :]
                    for t in range(t0, t1):
                        for c in range(KC):
                            mm = pe.matmul(psA[s % 2][:, c, :], src[:, t - t0, c * P:(c + 1) * P], k.ident[:, :],
                                           start=(t == 0 and c == 0), stop=(t == s and c == KC - 1), skip_group_check=True)
                    mm.then_inc(own_used if own else v_used, 1)

            def project(j, s):
                pe.wait_ge(a_evac, j * S + s + 1 + 2)
                pe.wait_ge(h_added, j * S + s + 1)
                for c in range(KC):
                    mm = pe.matmul(psH[s % 2][:, :], AT[:, s % 2, c, :], wp[:, c, :], start=(c == 0), stop=(c == KC - 1))
                mm.then_inc(h_ready, 1)

            def turned(j, s):
                pe.wait_ge(xn_ready, j * S + s + 1)
                pe.wait_ge(t_evac, (j * S + s) * KC + KC)
                for c in range(KC):
                    mm = pe.transpose(psT[s % 2][:, c, :], XN[:, s % 4, c * P:(c + 1) * P], k.ident[:, :])
                mm.then_inc(t_ready, 1)

            def logits(j, s):
                pe.wait_ge(t_evac, (j * S + s) * KC + KC + 2 * KC)
                if s == 0:
                    pe.wait_ge(l_copied, j + 1)
                for c in range(KC):
                    mm = pe.matmul(psL[:, s, :], XT[:, s % 2, c, :], wr[:, c, :],
                                   start=(s == 0 and c == 0), stop=(s == S - 1 and c == KC - 1), skip_group_check=True)
                mm.then_inc(l_ready, 1)

            def turn(i, entering, leaving, last):
                for s in range(S + 1):
                    if leaving and s < S:
                        attended(i - 1, s)
                    if last and s < S:
                        turned(i - 2, s)
                    if leaving and s >= 1:
                        project(i - 1, s - 1)
                    if last and s >= 1:
                        logits(i - 2, s - 1)

            turns(pe, turn)

        @block.scalar
        def _(act):
            act.sem_inc(a_evac, 2)
            act.sem_inc(t_evac, 2 * KC)
            act.sem_inc(l_copied, 1)
            act.wait_ge(weights, 64)

            def turn(i, entering, leaving, last):
                if last:
                    act.wait_ge(var_ready, i - 1)
                    nc.scalar.activation(var[:, :], var[:, :], ACT.Sqrt).then_inc(root, 1)
                for s in range(S):
                    if leaving:
                        j, own = i - 1, s in own_rows_v
                        n = sum(s_ <= s for s_, _, _ in (own_values if own else value_units))
                        act.wait_ge(own_used if own else v_used, j * (3 if own else NU) + n + 3)
                        act.wait_ge(h_ready, j * S + s + 1)
                        nc.scalar.copy(AT[:, s % 2, :, :], psA[s % 2][:, :, :]).then_inc(a_evac, 1)
                    if last:
                        j = i - 2
                        act.wait_ge(t_ready, j * S + s + 1 + 4)
                        act.wait_ge(l_ready, j * S + s + 1)
                        for c in range(KC):
                            nc.scalar.activation(XT[:, s % 2, c, :], psT[s % 2][:, c, :], ACT.Identity,
                                                 bias=lnb[:, c:c + 1], scale=lnw[:, c:c + 1]).then_inc(t_evac, 1)
                    if entering and s == S - 2:
                        act.wait_ge(sub_ready, i + 1)
                        nc.scalar.activation(sc[:, :, :, :], sc[:, :, :, :], ACT.Exp, scale=0.25).then_inc(exp_ready, 1)
                if last:
                    act.wait_ge(l_ready, j * S + S + 2)
                    nc.scalar.copy(k.LG[:, :, bass.ds(j, 1), :].rearrange("p s a e -> p s (a e)"),
                                   psL[:, :, :]).then_inc(l_copied, 1)

            turns(act, turn)

        @block.vector
        def _(dve):
            dve.sem_inc(s_summed, 3)
            dve.sem_inc(h_added, 2)
            dve.sem_inc(h_ready, 2)
            dve.sem_inc(t_ready, 4)
            dve.sem_inc(l_ready, 2)
            by_t = sc[:, :, :, :].rearrange("p s t h -> p s h t")
            by_t_p = PR[:, :, :, :].rearrange("p s t h -> p s h t")

            def summed(src, s, t0, t1):
                return nc.vector.tensor_reduce(sc[:, s, t0:t1, :], src[:, 0:t1 - t0, :].rearrange(
                    "p t (h d) -> p t h d", d=HD), AX.X, ALU.add)

            def own_score(i, n, ch):
                s, t0, t1 = own_scores[n]
                for t in range(t0, t1):
                    m = ch.mark(score_product(nc.vector, ownS[:, t - t0, :], i, s, t))
                ch.after(m)
                ch.step(summed(ownS, s, t0, t1))

            def own_value(j, n):
                s, t0, t1 = own_values[n]
                dve.wait_ge(own_used, j * 3 + n + 1)
                pass_gate(k, dve)
                for t in range(t0, t1):
                    ins = value_product(nc.vector, ownV[:, n, t - t0, :], j, s, t)
                ins.then_inc(own_made, 1)

            def probabilities(i, leaving, ch):
                dve.wait_ge(exp_ready, i + 1)
                ch.step(nc.vector.tensor_reduce(mx[:, :, :], by_t, AX.X, ALU.add))
                ch.step(nc.vector.reciprocal(mx[:, :, :], mx[:, :, :]))
                if leaving:
                    dve.wait_ge(v_made, i * NU)
                    dve.wait_ge(own_made, i * 3)
                nc.vector.tensor_tensor(by_t_p, by_t, bc(mx[:, :, :].unsqueeze(3), [P, S, NH, S]),
                                        ALU.mult).then_inc(p_ready, 1)
                dve.wait_ge(p_ready, i + 1)

            def add(j, s, ch):
                dve.wait_ge(h_ready, j * S + s + 1 + 2)
                hs = k.HS[:, bass.ds(j + s * TS, 1), :].rearrange("p a c -> p (a c)")
                ch.step(nc.vector.tensor_tensor(hs, hs, psH[s % 2][:, :], ALU.add))
                pass_gate(k, dve)
                nc.vector.bn_stats(k.BST[:, bass.ds(j + s * TS, 1), :].rearrange("p a c -> p (a c)"), hs).then_inc(h_added, 1)

            def statistics(j, ch):
                dve.wait_ge(h_added, j * S + S + 2)
                bst = k.BST[:, :, :].rearrange("p (s t) w -> p s t w", t=TS)[:, :, bass.ds(j, 1), :].rearrange(
                    "p s a w -> p s (a w)")
                stats_steps(nc, ch, bst, mean[:, :], var[:, :], tmp[:, :], var_ready)
                dve.wait_ge(root, j + 1)
                ch.step(nc.vector.reciprocal(rstd[:, :], var[:, :]))

            def normed(j, s):
                dve.wait_ge(t_ready, j * S + s + 1)
                hs = k.HS[:, bass.ds(j + s * TS, 1), :].rearrange("p a c -> p (a c)")
                nc.vector.tensor_scalar(XN[:, s % 4, :], hs, mean[:, s:s + 1], rstd[:, s:s + 1],
                                        ALU.subtract, ALU.mult).then_inc(xn_ready, 1)

            ENTER, LEAVE, LAST = 1 + 10 + 3 + 1 + 2, S, 6 + 1
            own_score_at, own_value_at = {0: 0, 2: 1, 4: 2}, {1: 0, 5: 1, 6: 2}
            add_at = {3: 0, 4: 1, 5: 2, 6: 3, 8: 4}

            def turn(i, entering, leaving, last):
                before = ENTER * min(i, TS) + LEAVE * max(i - 1, 0) if isinstance(i, int) else i * (ENTER + LEAVE) - LEAVE
                before = before + (i - 2) * LAST if last else before
                ch = Chain(dve, steps, before)
                if entering:
                    ch.step(nc.vector.memset(sc[:, :, :, :], NEG))
                for n in range(NU):
                    if entering:
                        s, t0, t1 = score_units[n]
                        dve.wait_ge(s_made, i * NU + n + 1)
                        summed(prodS[:, n % 3, :, :], s, t0, t1).then_inc(s_summed, 1)
                        if n in own_score_at:
                            own_score(i, own_score_at[n], ch)
                    if last and n == 0:
                        statistics(i - 2, ch)
                    if leaving and n in own_value_at:
                        own_value(i - 1, own_value_at[n])
                    if last and n >= 1:
                        normed(i - 2, n - 1)
                    if leaving and n in add_at:
                        add(i - 1, add_at[n], ch)
                if entering:
                    dve.wait_ge(s_summed, i * NU + NU + 3)
                    ch.step(nc.vector.tensor_reduce(mx[:, :, :], by_t, AX.X, ALU.max))
                    nc.vector.tensor_tensor(by_t, by_t, bc(mx[:, :, :].unsqueeze(3), [P, S, NH, S]),
                                            ALU.subtract).then_inc(sub_ready, 1)
                if leaving:
                    add(i - 1, 5, ch)
                if entering:
                    probabilities(i, leaving, ch)
                if leaving:
                    for s in range(6, S):
                        add(i - 1, s, ch)
                assert ch.n == ENTER * entering + LEAVE * leaving + LAST * last, ch.n

            turns(dve, turn)


def route(k):
    nc, a = k.nc, k.a
    with ExitStack() as ctx:
        before = k.sb(ctx, "before", [P, P])
        iota8 = k.sb(ctx, "iota8", [P, NE])
        best = k.sb(ctx, "best", [P, NT, 8])
        bidx = k.sb(ctx, "bidx", [P, NT, 8], U32)
        idxf = k.sb(ctx, "idxf", [P, NT, 2])
        oh = k.sb(ctx, "oh", [P, 2, NT, NE])
        both = k.sb(ctx, "both", [P, NT, NE])
        seen = k.sb(ctx, "seen", [P, NT, NE])
        pick = k.sb(ctx, "pick", [P, 2, NT, NE])
        rank = k.sb(ctx, "rank", [P, NT, 2])
        fits = k.sb(ctx, "fits", [P, NT, 2])
        ed, es = k.sb(ctx, "ed", [P, NT]), k.sb(ctx, "es", [P, NT])
        slot = k.sb(ctx, "slot", [P, NT, 2])
        sidx = k.sb(ctx, "sidx", [P, 2, TS, 2], U32)
        XN = k.sb(ctx, "s_XN", [P, 2, TS, D])
        psR = k.ps(ctx, "o_psR", [P, NT, NE])
        weights, steps = k.sem(ctx, "o_weights"), k.sem(ctx, "o_steps")
        d_ready, d_exp = k.sem(ctx, "o_d_ready"), k.sem(ctx, "o_d_exp")
        m_ready, r_ready = k.sem(ctx, "o_m_ready"), k.sem(ctx, "o_r_ready")
        row_ready, free = k.sem(ctx, "o_row_ready"), k.sem(ctx, "o_row_free")
        sent = [k.sem(ctx, f"o_sent{s}") for s in range(2)]
        block = ctx.enter_context(nc.Block())

        @block.sync
        def _(sp):
            sp.dma_start(before[:, :], a["before"]).then_inc(weights, 16)
            sp.dma_start(iota8[:, :], a["iota8"]).then_inc(weights, 16)

        @block.gpsimd
        def _(pool):
            pool.sem_inc(free, 2)
            with pool.Fori(0, NB // 2) as i:
                for x in range(2):
                    pool.wait_ge(row_ready, (i * 2 + x) * (TS + 1) + TS + 1)
                    pass_gate(k, pool)
                    for u in range(TS):
                        for j in range(2):
                            pool.indirect_dma_start(
                                k.xt_dram[:, :], bass.IndirectOffsetOnAxis(ap=sidx[:, x, u, j:j + 1], axis=0),
                                XN[:, x, u, :], None, bounds_check=SLOTS - 1, oob_is_err=False,
                            ).then_inc(sent[x], 16)
                    if x == 1:
                        for y in range(2):
                            pool.wait_ge(sent[y], i * (2 * TS * 16) + 2 * TS * 16)
                            pool.sem_inc(free, 1)

        @block.tensor
        def _(pe):
            pe.wait_ge(weights, 32)
            pe.wait_ge(m_ready, 1)
            pe.matmul(psR[:, :, :].rearrange("p t e -> p (t e)"), before[:, :],
                      both[:, :, :].rearrange("p t e -> p (t e)"), start=True, stop=False)
            pe.matmul(psR[:, :, :].rearrange("p t e -> p (t e)"), k.ones[:, :],
                      seen[:, :, :].rearrange("p t e -> p (t e)"), start=False, stop=True).then_inc(r_ready, 1)

        @block.scalar
        def _(act):
            act.wait_ge(d_ready, 1)
            nc.scalar.activation(ed[:, :], ed[:, :], ACT.Exp).then_inc(d_exp, 1)

        @block.vector
        def _(dve):
            ch = Chain(dve, steps)
            dve.wait_ge(weights, 32)
            LG = k.LG[:, :, :, :].rearrange("p s t e -> p (s t) e")
            n = ch.mark(nc.vector.memset(seen[:, 0, :], 0.0))
            for t in range(NT):
                n = ch.mark(nc.vector.max(best[:, t, :], LG[:, t, :]))
            ch.after(n)
            for t in range(NT):
                n = ch.mark(nc.vector.max_index(bidx[:, t, :], best[:, t, :], LG[:, t, :]))
            nc.vector.tensor_tensor(ed[:, :], best[:, :, 1], best[:, :, 0], ALU.subtract).then_inc(d_ready, 1)
            ch.after(n)
            ch.step(nc.vector.tensor_copy(idxf[:, :, :], bidx[:, :, 0:2]))
            for j in range(2):
                n = ch.mark(nc.vector.tensor_tensor(oh[:, j, :, :], bc(iota8[:, :].unsqueeze(1), [P, NT, NE]),
                                                    bc(idxf[:, :, j:j + 1], [P, NT, NE]), ALU.is_equal))
            ch.after(n)
            ch.step(nc.vector.tensor_tensor(both[:, :, :], oh[:, 0, :, :], oh[:, 1, :, :], ALU.add))
            for t in range(NT - 1):
                ch.step(nc.vector.tensor_tensor(seen[:, t + 1, :], seen[:, t, :], both[:, t, :], ALU.add))
            dve.sem_inc(m_ready, 1)
            dve.wait_ge(d_exp, 1)
            ch.step(nc.vector.tensor_scalar(es[:, :], ed[:, :], 1.0, None, ALU.add))
            ch.step(nc.vector.reciprocal(es[:, :], es[:, :]))
            dve.wait_ge(r_ready, 1)
            for j in range(2):
                n = ch.mark(nc.vector.tensor_tensor(pick[:, j, :, :], oh[:, j, :, :], psR[:, :, :], ALU.mult))
            ch.after(n)
            for j in range(2):
                n = ch.mark(nc.vector.tensor_reduce(rank[:, :, j], pick[:, j, :, :], AX.X, ALU.add))
            ch.after(n)
            ch.step(nc.vector.tensor_scalar(fits[:, :, :], rank[:, :, :], float(CAP), None, ALU.is_lt))
            ch.step(nc.vector.scalar_tensor_tensor(slot[:, :, :], idxf[:, :, :], float(CAP), rank[:, :, :], ALU.mult, ALU.add))
            ch.step(nc.vector.scalar_tensor_tensor(slot[:, :, :], slot[:, :, :], -float(SLOTS), fits[:, :, :], ALU.add, ALU.mult))
            ch.step(nc.vector.tensor_scalar(slot[:, :, :], slot[:, :, :], float(SLOTS), None, ALU.add))
            ch.step(nc.vector.tensor_copy(k.slots[:, :, :], slot[:, :, :]))
            with dve.Fori(0, NB // 2) as i:
                for x in range(2):
                    dve.wait_ge(free, i * 2 + x + 1)
                    pass_gate(k, dve)
                    n = i * (2 * TS) + x * TS
                    nc.vector.tensor_copy(sidx[:, x, :, :], k.slots[:, bass.ds(n, TS), :]).then_inc(row_ready, 1)
                    for u in range(TS):
                        m = i * (2 * TS) + (x * TS + u)
                        nc.vector.tensor_scalar(XN[:, x, u, :], k.HS[:, bass.ds(m, 1), :].rearrange("p a c -> p (a c)"),
                                                k.mean[:, bass.ds(m, 1)], k.rstd[:, bass.ds(m, 1)],
                                                ALU.subtract, ALU.mult).then_inc(row_ready, 1)
            n = ch.mark(nc.vector.tensor_tensor(k.prob[:, :, 0], es[:, :], fits[:, :, 0], ALU.mult))
            ch.step(nc.vector.tensor_tensor(ed[:, :], es[:, :], ed[:, :], ALU.mult))
            ch.mark(nc.vector.tensor_tensor(k.prob[:, :, 1], ed[:, :], fits[:, :, 1], ALU.mult))


def experts(k):
    nc, a = k.nc, k.a
    CH = 2 * P
    NCH = CAP // CH
    with ExitStack() as ctx:
        w1 = k.sb(ctx, "w1", [P, 2, KC, FE])
        w2 = k.sb(ctx, "w2", [P, 2, FE // P, D])
        lnw, lnb = k.sb(ctx, "e_w", [P, KC]), k.sb(ctx, "e_b", [P, KC])
        XE = k.sb(ctx, "XE", [P, 4, 2, D])
        XT = k.sb(ctx, "e_XT", [P, 2, KC, CH])
        HT = k.sb(ctx, "e_HT", [P, 2, FE // P, CH])
        YE = k.sb(ctx, "YE", [P, 2, 2, D])
        psX = k.ps(ctx, "e_psX", [P, KC, CH])
        psH = [[k.ps(ctx, f"e_psH{s}{h}", [P, 2, CH]) for h in range(2)] for s in range(2)]
        psY = [k.ps(ctx, f"e_psY{s}", [P, 2, D]) for s in range(2)]
        consts = k.sem(ctx, "e_consts")
        w_loaded = [k.sem(ctx, f"e_w_loaded{s}") for s in range(2)]
        x_loaded = [k.sem(ctx, f"e_x_loaded{s}") for s in range(2)]
        y_stored = [k.sem(ctx, f"e_y_stored{s}") for s in range(2)]
        x_ready, x_evac = k.sem(ctx, "e_x_ready"), k.sem(ctx, "e_x_evac")
        h_ready, h_done = k.sem(ctx, "e_h_ready"), k.sem(ctx, "e_h_done")
        y_ready, y_evac = k.sem(ctx, "e_y_ready"), k.sem(ctx, "e_y_evac")
        block = ctx.enter_context(nc.Block())
        N = 2 * NCH
        assert N % 2 == 0

        @block.sync
        def _(sp):
            sp.dma_start(lnw[:, :], a["ln2w"]).then_inc(consts, 16)
            sp.dma_start(lnb[:, :], a["ln2b"]).then_inc(consts, 16)
            with sp.Fori(0, NE // 2) as i:
                for s in range(2):
                    sp.wait_ge(y_ready, i * N + (s + 1) * NCH)
                    sp.dma_start(w1[:, s, :, :], a["w1"][bass.ds(i * 2 + s, 1), :, :].rearrange("a (k p) n -> p (a k) n", p=P)).then_inc(w_loaded[s], 16)
                    sp.dma_start(w2[:, s, :, :], a["w2"][bass.ds(i * 2 + s, 1), :, :].rearrange("a (k p) n -> p (a k) n", p=P)).then_inc(w_loaded[s], 16)
                    for c in range(s * NCH, (s + 1) * NCH):
                        sp.wait_ge(x_ready, i * N + c + 1)
                        sp.dma_start(XE[:, c % 2, :, :], k.xt_dram[bass.ds((i * N + c) * CH, CH), :].rearrange(
                            "(j p) n -> p j n", p=P)).then_inc(x_loaded[c % 2], 16)

        @block.tensor
        def _(pe):
            pe.sem_inc(y_ready, N)
            pe.sem_inc(x_ready, 2)

            def turn(i, c):
                pe.wait_ge(x_loaded[c % 2], i * (16 * N // 2) + 16 * (c // 2 + 1))
                pe.wait_ge(x_evac, (i * N + c) * 2 + 2)
                for j in range(2):
                    for kc in range(KC):
                        mm = pe.transpose(psX[:, kc, j * P:(j + 1) * P], XE[:, c % 2, j, kc * P:(kc + 1) * P], k.ident[:, :])
                mm.then_inc(x_ready, 1)

            def hidden(i, c):
                s = c // NCH
                if c % NCH == 0:
                    pe.wait_ge(w_loaded[s], i * 32 + 32)
                pe.wait_ge(x_evac, (i * N + c) * 2 + 4)
                for half in range(2):
                    pe.wait_ge(h_done, (i * N + c) * 2 + half + 1)
                    for m in range(2):
                        for kc in range(KC):
                            f = (half * 2 + m) * P
                            mm = pe.matmul(psH[c % 2][half][:, m, :], w1[:, s, kc, f:f + P], XT[:, c % 2, kc, :],
                                           start=(m == 0 and kc == 0), stop=(m == 1 and kc == KC - 1), skip_group_check=True)
                    mm.then_inc(h_ready, 1)

            def rows(i, c):
                s = c // NCH
                pe.wait_ge(h_done, (i * N + c) * 2 + 2 + 4)
                pe.wait_ge(y_evac, i * N + c + 1)
                for j in range(2):
                    for m in range(FE // P):
                        mm = pe.matmul(psY[c % 2][:, j, :], HT[:, c % 2, m, j * P:(j + 1) * P], w2[:, s, m, :],
                                       start=(j == 0 and m == 0), stop=(j == 1 and m == FE // P - 1), skip_group_check=True)
                mm.then_inc(y_ready, 1)

            with pe.Fori(0, NE // 2) as i:
                turn(i, 0)
                for c in range(N):
                    if c + 1 < N:
                        turn(i, c + 1)
                    hidden(i, c)
                    if c >= 1:
                        rows(i, c - 1)
                rows(i, N - 1)

        @block.scalar
        def _(act):
            act.sem_inc(h_done, 4)
            act.sem_inc(y_stored[0], 16)
            act.sem_inc(y_stored[1], 16)

            def store(i, c):
                act.wait_ge(y_evac, i * N + c + 1 + 2)
                act.dma_start(k.y_dram[bass.ds((i * N + c) * CH, CH), :].rearrange("(j p) n -> p j n", p=P),
                              YE[:, c % 2, :, :]).then_inc(y_stored[c % 2], 16)

            with act.Fori(0, NE // 2) as i:
                for c in range(N):
                    act.wait_ge(y_ready, i * N + c + 1 + N - 2)
                    for half in range(2):
                        act.wait_ge(h_ready, (i * N + c) * 2 + half + 1)
                        nc.scalar.activation(HT[:, c % 2, 2 * half:2 * half + 2, :], psH[c % 2][half][:, :, :],
                                             ACT.Gelu_apprx_tanh).then_inc(h_done, 1)
                    if c >= 2:
                        store(i, c - 2)
                store(i, N - 2)
                store(i, N - 1)
            for s in range(2):
                act.wait_ge(y_stored[s], 16 + 16 * (NE // 2) * (N // 2))

        @block.vector
        def _(dve):
            dve.sem_inc(x_evac, 2)
            dve.sem_inc(y_evac, 2)
            dve.wait_ge(consts, 32)

            def evac_x(i, c):
                dve.wait_ge(x_ready, i * N + c + 1 + 2)
                for kc in range(KC):
                    nc.vector.tensor_scalar(XT[:, c % 2, kc, :], psX[:, kc, :], lnw[:, kc:kc + 1], lnb[:, kc:kc + 1],
                                            ALU.mult, ALU.add).then_inc(x_evac, 1)

            def evac_y(i, c):
                dve.wait_ge(y_ready, i * N + c + 1 + N)
                dve.wait_ge(y_stored[c % 2], i * (16 * N // 2) + 16 * (c // 2 + 1))
                nc.vector.tensor_copy(YE[:, c % 2, :, :], psY[c % 2][:, :, :]).then_inc(y_evac, 1)

            with dve.Fori(0, NE // 2) as i:
                evac_x(i, 0)
                for c in range(N):
                    if c >= 2:
                        evac_y(i, c - 2)
                    if c + 1 < N:
                        evac_x(i, c + 1)
                evac_y(i, N - 2)
                evac_y(i, N - 1)


def combine(k):
    nc = k.nc
    U = 4
    with ExitStack() as ctx:
        cidx = k.sb(ctx, "cidx", [P, U, 2], U32)
        YG = k.sb(ctx, "YG", [P, U, 2, D])
        steps, i_ready, used = k.sem(ctx, "c_steps"), k.sem(ctx, "c_i_ready"), k.sem(ctx, "c_used")
        got = [k.sem(ctx, f"c_got{u}") for u in range(U)]
        block = ctx.enter_context(nc.Block())

        @block.gpsimd
        def _(pool):
            with pool.Fori(0, NT // U) as i:
                for u in range(U):
                    pool.wait_ge(used, i * U + u + 1)
                    nc.gpsimd.tensor_copy(cidx[:, u, :], k.slots[:, bass.ds(i * U + u, 1), :].rearrange("p a j -> p (a j)")).then_inc(i_ready, 1)
                    pool.wait_ge(i_ready, i * U + u + 1)
                    pass_gate(k, pool)
                    for j in range(2):
                        pool.indirect_dma_start(YG[:, u, j, :], None, k.y_dram[:, :],
                                                bass.IndirectOffsetOnAxis(ap=cidx[:, u, j:j + 1], axis=0)).then_inc(got[u], 16)

        @block.vector
        def _(dve):
            dve.sem_inc(used, U)
            with dve.Fori(0, NT // U) as i:
                ch = Chain(dve, steps, i * 3 * U)
                for u in range(U):
                    x = k.X[:, bass.ds(i * U + u, 1), :].rearrange("p a c -> p (a c)")
                    h = k.HS[:, bass.ds(i * U + u, 1), :].rearrange("p a c -> p (a c)")
                    pr = k.prob[:, bass.ds(i * U + u, 1), :].rearrange("p a j -> p (a j)")
                    ch.step(nc.vector.tensor_tensor(x, x, h, ALU.add))
                    dve.wait_ge(got[u], i * 32 + 32)
                    for j in range(2):
                        ch.step(nc.vector.scalar_tensor_tensor(x, YG[:, u, j, :], pr[:, j:j + 1], x, ALU.mult, ALU.add))
                    pass_gate(k, dve)
                    nc.vector.bn_stats(k.BST[:, bass.ds(i * U + u, 1), :].rearrange("p a c -> p (a c)"), x).then_inc(used, 1)


def retention(k):
    nc, a = k.nc, k.a
    with ExitStack() as ctx:
        wqkv = k.sb(ctx, "n_wqkv", [P, KC, 3 * D])
        wo = k.sb(ctx, "n_wo", [P, KC, D])
        gam, bet = k.sb(ctx, "n_gam", [P, KC]), k.sb(ctx, "n_bet", [P, KC])
        rotC, rotS = k.sb(ctx, "rotC", [P, TS, 2 * D]), k.sb(ctx, "rotS", [P, TS, 2 * D])
        causal = k.sb(ctx, "causal", [P, P])
        carry = k.sb(ctx, "carry", [P, KC, P])
        XN = k.sb(ctx, "n_XN", [P, 2, D])
        XT = k.sb(ctx, "n_XT", [P, KC, P])
        m1, m2 = k.sb(ctx, "rot1", [P, 2 * D]), k.sb(ctx, "rot2", [P, 2 * D])
        Qr = k.sb(ctx, "Qr", [P, D])
        Kr = k.sb(ctx, "Kr", [P, 2, D])
        Kpar = [k.sb(ctx, f"Kpar{par}", [P, KC, P]) for par in range(2)]
        V = k.sb(ctx, "n_V", [P, 2, D])
        Vpar = [k.sb(ctx, f"Vpar{par}", [P, 2, D]) for par in range(2)]
        KT = k.sb(ctx, "n_KT", [P, 2, KC, P])
        QT = k.sb(ctx, "n_QT", [P, KC, P])
        ST = k.sb(ctx, "n_ST", [P, 4, KC, 2, P])
        state = k.sb(ctx, "state", [P, KC, P])
        snew = k.sb(ctx, "snew", [P, KC, P])
        wmean = k.sb(ctx, "wmean", [P, KC, H1])
        group = k.sb(ctx, "group", [P, P])
        eps = k.sb(ctx, "n_eps", [P, 1])
        R = k.sb(ctx, "n_R", [P, 2, KC, P])
        sq = k.sb(ctx, "n_sq", [P, KC, P])
        root = k.sb(ctx, "n_root", [P, KC, P])
        inv = k.sb(ctx, "n_inv", [P, KC, P])
        RN = k.sb(ctx, "n_RN", [P, KC, P])
        RT = k.sb(ctx, "n_RT", [P, KC, P])
        psT = k.ps(ctx, "n_psT", [P, 2, KC, P])
        psQK = k.ps(ctx, "n_psQK", [P, 2 * D])
        psV = k.ps(ctx, "n_psV", [P, D])
        psK = k.ps(ctx, "n_psK", [P, 2, KC, P])
        psX = k.ps(ctx, "n_psX", [P, KC, P])
        psS = [k.ps(ctx, f"n_psS{s}", [P, KC, 2, P]) for s in range(2)]
        psR = k.ps(ctx, "n_psR", [P, KC, P])
        weights, zeroed = k.sem(ctx, "n_weights"), k.sem(ctx, "n_zeroed")
        xn_ready, xt_ready, xt_evac = k.sem(ctx, "n_xn_ready"), k.sem(ctx, "n_xt_ready"), k.sem(ctx, "n_xt_evac")
        sq_ready, m_ready, m_root = k.sem(ctx, "n_sq_ready"), k.sem(ctx, "n_m_ready"), k.sem(ctx, "n_m_root")
        rn_ready, rt_ready = k.sem(ctx, "n_rn_ready"), k.sem(ctx, "n_rt_ready")
        qk_ready, v_ready, v_evac = k.sem(ctx, "n_qk_ready"), k.sem(ctx, "n_v_ready"), k.sem(ctx, "n_v_evac")
        rot_done, rot_ready = k.sem(ctx, "n_rot_done"), k.sem(ctx, "n_rot_ready")
        x_ready, x_evac = k.sem(ctx, "n_x_ready"), k.sem(ctx, "n_x_evac")
        s_ready, s_masked = k.sem(ctx, "n_s_ready"), k.sem(ctx, "n_s_masked")
        r_ready, r_read = k.sem(ctx, "n_r_ready"), k.sem(ctx, "n_r_read")
        st_ready, st_done = k.sem(ctx, "n_st_ready"), k.sem(ctx, "n_st_done")
        z_ready, z_added = k.sem(ctx, "n_z_ready"), k.sem(ctx, "n_z_added")
        dstep, centred = k.sem(ctx, "n_dstep"), k.sem(ctx, "n_centred")
        block = ctx.enter_context(nc.Block())

        @block.sync
        def _(sp):
            sp.dma_start(wqkv[:, :, :], a["wqkv1"].rearrange("(k p) n -> p k n", p=P)).then_inc(weights, 16)
            sp.dma_start(rotC[:, :, :], a["rotC"]).then_inc(weights, 16)
            sp.dma_start(rotS[:, :, :], a["rotS"]).then_inc(weights, 16)
            sp.dma_start(causal[:, :], a["causal"]).then_inc(weights, 16)
            sp.dma_start(carry[:, :, :], a["carry"]).then_inc(weights, 16)
            sp.dma_start(wo[:, :, :], a["wo1"].rearrange("(k p) n -> p k n", p=P)).then_inc(weights, 16)
            sp.dma_start(gam[:, :], a["gamma"]).then_inc(weights, 16)
            sp.dma_start(bet[:, :], a["beta"]).then_inc(weights, 16)
            sp.dma_start(group[:, :], a["group"]).then_inc(weights, 16)

        def stream(eng, step):
            for s in range(TS):
                step(0, s, True, s >= 1, s >= 2)
            with eng.Fori(1, NB) as i:
                for s in range(TS):
                    step(i, s, True, True, True)
            step(NB, 0, False, True, True)
            step(NB, 1, False, False, True)

        def states(i, s):
            return i * (TS - 1) + max(s - 1, 0)

        @block.tensor
        def _(pe):
            pe.sem_inc(x_ready, 1)
            pe.wait_ge(weights, 16 * 9)
            pe.wait_ge(centred, 1)

            def turn_x(g, s):
                pe.wait_ge(xn_ready, g + 1)
                pe.wait_ge(xt_evac, g + 1)
                pe.wait_ge(m_root, g + 1)
                pe.wait_ge(st_done, g + 1)
                for c in range(KC):
                    mm = pe.transpose(psT[:, 0, c, :], XN[:, s % 2, c * P:(c + 1) * P], k.ident[:, :])
                mm.then_inc(xt_ready, 1)

            def project(g, s):
                pe.wait_ge(xt_evac, g + 2)
                pe.wait_ge(rot_done, g + 1)
                for c in range(KC):
                    mm = pe.matmul(psQK[:, :], XT[:, c, :], wqkv[:, c, 0:2 * D], start=(c == 0), stop=(c == KC - 1))
                mm.then_inc(qk_ready, 1)
                pe.wait_ge(v_evac, g + 1)
                pe.wait_ge(z_added, g + 1)
                for c in range(KC):
                    mm = pe.matmul(psV[:, :], XT[:, c, :], wqkv[:, c, 2 * D:], start=(c == 0), stop=(c == KC - 1))
                mm.then_inc(v_ready, 1)

            def turn_qk(g, s):
                pe.wait_ge(rot_ready, g + 2)
                pe.wait_ge(x_evac, g * 2 + 2)
                for par in range(2):
                    for c in range(KC):
                        pe.transpose(psK[:, par, c, :], Kpar[par][:, c, :], k.ident[:, :])
                for c in range(KC):
                    mm = pe.transpose(psX[:, c, :], Qr[:, c * P:(c + 1) * P], k.ident[:, :])
                mm.then_inc(x_ready, 1)

            def scores(g, half):
                if half == 0:
                    pe.wait_ge(x_evac, g * 2 + 4)
                pe.wait_ge(s_masked, g * 4 + 2 * half + 2)
                for c in range(KC):
                    for par in range(2):
                        for b in range(2):
                            r = 32 * (2 * half + b)
                            mm = pe.matmul(psS[b][:, c, par, :], KT[r:r + 32, par, c, :], QT[r:r + 32, c, :],
                                           start=(c == 0 and par == 0), stop=(c == 1 and par == 1), skip_group_check=True)
                mm.then_inc(s_ready, 1)

            def from_state(g):
                pe.wait_ge(r_read, g + 1)
                pe.wait_ge(st_done, g + 2)
                for c in range(KC):
                    pe.matmul(psR[:, c, :], state[:, c, :], QT[:, c, :], start=(c == 0), stop=False,
                              skip_group_check=True)

            def from_chunk(g, s, half):
                u = (s - 1) % TS
                pe.wait_ge(s_masked, g * 4 + 2 * half + 2 + 2)
                for r in (2 * half, 2 * half + 1):
                    for c in range(KC):
                        for par in range(2):
                            h = (c * 4 + r) * 2
                            mm = pe.matmul(psR[32 * r:32 * r + 32, c, :], Vpar[par][:, u % 2, h * DH:(h + 2) * DH],
                                           ST[:, r, c, par, :], start=False, stop=(r == 3 and c == 1 and par == 1),
                                           skip_group_check=True)
                if half == 1:
                    mm.then_inc(r_ready, 1)

            def to_state(s):
                u = (s - 1) % TS
                for c in range(KC):
                    mm = pe.matmul(psT[:, 1, c, :], Kr[:, u % 2, c * P:(c + 1) * P], V[:, u % 2, c * P:(c + 1) * P],
                                   start=(c == 0), stop=(c == KC - 1), skip_group_check=True)
                mm.then_inc(st_ready, 1)

            def variances(g):
                pe.wait_ge(sq_ready, g + 1)
                pe.wait_ge(xt_evac, min(g + 3, NT + 1) if isinstance(g, int) else g + 3)
                pe.wait_ge(st_done, min(g + 3, NT + 2) if isinstance(g, int) else g + 3)
                pe.matmul(psT[:, 0, :, :], group[:, :], sq[:, :, :], start=True, stop=True).then_inc(m_ready, 1)

            def out(g, entering):
                pe.wait_ge(rt_ready, g + 1 + 1)
                pe.wait_ge(v_evac, g + 4 if entering else NT + 1)
                pe.wait_ge(z_added, g + 3)
                for c in range(KC):
                    mm = pe.matmul(psV[:, :], RT[:, c, :], wo[:, c, :], start=(c == 0), stop=(c == KC - 1))
                mm.then_inc(z_ready, 1)

            def step(i, s, entering, attending, leaving):
                g = i * TS + s
                if attending:
                    scores(g - 1, 0)
                if leaving:
                    variances(g - 2)
                if entering:
                    turn_x(g, s)
                if attending:
                    from_state(g - 1)
                if entering:
                    project(g, s)
                if attending:
                    scores(g - 1, 1)
                    from_chunk(g - 1, s, 0)
                    from_chunk(g - 1, s, 1)
                if entering:
                    turn_qk(g, s)
                if leaving:
                    out(g - 2, entering)
                if attending and s != 0:
                    to_state(s)

            stream(pe, step)

        @block.scalar
        def _(act):
            act.sem_inc(xt_evac, 1)
            act.sem_inc(m_root, 2)
            act.sem_inc(r_read, 1)
            act.sem_inc(rt_ready, 1)
            act.sem_inc(v_evac, 1)
            act.sem_inc(x_evac, 2)
            act.wait_ge(weights, 16 * 9)
            act.wait_ge(zeroed, 5)

            def x_turned(g):
                act.wait_ge(xt_ready, g + 1)
                nc.scalar.copy(XT[:, :, :], psT[:, 0, :, :]).then_inc(xt_evac, 1)

            def values(g, s):
                act.wait_ge(v_ready, g + 1)
                nc.scalar.copy(V[:, s % 2, :], psV[:, :])
                for par in range(2):
                    def side(x):
                        return x.rearrange("p (g h d) -> p g h d", h=2, d=DH)[:, :, par, :]
                    ins = nc.scalar.copy(side(Vpar[par][:, s % 2, :]), side(psV[:, :]))
                ins.then_inc(v_evac, 1)

            def result_read(g, s):
                act.wait_ge(r_ready, g + 1)
                act.wait_ge(rn_ready, g + 1)
                nc.scalar.copy(R[:, (s - 1) % 2, :, :], psR[:, :, :]).then_inc(r_read, 1)

            def root_of(g):
                act.wait_ge(m_ready, g + 1)
                act.wait_ge(rn_ready, g + 2)
                nc.scalar.activation(root[:, :, :], psT[:, 0, :, :], ACT.Sqrt, bias=eps[:, 0:1]).then_inc(m_root, 1)

            def scaled(g):
                act.wait_ge(rn_ready, g + 1 + 2)
                for c in range(KC):
                    ins = nc.scalar.activation(RT[:, c, :], RN[:, c, :], ACT.Identity, bias=bet[:, c:c + 1],
                                               scale=gam[:, c:c + 1])
                ins.then_inc(rt_ready, 1)

            def qk_turned(g):
                act.wait_ge(x_ready, g + 2)
                nc.scalar.copy(KT[:, :, :, :], psK[:, :, :, :]).then_inc(x_evac, 1)
                nc.scalar.copy(QT[:, :, :], psX[:, :, :]).then_inc(x_evac, 1)

            def step(i, s, entering, attending, leaving):
                g = i * TS + s
                if leaving:
                    root_of(g - 2)
                if entering:
                    x_turned(g)
                    values(g, s)
                if leaving:
                    scaled(g - 2)
                if attending:
                    result_read(g - 1, s)
                if entering:
                    qk_turned(g)

            stream(act, step)

        @block.gpsimd
        def _(pool):
            pool.sem_inc(rot_ready, 1)
            for par in range(2):
                nc.gpsimd.memset(Kpar[par][:, :, :], 0.0).then_inc(zeroed, 1)
                nc.gpsimd.memset(Vpar[par][:, :, :], 0.0).then_inc(zeroed, 1)
            nc.gpsimd.memset(eps[:, :], EPS).then_inc(zeroed, 1)
            pool.wait_ge(zeroed, 5)

            def squared(g, s):
                pool.wait_ge(r_read, g + 2)
                pool.wait_ge(m_ready, g) if not isinstance(g, int) or g else None
                x = R[:, (s - 1) % 2, :, :]
                nc.gpsimd.tensor_tensor(sq[:, :, :], x, x, ALU.mult).then_inc(sq_ready, 1)

            def rotated(g, s):
                pool.wait_ge(rot_done, g + 2)
                pool.wait_ge(x_ready, g + 1)
                nc.gpsimd.tensor_tensor(Qr[:, :], m1[:, 0:D], m2[:, 0:D], ALU.add)
                nc.gpsimd.tensor_tensor(Kr[:, s % 2, :], m1[:, D:], m2[:, D:], ALU.add)
                for par in range(2):
                    def side(x):
                        return x.rearrange("p (g h d) -> p g h d", h=2, d=DH)[:, :, par, :]
                    dst = Kpar[par][:, :, :].rearrange("p c (g h d) -> p (c g) h d", h=2, d=DH)[:, :, par, :]
                    ins = nc.gpsimd.tensor_tensor(dst, side(m1[:, D:]), side(m2[:, D:]), ALU.add)
                ins.then_inc(rot_ready, 1)

            def step(i, s, entering, attending, leaving):
                g = i * TS + s
                if entering:
                    rotated(g, s)
                if attending:
                    squared(g - 1, s)

            stream(pool, step)

        @block.vector
        def _(dve):
            dve.sem_inc(rot_done, 1)
            dve.sem_inc(s_masked, 2)
            dve.sem_inc(st_done, 1)
            nc.vector.memset(state[:, :, :], 0.0).then_inc(st_done, 1)
            dve.sem_inc(rn_ready, 2)
            dve.sem_inc(z_added, 3)
            dve.wait_ge(weights, 16 * 9)

            wv = wqkv[:, :, 2 * D:].rearrange("p c (h d) -> p c h d", d=DH)
            first = Chain(dve, dstep)
            for c in range(KC):
                n = first.mark(nc.vector.tensor_reduce(wmean[:, c, :], wv[:, c, :, :], AX.X, ALU.add))
            first.after(n)
            first.step(nc.vector.tensor_scalar(wmean[:, :, :], wmean[:, :, :], 1.0 / DH, None, ALU.mult))
            for c in range(KC):
                n = first.mark(nc.vector.tensor_tensor(wv[:, c, :, :], wv[:, c, :, :],
                                                       bc(wmean[:, c, :].unsqueeze(2), [P, H1, DH]), ALU.subtract))
            first.after(n)
            dve.sem_inc(centred, 1)
            chains = []
            STEPS = TS * 2 + TS - 2

            def norm(g, s):
                normalise(k, XN[:, s % 2, :], g).then_inc(xn_ready, 1)

            def rotate(g, s):
                dve.wait_ge(qk_ready, g + 1)
                dve.wait_ge(rot_ready, g + 1)
                nc.vector.tensor_tensor(m1[:, :], psQK[:, :], rotC[:, s, :], ALU.mult)
                for x in range(2):
                    def lane(y, z):
                        return y.rearrange("p (n two) -> p n two", two=2)[:, :, z]
                    ins = nc.vector.tensor_tensor(lane(m2[:, :], x), lane(psQK[:, :], 1 - x), lane(rotS[:, s, :], x), ALU.mult)
                ins.then_inc(rot_done, 1)

            def mask(g, half):
                dve.wait_ge(s_ready, g * 2 + half + 1)
                for r in (2 * half, 2 * half + 1):
                    nc.vector.tensor_tensor(ST[:, r, :, :, :].rearrange("p c a t -> p (c a) t"),
                                            psS[r % 2][:, :, :, :].rearrange("p c a t -> p (c a) t"),
                                            bc(causal[:, :].unsqueeze(1), [P, 4, P]), ALU.mult).then_inc(s_masked, 1)

            def carry_on(g, s, old, ch):
                if s == 0:
                    dve.wait_ge(r_ready, g + 1)
                    nc.vector.memset(state[:, :, :], 0.0).then_inc(st_done, 1)
                    return
                dve.wait_ge(st_ready, old + 1)
                new = psT[:, 1, :, :]
                if (s - 1) % TS > 0:
                    ch.step(nc.vector.tensor_tensor(snew[:, :, :], psT[:, 1, :, :], state[:, :, :], ALU.add))
                    new = snew[:, :, :]
                nc.vector.tensor_tensor(state[:, :, :], new, carry[:, :, :], ALU.mult).then_inc(st_done, 1)

            def result(g, s, ch):
                dve.wait_ge(m_root, g + 1 + 2)
                ch.step(nc.vector.reciprocal(inv[:, :, :], root[:, :, :]))
                dve.wait_ge(rt_ready, g + 1)
                nc.vector.tensor_tensor(RN[:, :, :], R[:, (s - 2) % 2, :, :], inv[:, :, :], ALU.mult).then_inc(rn_ready, 1)

            def add(g, ch):
                dve.wait_ge(z_ready, g + 1)
                x = k.X[:, bass.ds(g, 1), :].rearrange("p a c -> p (a c)")
                bst = k.BST[:, bass.ds(g, 1), :].rearrange("p a c -> p (a c)")
                ch.step(nc.vector.tensor_tensor(x, x, psV[:, :], ALU.add))
                pass_gate(k, dve)
                nc.vector.bn_stats(bst, x).then_inc(z_added, 1)

            def step(i, s, entering, attending, leaving):
                g = i * TS + s
                if s == 0:
                    done = sum(c.n for c in chains[:1])
                    chains.append(Chain(dve, dstep, (i - 1) * STEPS + done + first.n if chains else first.n))
                ch = chains[-1]
                if entering:
                    norm(g, s)
                if attending:
                    mask(g - 1, 0)
                if leaving:
                    result(g - 2, s, ch)
                if entering:
                    rotate(g, s)
                if attending:
                    mask(g - 1, 1)
                if leaving:
                    add(g - 2, ch)
                if attending:
                    carry_on(g - 1, s, states(i, s), ch)
                if s == TS - 1 and len(chains) == 2:
                    assert ch.n == STEPS

            stream(dve, step)


def swiglu(k):
    nc, a = k.nc, k.a
    M = FF // P
    with ExitStack() as ctx:
        wgu = k.sb(ctx, "wgu", [P, KC, 2 * FF])
        wd = k.sb(ctx, "wd", [P, M, D])
        XN = k.sb(ctx, "f_XN", [P, TS, D])
        XT = k.sb(ctx, "f_XT", [P, KC, T])
        SG = k.sb(ctx, "f_SG", [P, 2, T])
        HT = k.sb(ctx, "f_HT", [P, M, T])
        psT = [k.ps(ctx, f"f_psT{c}", [P, T]) for c in range(KC)]
        psG = [k.ps(ctx, f"f_psG{s}", [P, T]) for s in range(2)]
        psU = [k.ps(ctx, f"f_psU{s}", [P, T]) for s in range(2)]
        psY = [k.ps(ctx, f"f_psY{s}", [P, D]) for s in range(2)]
        casts = k.sem(ctx, "f_casts")
        xn_ready, t_ready, t_evac = k.sem(ctx, "f_xn_ready"), k.sem(ctx, "f_t_ready"), k.sem(ctx, "f_t_evac")
        g_ready, g_done, u_done = k.sem(ctx, "f_g_ready"), k.sem(ctx, "f_g_done"), k.sem(ctx, "f_u_done")
        y_ready, y_added = k.sem(ctx, "f_y_ready"), k.sem(ctx, "f_y_added")
        with ExitStack() as c2:
            raw = k.sb(c2, "w_raw", [P, KC * 2 * FF + M * D], I32)
            weights = k.sem(ctx, "f_weights")
            n1 = KC * 2 * FF
            with nc.Block() as load:
                @load.sync
                def _(sp):
                    sp.dma_start(raw[:, 0:n1].rearrange("p (k n) -> p k n", k=KC),
                                 a["wgu"].rearrange("(k p) n -> p k n", p=P)).then_inc(weights, 16)
                    sp.dma_start(raw[:, n1:].rearrange("p (m n) -> p m n", m=M),
                                 a["wd"].rearrange("(m p) n -> p m n", p=P)).then_inc(weights, 16)

                @load.vector
                def _(dve):
                    dve.wait_ge(weights, 32)
                    nc.vector.tensor_copy(wgu[:, :, :].rearrange("p k n -> p (k n)"), raw[:, 0:n1]).then_inc(casts, 1)

                @load.gpsimd
                def _(pool):
                    pool.wait_ge(weights, 32)
                    nc.gpsimd.tensor_copy(wd[:, :, :].rearrange("p m n -> p (m n)"), raw[:, n1:]).then_inc(casts, 1)
        block = ctx.enter_context(nc.Block())

        @block.tensor
        def _(pe):
            pe.sem_inc(t_ready, 1)
            pe.sem_inc(y_ready, 4)
            pe.wait_ge(casts, 2)

            def turn(i):
                pe.wait_ge(t_evac, i * 2 + 2)
                for u in range(TS):
                    pe.wait_ge(xn_ready, i * TS + u + 1)
                    for c in range(KC):
                        mm = pe.transpose(psT[c][:, u * P:(u + 1) * P], XN[:, u, c * P:(c + 1) * P], k.ident[:, :])
                mm.then_inc(t_ready, 1)

            with pe.Fori(0, NB) as i:
                turn(i)
                pe.wait_ge(t_evac, i * 2 + 4)
                for m in range(M):
                    pe.wait_ge(g_done, i * M + m + 1)
                    for c in range(KC):
                        mm = pe.matmul(psG[m % 2][:, :], wgu[:, c, m * P:(m + 1) * P], XT[:, c, :], start=(c == 0), stop=(c == KC - 1))
                    mm.then_inc(g_ready, 1)
                    pe.wait_ge(u_done, i * M + m + 1)
                    for c in range(KC):
                        mm = pe.matmul(psU[m % 2][:, :], wgu[:, c, FF + m * P:FF + (m + 1) * P], XT[:, c, :], start=(c == 0), stop=(c == KC - 1))
                    mm.then_inc(g_ready, 1)
                pe.wait_ge(u_done, i * M + M + 2)
                for u in range(TS):
                    pe.wait_ge(y_added, i * TS + u + 1)
                    for m in range(M):
                        mm = pe.matmul(psY[u % 2][:, :], HT[:, m, u * P:(u + 1) * P], wd[:, m, :], start=(m == 0), stop=(m == M - 1))
                    mm.then_inc(y_ready, 1)

        @block.scalar
        def _(act):
            act.sem_inc(t_evac, 2)
            act.sem_inc(g_done, 2)
            with act.Fori(0, NB) as i:
                act.wait_ge(t_ready, i + 2)
                for c in range(KC):
                    nc.scalar.copy(XT[:, c, :], psT[c][:, :]).then_inc(t_evac, 1)
                for m in range(M):
                    act.wait_ge(g_ready, (i * M + m) * 2 + 1)
                    act.wait_ge(u_done, i * M + m + 1)
                    nc.scalar.activation(SG[:, m % 2, :], psG[m % 2][:, :], ACT.Silu, scale=QSCALE).then_inc(g_done, 1)

        @block.sync
        def _(sp):
            with sp.Fori(0, NB) as i:
                sp.wait_ge(y_added, i * TS + TS + 2)
                sp.dma_start(k.out[bass.ds(i * T, T), :].rearrange("(j p) c -> p j c", p=P),
                             k.X[:, bass.ds(i * TS, TS), :]).then_inc(k.stored, 16)
            sp.wait_ge(k.stored, 16 * NB)

        @block.vector
        def _(dve):
            dve.sem_inc(u_done, 2)
            dve.sem_inc(y_added, 2)
            with dve.Fori(0, NB) as i:
                dve.wait_ge(t_ready, i + 1)
                for u in range(TS):
                    normalise(k, XN[:, u, :], i * TS + u).then_inc(xn_ready, 1)
                for m in range(M):
                    dve.wait_ge(g_ready, (i * M + m) * 2 + 2)
                    dve.wait_ge(g_done, i * M + m + 1 + 2)
                    dve.wait_ge(y_ready, i * TS + TS)
                    nc.vector.scalar_tensor_tensor(HT[:, m, :], psU[m % 2][:, :], QSCALE, SG[:, m % 2, :],
                                                   ALU.mult, ALU.mult).then_inc(u_done, 1)
                for u in range(TS):
                    dve.wait_ge(y_ready, i * TS + u + 1 + 4)
                    x = k.X[:, bass.ds(i * TS + u, 1), :].rearrange("p a c -> p (a c)")
                    nc.vector.scalar_tensor_tensor(x, psY[u % 2][:, :], QSCALE, x, ALU.mult, ALU.add).then_inc(y_added, 1)


def lay_out(x):
    f = np.ascontiguousarray
    c = {}
    c["x"] = f(x["L0_attn_X"]).reshape(NB * T, D)
    c["wg"] = f(x["L0_attn_w_G"].reshape(H0 * E0, D).T)
    c["bg"] = f(x["L0_attn_b_G"].reshape(1, H0 * E0))
    c["wkv"] = f(np.concatenate([x["L0_attn_w_K"], x["L0_attn_w_V"]], axis=1).reshape(H0 * P, D).T)
    c["wq"] = f(x["L0_attn_w_Q"].reshape(H0 * DK, D).T)
    c["wo"] = f(x["L0_attn_w_O"].reshape(2, 4, DK, D).transpose(1, 0, 2, 3)).reshape(H0 * DK, D)
    c["ikv"] = f(np.concatenate([x["L0_attn_init_K_rec"], x["L0_attn_init_V_rec"]], axis=2).transpose(2, 0, 1))
    c["ident"] = np.eye(P, dtype=np.float32)
    q, s = np.arange(32)[:, None], np.arange(64)[None, :]
    seen = (s > q) & (s <= q + L0)
    c["mask"] = f(np.repeat(np.where(seen, 0.0, NEG).astype(np.float32), E0, axis=1))
    c["sel"] = f(np.tile(np.eye(32, dtype=np.float32), (1, 4)))
    col = lambda v: f(v.reshape(KC, P).T)
    c["qkv1"] = f(x["L0_ffn_qkv_weight"].T)
    c["proj"] = f(x["L0_ffn_proj_weight"].T)
    c["router"] = f(x["L0_ffn_router_weight"])
    c["ln1w"], c["ln1b"] = col(x["L0_ffn_ln1_weight"]), col(x["L0_ffn_ln1_bias"])
    c["ln2w"], c["ln2b"] = col(x["L0_ffn_ln2_weight"]), col(x["L0_ffn_ln2_bias"])
    c["w1"], c["w2"] = f(x["L0_ffn_moe_w1"]), f(x["L0_ffn_moe_w2"])
    c["before"] = np.triu(np.ones((P, P), np.float32), 1)
    c["iota8"] = f(np.tile(np.arange(NE, dtype=np.float32), (P, 1)))
    flat = lambda w: w.reshape(D, D)
    c["wqkv1"] = f(np.concatenate([flat(x["L1_attn_WQ"]), flat(x["L1_attn_WK"]), flat(x["L1_attn_WV"])]).T)
    c["wo1"] = f(x["L1_attn_WO"])
    c["gamma"], c["beta"] = col(x["L1_attn_gamma"]), col(x["L1_attn_beta"])
    c["rotC"], c["rotS"], c["carry"] = decay_tables()
    c["group"] = np.kron(np.eye(P // DH), np.full((DH, DH), 1.0 / DH)).astype(np.float32)
    c["causal"] = np.triu(np.ones((P, P), np.float32))
    c["wgu"] = f(np.concatenate([x["L1_ffn_w_gate"], x["L1_ffn_w_up"]]).T)
    c["wd"] = f(x["L1_ffn_w_down"].T)
    return c


def decay_tables():
    freq = (10.0 ** (-4.0 * (np.arange(0, DH, 2, dtype=np.float32) / np.float32(DH)))).astype(np.float32)
    angle = (np.arange(T, dtype=np.float32)[:, None] * freq[None, :]).astype(np.float64)
    gamma = 1.0 - 2.0 ** (-5.0 - np.arange(H1, dtype=np.float64))
    i = np.arange(P, dtype=np.float64)
    both = np.stack([gamma[None, :] ** i[:, None], gamma[None, :] ** -i[:, None]], axis=1)
    def spread(t):
        t = t.reshape(TS, P, 1, 1, DH).transpose(1, 0, 2, 3, 4) * both[:, None, :, :, None]
        return np.ascontiguousarray(t.reshape(P, TS, 2 * D).astype(np.float32))
    cos = np.repeat(np.cos(angle), 2, axis=1)
    sin = np.stack([-np.sin(angle), np.sin(angle)], axis=2).reshape(T, DH)
    carry = np.zeros((P, KC, P))
    for h in range(H1):
        r = slice(h % 8 * DH, h % 8 * DH + DH)
        carry[r, h // 8, r] = gamma[h] ** P
    return spread(cos), spread(sin), carry.astype(np.float32)


UPTO = 4
_SHAPE = (NB, T, D)


def kernel(**inputs):
    import numpy as _np
    import concourse.bacc as _bacc
    from concourse import mybir as _mybir
    from concourse.bass_utils import run_bass_kernel_spmd as _run

    arrays = lay_out(inputs)
    nc = _bacc.Bacc("TRN2", target_bir_lowering=False, num_devices=1)
    args = {}
    for name, v in arrays.items():
        args[name] = nc.dram_tensor("in_" + name, v.shape, _mybir.dt.from_np(v.dtype), kind="ExternalInput").ap()
    out = nc.dram_tensor("out_x", (NB * T, D), F32, kind="ExternalOutput").ap()
    build(nc, args, out, UPTO)
    r = _run(nc, [{"in_" + n: v for n, v in arrays.items()}], core_ids=[0])
    return r.results[0]["out_x"].reshape(_SHAPE)
```

```python
from contextlib import ExitStack

import numpy as np

import concourse.bass as bass
from concourse import mybir

F32 = mybir.dt.float32
BF16 = mybir.dt.bfloat16
I32 = mybir.dt.int32
U32 = mybir.dt.uint32
ALU = mybir.AluOpType
ACT = mybir.ActivationFunctionType
AX = mybir.AxisListType

P = 128
NB, T, D = 8, 512, 256
NT = NB * T // P
TS = T // P
KC = D // P
EPS = 1e-5
H0, E0, L0, DK = 8, 4, 32, 64
WIN = L0 + T
NH, NKV, HD = 16, 4, 16
QG = NH // NKV
QKVW = NKV * (QG + 2) * HD
NE, FE = 8, 512
CAP = 1280
SLOTS = NE * CAP
H1, DH = 16, 16
FF = 768
QSCALE = 1.0 / 127.0
NEG = -1e30


def bc(ap, shape):
    return ap.broadcast_to(shape)


class Chain:

    def __init__(self, eng, sem, base=0):
        self.eng, self.sem, self.base, self.n = eng, sem, base, 0

    def step(self, ins):
        self.n += 1
        ins.then_inc(self.sem, 1)
        self.eng.wait_ge(self.sem, self.base + self.n)

    def mark(self, ins):
        self.n += 1
        ins.then_inc(self.sem, 1)
        return self.n

    def after(self, n):
        self.eng.wait_ge(self.sem, self.base + n)


def pass_gate(k, eng):
    eng.sem_inc(k.gates_passed, 1)


class Kernel:
    def __init__(self, nc, a, out):
        self.nc, self.a, self.out = nc, a, out
        self.n = 0

    def sb(self, ctx, name, shape, dt=F32):
        return ctx.enter_context(self.nc.sbuf_tensor(name, shape, dt))

    def ps(self, ctx, name, shape, dt=F32):
        return ctx.enter_context(self.nc.psum_tensor(name, shape, dt))

    def sem(self, ctx, name):
        return ctx.enter_context(self.nc.semaphore(name))


def build(nc, a, out):
    k = Kernel(nc, a, out)
    with ExitStack() as ctx:
        k.X = k.sb(ctx, "X", [P, NT, D])
        k.BST = k.sb(ctx, "BST", [P, NT, 6])
        k.mean = k.sb(ctx, "mean", [P, NT])
        k.rstd = k.sb(ctx, "rstd", [P, NT])
        k.ident = k.sb(ctx, "ident", [P, P])
        k.ones = k.sb(ctx, "ones", [P, P])
        k.mhalf = k.sb(ctx, "mhalf", [P, NT])
        k.stored = k.sem(ctx, "out_stored")
        k.ln_steps, k.ln_var, k.ln_root = k.sem(ctx, "ln_steps"), k.sem(ctx, "ln_var"), k.sem(ctx, "ln_root")
        k.gates_passed = k.sem(ctx, "gates_passed")
        k.xt_dram = nc.dram_tensor("expert_in", (SLOTS + P, D), F32, kind="Internal").ap()
        k.xT_dram = nc.dram_tensor("x_turned", (P, KC, NB * T), F32, kind="Internal").ap()
        k.y_dram = nc.dram_tensor("expert_out", (SLOTS + P, D), F32, kind="Internal").ap()
        with ExitStack() as c1:
            k.Rec = k.sb(c1, "Rec", [P, NB, WIN, E0])
            window_w = WindowWeights(k, c1)
            with ExitStack() as c2:
                recurrence_w = RecurrenceWeights(k, c2)
                setup(k, recurrence_w)
                recurrence(k, recurrence_w, window_w)
            window_attention(k, window_w)
        k.ffn_raw = k.sb(ctx, "ffn_raw", [P, KC * 2 * FF + FF // P * D], I32)
        k.ffn_loaded = k.sem(ctx, "f_loaded")
        with ExitStack() as c2:
            k.HS = k.sb(c2, "HS", [P, NT, D])
            k.slots = k.sb(c2, "slots", [P, NT, 2], U32)
            k.prob = k.sb(c2, "prob", [P, NT, 2])
            k.LG = k.sb(c2, "LG", [P, NB, TS, NE])
            with ExitStack() as c3:
                k.QKV = k.sb(c3, "QKV", [P, NT, QKVW])
                position_qkv(k)
                position_attention(k)
            w = RetentionWeights(k, c2)
            route(k, w)
            experts(k)
            retention(k, w)
        swiglu(k)


class RecurrenceWeights:

    def __init__(self, k, ctx):
        self.wg = k.sb(ctx, "wg", [P, KC, H0 * E0])
        self.bg = k.sb(ctx, "bg", [1, H0 * E0])
        self.wkv = k.sb(ctx, "wkv", [P, KC, H0 * P])
        self.ikv = k.sb(ctx, "ikv", [P, E0, L0])
        self.loaded = k.sem(ctx, "r_weights")
        self.a = k.a

    def load(self, sp):
        a = self.a
        sp.dma_start(self.wg[:, :, :], a["wg"].rearrange("(k p) n -> p k n", p=P)).then_inc(self.loaded, 16)
        sp.dma_start(self.bg[:, :], a["bg"]).then_inc(self.loaded, 16)
        sp.dma_start(self.wkv[:, :, :], a["wkv"].rearrange("(k p) n -> p k n", p=P)).then_inc(self.loaded, 16)
        sp.dma_start(self.ikv[:, :, :], a["ikv"]).then_inc(self.loaded, 16)


class WindowWeights:

    def __init__(self, k, ctx):
        self.wq = k.sb(ctx, "wq", [P, KC, H0 * DK])
        self.wo = k.sb(ctx, "wo", [P, 4, D])
        self.mask_f = k.sb(ctx, "mask_f", [32, E0 * 2 * L0])
        self.sel_f = k.sb(ctx, "sel_f", [32, P])
        self.loaded = k.sem(ctx, "w_weights")
        self.a = k.a

    def load(self, sp):
        a = self.a
        sp.dma_start(self.wq[:, :, :], a["wq"].rearrange("(k p) n -> p k n", p=P)).then_inc(self.loaded, 16)
        sp.dma_start(self.wo[:, :, :], a["wo"].rearrange("(k p) n -> p k n", p=P)).then_inc(self.loaded, 16)
        sp.dma_start(self.mask_f[:, :], a["mask"]).then_inc(self.loaded, 16)
        sp.dma_start(self.sel_f[:, :], a["sel"]).then_inc(self.loaded, 16)


def setup(k, following):
    nc, a = k.nc, k.a
    with ExitStack() as ctx:
        parts = [k.sem(ctx, f"x_part{n}") for n in range(2)]
        const = k.sem(ctx, "const_loaded")
        stats = k.sem(ctx, "x_stats")
        ones_set = k.sem(ctx, "ones_set")
        block = ctx.enter_context(nc.Block())

        @block.sync
        def _(sp):
            for n in range(NB):
                sp.dma_start(k.X[:, n * TS:(n + 1) * TS, :],
                             a["x"][n * T:(n + 1) * T, :].rearrange("(i p) c -> p i c", p=P)
                             ).then_inc(parts[n // (NB // 2)], 16)
            sp.dma_start(k.ident[:, :], a["ident"]).then_inc(const, 16)
            following.load(sp)
            sp.wait_ge(const, 16)

        @block.gpsimd
        def _(pool):
            nc.gpsimd.memset(k.mhalf[:, :], -0.5).then_inc(ones_set, 1)
            nc.gpsimd.memset(k.ones[:, :], 1.0).then_inc(ones_set, 1)

        @block.vector
        def _(dve):
            for n in range(2):
                dve.wait_ge(parts[n], 64)
                for t in range(n * NT // 2, (n + 1) * NT // 2):
                    nc.vector.bn_stats(k.BST[:, t, :], k.X[:, t, :]).then_inc(stats, 1)


def stats_steps(nc, chain, bst, mean, var, tmp, ready):
    me, mo, ve, vo = bst[:, :, 1], bst[:, :, 4], bst[:, :, 2], bst[:, :, 5]
    m1 = chain.mark(nc.vector.tensor_tensor(mean, me, mo, ALU.add))
    m2 = chain.mark(nc.vector.tensor_tensor(tmp, me, mo, ALU.subtract))
    m3 = chain.mark(nc.vector.tensor_tensor(var, ve, vo, ALU.add))
    chain.after(m1)
    chain.mark(nc.vector.tensor_scalar(mean, mean, 0.5, None, ALU.mult))
    chain.after(m2)
    chain.step(nc.vector.tensor_tensor(tmp, tmp, tmp, ALU.mult))
    chain.after(m3)
    chain.step(nc.vector.scalar_tensor_tensor(var, tmp, D / 4.0, var, ALU.mult, ALU.add))
    nc.vector.tensor_scalar(var, var, 1.0 / D, EPS, ALU.mult, ALU.add).then_inc(ready, 1)


class RowStats:

    def __init__(self, k, ctx):
        self.k, self.n = k, k.n
        self.tmp = k.sb(ctx, f"ln{k.n}_tmp", [P, NT])
        self.var = k.sb(ctx, f"ln{k.n}_var", [P, NT])
        k.n += 1

    def sums(self, dve):
        k = self.k
        chain = Chain(dve, k.ln_steps, self.n * 6)
        stats_steps(k.nc, chain, k.BST[:, :, :], k.mean[:, :], self.var[:, :], self.tmp[:, :], k.ln_var)
        assert chain.n == 6

    def roots(self, pool):
        k = self.k
        pool.wait_ge(k.ln_var, self.n + 1)
        for r in (slice(0, TS), slice(TS, NT)):
            k.nc.gpsimd.tensor_tensor(k.rstd[:, r], self.var[:, r], k.mhalf[:, r], ALU.pow).then_inc(k.ln_root, 1)

    def ready(self, eng, part):
        eng.wait_ge(self.k.ln_root, self.n * 2 + part + 1)


def normalise(k, dst, tile):
    return k.nc.vector.tensor_scalar(dst, k.X[:, bass.ds(tile, 1), :], k.mean[:, bass.ds(tile, 1)],
                                     k.rstd[:, bass.ds(tile, 1)], ALU.subtract, ALU.mult)


def recurrence(k, w, following):
    nc, a = k.nc, k.a
    HE = H0 * E0
    HH = H0 // 2
    EV = E0 - 1
    summed_pairs = [(h, e) for h in range(H0) for e in range(EV if h < HH else EV - 1)]
    NV = len(summed_pairs)
    with ExitStack() as ctx:
        wg, bg, wkv, ikv, weights = w.wg, w.bg, w.wkv, w.ikv, w.loaded
        XN = k.sb(ctx, "XN1", [P, 2, D])
        XT = k.sb(ctx, "XT1", [P, TS, KC, P])
        eg = k.sb(ctx, "eg", [P, TS, HE])
        G = k.sb(ctx, "G", [P, TS, HE])
        A = k.sb(ctx, "A", [P, TS, E0])
        gated = k.sb(ctx, "gated", [P, 2, H0 + HH, P])
        acc = k.sb(ctx, "acc", [P, 2, E0 + 1, P])
        gT = k.sb(ctx, "gT", [P, E0, T])
        AT = k.sb(ctx, "AT", [P, E0, T])
        seed = k.sb(ctx, "seed", [P, E0, L0])
        psT = k.ps(ctx, "psT", [P, KC, P])
        psG = k.ps(ctx, "psG", [P, TS, HE])
        psKV = [[k.ps(ctx, f"psKV{s}{h}", [P, 4, P]) for h in range(2)] for s in range(2)]
        psR = k.ps(ctx, "psR", [P, E0, P])
        psA = k.ps(ctx, "psA", [P, E0, P])
        xn_ready, t_ready, t_evac = k.sem(ctx, "r_xn_ready"), k.sem(ctx, "r_t_ready"), k.sem(ctx, "r_t_evac")
        g_ready, g_exp, g_gate = k.sem(ctx, "r_g_ready"), k.sem(ctx, "r_g_exp"), k.sem(ctx, "r_g_gate")
        kv_ready, acc_step = k.sem(ctx, "r_kv_ready"), k.sem(ctx, "r_acc_step")
        gated_ready, gated_step, gated_summed = k.sem(ctx, "r_gated"), k.sem(ctx, "r_gated_step"), k.sem(ctx, "r_gated_summed")
        ra_ready, ra_evac = k.sem(ctx, "r_ra_ready"), k.sem(ctx, "r_ra_evac")
        scan_done = k.sem(ctx, "r_scan_done")
        rows = RowStats(k, ctx)
        xt_stored = [k.sem(ctx, f"r_xt_stored{u}") for u in range(TS)]
        gate_step, scan_step = k.sem(ctx, "r_gate_step"), k.sem(ctx, "r_scan_step")
        init_set = k.sem(ctx, "r_init_set")
        zero = k.sb(ctx, "zero_rows", [P, CAP // P, D])
        zero_set, zero_stored = k.sem(ctx, "zero_set"), k.sem(ctx, "zero_stored")
        block = ctx.enter_context(nc.Block())

        def stream(eng, step):
            def peeled(g):
                step(g // TS, g % TS, lambda d: 0 <= g + d < NT)
            for g in range(-TS, TS):
                peeled(g)
            with eng.Fori(1, NB - 1) as i:
                for u in range(TS):
                    step(i, u, lambda d: True)
            for g in range(NT - TS, NT + 1):
                peeled(g)

        @block.sync
        def _(sp):
            following.load(sp)
            for u in range(TS):
                sp.sem_inc(xt_stored[u], 16)
            sp.wait_ge(zero_set, 1)
            sp.dma_start(k.y_dram[SLOTS:SLOTS + P, :], zero[:, 0, :]).then_inc(zero_stored, 16)
            assert NE == NB
            with sp.Fori(0, NB) as i:
                sp.dma_start(k.xt_dram[bass.ds(i * CAP, CAP), :].rearrange("(i p) c -> p i c", p=P),
                             zero[:, :, :]).then_inc(zero_stored, 16)
                for u in range(TS):
                    sp.wait_ge(t_evac, i * TS + u + 2)
                    sp.dma_start(k.xT_dram[:, :, bass.ds(i * T + u * P, P)], XT[:, u, :, :]).then_inc(xt_stored[u], 16)
            for u in range(TS):
                sp.wait_ge(xt_stored[u], 16 * (NB + 1))
            sp.wait_ge(zero_stored, 16 * (NE + 1))

        @block.gpsimd
        def _(pool):
            pool.sem_inc(gated_summed, 2)
            rows.roots(pool)
            nc.gpsimd.memset(zero[:, :, :], 0.0).then_inc(zero_set, 1)
            pool.wait_ge(weights, 64)
            for n in range(NB):
                nc.gpsimd.tensor_copy(k.Rec[:, n, 0:L0, :].rearrange("p t e -> p e t"), ikv[:, :, :]).then_inc(init_set, 1)

            def head_sum(t, v):
                ch = Chain(pool, gated_step, t * 2)
                x = gated[:, v % 2, :, :]
                pool.wait_ge(gated_ready, t * 2 + 2 + 8)
                ch.step(nc.gpsimd.tensor_tensor(x[:, HH:H0, :], x[:, HH:H0, :], x[:, 0:HH, :], ALU.add))
                two = x[:, HH:, :].rearrange("p (e h) c -> p e h c", e=2)
                ch.step(nc.gpsimd.tensor_tensor(two[:, :, 0:2, :], two[:, :, 0:2, :], two[:, :, 2:4, :], ALU.add))
                pool.wait_ge(ra_ready, t * 2 + 5)
                nc.gpsimd.tensor_tensor(acc[:, v % 2, EV:, :], two[:, :, 0, :], two[:, :, 1, :], ALU.add).then_inc(gated_summed, 1)

            def step(i, u, has):
                if has(0):
                    head_sum(i * TS + u, u)

            stream(pool, step)

        @block.tensor
        def _(pe):
            pe.sem_inc(t_ready, 2)
            pe.sem_inc(kv_ready, 4)
            pe.sem_inc(ra_ready, 8)
            pe.wait_ge(weights, 64)

            def turned(t, v):
                pe.wait_ge(t_evac, t + 1)
                pe.wait_ge(xn_ready, t + 1)
                for c in range(KC):
                    mm = pe.transpose(psT[:, c, :], XN[:, v % 2, c * P:(c + 1) * P], k.ident[:, :])
                mm.then_inc(t_ready, 1)

            def gates(t, v):
                pe.wait_ge(t_evac, t + 2)
                pe.wait_ge(g_exp, t + 1)
                for c in range(KC):
                    pe.matmul(psG[:, v, :], XT[:, v, c, :], wg[:, c, :], start=(c == 0), stop=False)
                pe.matmul(psG[:, v, :], k.ones[0:1, :], bg[0:1, :], start=False, stop=True).then_inc(g_ready, 1)

            def keys_values(t, v):
                pe.wait_ge(t_evac, t + 2)
                pe.wait_ge(acc_step, t * NV + NV)
                pe.wait_ge(gated_ready, t * 2 + 6)
                for half in range(2):
                    for c in range(KC):
                        mm = pe.matmul(psKV[v % 2][half][:, :, :], XT[:, v, c, :],
                                       wkv[:, c, half * 512:(half + 1) * 512], start=(c == 0), stop=(c == KC - 1))
                mm.then_inc(kv_ready, 1)

            def sums_turned(t, v):
                pe.wait_ge(acc_step, t * NV + 3 * NV)
                pe.wait_ge(gated_summed, t + 3)
                pe.wait_ge(ra_evac, t * 2 + 1)
                for e in (0, 1, 3):
                    pe.transpose(psR[:, e, :], acc[:, v % 2, e, :], k.ident[:, :])
                pe.matmul(psR[:, EV - 1, :], acc[:, v % 2, EV - 1, :], k.ident[:, :], start=True, stop=False)
                pe.matmul(psR[:, EV - 1, :], acc[:, v % 2, E0, :], k.ident[:, :], start=False, stop=True).then_inc(ra_ready, 1)
                pe.wait_ge(ra_evac, t * 2 + 2)
                for e in range(E0):
                    mm = pe.transpose(psA[:, e, :], bc(A[:, v, e:e + 1], [P, P]), k.ident[:, :])
                mm.then_inc(ra_ready, 1)

            def step(i, u, has):
                g = i * TS + u
                if has(3):
                    turned(g + 3, (u + 3) % TS)
                if has(2):
                    gates(g + 2, (u + 2) % TS)
                if has(1):
                    keys_values(g + 1, (u + 1) % TS)
                if has(-1):
                    sums_turned(g - 1, (u - 1) % TS)

            stream(pe, step)

        @block.scalar
        def _(act):
            act.sem_inc(t_evac, 1)
            act.sem_inc(g_exp, 1)
            act.sem_inc(gated_ready, 8)
            act.sem_inc(ra_evac, 2)

            def turned(t, v, i):
                act.wait_ge(t_ready, t + 3)
                act.wait_ge(kv_ready, t + 1)
                act.wait_ge(xt_stored[v], i * 16 + 16)
                nc.scalar.copy(XT[:, v, :, :], psT[:, :, :]).then_inc(t_evac, 1)

            def exponential(t, v):
                act.wait_ge(g_ready, t + 1)
                act.wait_ge(g_gate, t + 1)
                nc.scalar.activation(eg[:, v, :], psG[:, v, :], ACT.Exp, scale=-1.0).then_inc(g_exp, 1)

            def gate(t, v, half):
                if half == 1:
                    act.wait_ge(kv_ready, t + 1 + 4)
                    act.wait_ge(g_gate, t + 1 + 4)
                    act.wait_ge(gated_summed, t + 1)
                else:
                    act.wait_ge(acc_step, t * NV + (HH * EV + 2 * NV))
                for h in range(4 * half, 4 * half + 4):
                    for e in (EV, EV - 1)[:1 + half]:
                        place = h if e == EV else h + HH
                        ins = nc.scalar.activation(gated[:, v % 2, place, :], psKV[v % 2][half][:, h % 4, :], ACT.Copy,
                                                   scale=G[:, v, h * E0 + e:h * E0 + e + 1])
                ins.then_inc(gated_ready, 1)

            def sums_turned(t, v, i):
                if v == 0:
                    act.wait_ge(scan_done, i + 1)
                act.wait_ge(ra_ready, t * 2 + 1 + 8)
                nc.scalar.copy(gT[:, :, v * P:(v + 1) * P], psR[:, :, :]).then_inc(ra_evac, 1)
                act.wait_ge(ra_ready, t * 2 + 2 + 8)
                nc.scalar.copy(AT[:, :, v * P:(v + 1) * P], psA[:, :, :]).then_inc(ra_evac, 1)

            def step(i, u, has):
                g = i * TS + u
                if has(0):
                    gate(g, u, 1)
                if has(3):
                    turned(g + 3, (u + 3) % TS, i + (u + 3) // TS)
                if has(2):
                    exponential(g + 2, (u + 2) % TS)
                if has(-1):
                    sums_turned(g - 1, (u - 1) % TS, i)
                if has(0):
                    gate(g, u, 0)

            stream(act, step)

        @block.vector
        def _(dve):
            dve.sem_inc(g_gate, 4)
            dve.sem_inc(acc_step, 2 * NV)
            dve.sem_inc(scan_done, 1)
            rows.sums(dve)
            rows.ready(dve, 0)
            dve.wait_ge(weights, 64)

            def normed(t, v):
                dve.wait_ge(t_ready, t + 1)
                normalise(k, XN[:, v % 2, :], t).then_inc(xn_ready, 1)

            GATE_PARTS = 5

            def gates(t, v, part):
                if part > 0:
                    dve.wait_ge(gate_step, t * 4 + part)
                if part == 0:
                    dve.wait_ge(g_exp, t + 2)
                    dve.wait_ge(gated_ready, t * 2 + 2)
                    nc.vector.tensor_scalar(G[:, v, :], eg[:, v, :], 1.0, None, ALU.add).then_inc(gate_step, 1)
                elif part == 1:
                    nc.vector.reciprocal(G[:, v, :], G[:, v, :]).then_inc(gate_step, 1)
                elif part == 2:
                    dve.wait_ge(ra_ready, t * 2 + 2)
                    nc.vector.tensor_reduce(A[:, v, :], G[:, v, :].rearrange("p (h e) -> p e h", e=E0), AX.X,
                                            ALU.add).then_inc(gate_step, 1)
                elif part == 3:
                    nc.vector.tensor_scalar(A[:, v, :], A[:, v, :], 1.0, -1.0, ALU.min, ALU.mult).then_inc(gate_step, 1)
                else:
                    nc.vector.tensor_scalar(A[:, v, :], A[:, v, :], 1.0, None, ALU.add).then_inc(g_gate, 1)

            def head_sum(t, v, gates_after):
                dve.wait_ge(kv_ready, t + 1 + 4)
                dve.wait_ge(g_gate, t + 1 + 4)
                dve.wait_ge(ra_ready, t * 2 + 5)
                for n, (h, e) in enumerate(summed_pairs):
                    if (h, e) == (HH, 0):
                        dve.wait_ge(gated_ready, t * 2 + 1 + 8)
                    g = G[:, v, h * E0 + e:h * E0 + e + 1]
                    kv = psKV[v % 2][h // 4][:, h % 4, :]
                    if h == 0:
                        ins = nc.vector.tensor_scalar(acc[:, v % 2, e, :], kv, g, None, ALU.mult)
                    else:
                        dve.wait_ge(acc_step, t * NV + (summed_pairs.index((h - 1, e)) + 1 + 2 * NV))
                        ins = nc.vector.scalar_tensor_tensor(acc[:, v % 2, e, :], kv, g, acc[:, v % 2, e, :],
                                                             ALU.mult, ALU.add)
                    ins.then_inc(acc_step, 1)
                    if gates_after and n % 4 == 3:
                        gates(t + 1, (v + 1) % TS, n // 4)

            def scan(i):
                ch = Chain(dve, scan_step, i * 3)
                dve.wait_ge(ra_evac, i * 2 * TS + 2 * TS + 2)
                gs = gT[:, :, :].rearrange("p e (l c) -> p e l c", c=T // L0)[:, :, :, 0]
                As = AT[:, :, :].rearrange("p e (l c) -> p e l c", c=T // L0)[:, :, :, 0]
                ch.step(nc.vector.tensor_tensor(seed[:, :, :], As, ikv[:, :, :], ALU.mult))
                ch.step(nc.vector.tensor_tensor(gs, gs, seed[:, :, :], ALU.add))
                ch.step(nc.vector.memset(As, 0.0))
                for e in range(E0):
                    n = nc.vector.tensor_tensor_scan(k.Rec[:, bass.ds(i, 1), L0:WIN, e].rearrange("p a t -> p (a t)"),
                                                     AT[:, e, :], gT[:, e, :], 0.0, ALU.mult, ALU.add)
                n.then_inc(scan_done, 1)

            def step(i, u, has):
                g = i * TS + u
                if isinstance(g, int) and g == 0:
                    rows.ready(dve, 1)
                if has(4):
                    normed(g + 4, u)
                if has(0):
                    head_sum(g, u, has(1))
                elif has(1):
                    for part in range(GATE_PARTS):
                        gates(g + 1, (u + 1) % TS, part)
                if u == 0 and has(-1):
                    scan(i - 1)

            stream(dve, step)


def window_attention(k, w):
    nc, a = k.nc, k.a
    QB = 32
    NQ = T // QB
    KW = 2 * L0
    NG = (NQ + 1 + 3) // 4
    MADE = 4 + NG
    SP2 = 2 * NQ
    at = {1: 0, 4: 1, 7: 2, 10: 3, 11: 4, 12: 5, 13: 6, 14: 7, 15: 8}
    scale = 1.0 / 8.0
    with ExitStack() as ctx:
        wq, wo, mask_f, sel_f, weights = w.wq, w.wo, w.mask_f, w.sel_f, w.loaded
        mask = k.sb(ctx, "mask", [QB, E0 * KW], BF16)
        sel = k.sb(ctx, "sel", [QB, P], BF16)
        R = k.sb(ctx, "R", [P, WIN, E0])
        XS = k.sb(ctx, "XS", [P, KC, T])
        QT = [k.sb(ctx, f"QT{r}", [DK, 2, NQ, 4, QB]) for r in range(2)]
        V = [k.sb(ctx, f"V{r}", [P, NQ + 1, DK]) for r in range(2)]
        mx = k.sb(ctx, "mx", [P, 2, 2])
        nm = k.sb(ctx, "nm", [P, 2, 2])
        sums = k.sb(ctx, "sums", [P, 4, 2])
        rs = k.sb(ctx, "rs", [P, 2, 2])
        probs = k.sb(ctx, "probs", [P, 2, 2, E0 * KW])
        PT = k.sb(ctx, "PT", [P, 2, 2, 2, P])
        Y = k.sb(ctx, "Y", [P, 2, 2, DK])
        YT = k.sb(ctx, "YT", [P, 4, T])
        psS = [k.ps(ctx, f"psS{s}", [P, 2, E0 * KW]) for s in range(2)]
        psP = [k.ps(ctx, f"psP{s}", [P, 2, 2, P]) for s in range(2)]
        psO = k.ps(ctx, "psO", [P, 2, DK])
        psY = k.ps(ctx, "psY", [P, 4, QB])
        psZ = k.ps(ctx, "psZ", [P, D])
        psB = k.ps(ctx, "psB", [P, T])
        casts = k.sem(ctx, "w_casts")
        r_ready, x_ready = k.sem(ctx, "w_r_ready"), k.sem(ctx, "w_x_ready")
        b_ready, b_evac = k.sem(ctx, "w_b_ready"), k.sem(ctx, "w_b_evac")
        s_ready, m_ready, e_done = k.sem(ctx, "w_s_ready"), k.sem(ctx, "w_m_ready"), k.sem(ctx, "w_e_done")
        p_ready, p_evac = k.sem(ctx, "w_p_ready"), k.sem(ctx, "w_p_evac")
        o_ready, o_evac = k.sem(ctx, "w_o_ready"), k.sem(ctx, "w_o_evac")
        y_ready, y_evac = k.sem(ctx, "w_y_ready"), k.sem(ctx, "w_y_evac")
        z_ready, z_added = k.sem(ctx, "w_z_ready"), k.sem(ctx, "w_z_added")
        dstep = k.sem(ctx, "w_dstep")
        block = ctx.enter_context(nc.Block())

        def turns(eng, step, ends):
            for s in range(SP2):
                step(0, s, s)
            with eng.Fori(1, NB // 2) as j:
                for s in range(SP2):
                    step(j, s, SP2)
            for s in range(ends):
                step(NB // 2, s, -1)

        class At:
            def __init__(self, j, s, lag):
                w = s - lag
                self.g = j * SP2 + w
                self.r, self.q = (w % SP2) // NQ, w % NQ
                self.t = j * 2 + w // NQ

        def lagging(j, s, late, lag):
            if late >= 0 and lag > late or late < 0 and lag <= s:
                return None
            return At(j, s, lag)

        @block.sync
        def _(sp):
            sp.dma_start(XS[:, :, :], k.xT_dram[:, :, 0:T]).then_inc(x_ready, 16)
            with sp.Fori(1, NB) as t:
                sp.wait_ge(b_ready, t * MADE - MADE + 4)
                sp.dma_start(XS[:, :, :], k.xT_dram[:, :, bass.ds(t * T, T)]).then_inc(x_ready, 16)
            sp.wait_ge(b_ready, NB * MADE - MADE + 4)
            sp.dma_start(XS[:, :, :], k.xT_dram[:, :, (NB - 1) * T:]).then_inc(x_ready, 16)

        @block.gpsimd
        def _(pool):
            def fetch(t):
                nc.gpsimd.tensor_copy(R[:, :, :].rearrange("p t e -> p (t e)"),
                                      k.Rec[:, bass.ds(t, 1), :, :].rearrange("p a t e -> p (a t e)")).then_inc(r_ready, 1)
            fetch(0)
            with pool.Fori(1, NB) as t:
                pool.wait_ge(b_ready, t * MADE)
                pass_gate(k, pool)
                fetch(t)
            pool.wait_ge(b_ready, NB * MADE)
            fetch(NB - 1)

        @block.tensor
        def _(pe):
            pe.sem_inc(p_ready, 2)
            pe.sem_inc(o_ready, 2)
            pe.sem_inc(y_ready, 2)
            pe.sem_inc(z_ready, 4)
            pe.wait_ge(weights, 64)
            pe.wait_ge(casts, 2)

            def make(t, r, n):
                pe.wait_ge(b_evac, t * MADE + n + 1)
                if n < 4:
                    pe.wait_ge(x_ready, t * 16 + 16)
                    for c in range(KC):
                        mm = pe.matmul(psB[:, :], wq[:, c, n * P:(n + 1) * P], XS[:, c, :],
                                       start=(c == 0), stop=(c == KC - 1))
                else:
                    if n == 4:
                        pe.wait_ge(r_ready, t + 1)
                    for q in range(4 * (n - 4), min(4 * (n - 4) + 4, NQ + 1)):
                        mm = pe.transpose(psB[:, q % 4 * P:(q % 4 + 1) * P],
                                          R[:, q * QB:(q + 1) * QB, :].rearrange("d t e -> d (t e)"), k.ident[:, :])
                mm.then_inc(b_ready, 1)

            def scores(b):
                if b.q == 0:
                    pe.wait_ge(b_evac, b.t * MADE + 4 + 1)
                pe.wait_ge(e_done, b.g * 2 + 2)
                pass_gate(k, pe)
                for hg in range(2):
                    o = psS[b.q % 2][:, hg, :]
                    pe.matmul(o, QT[b.r][:, hg, b.q, :, :].rearrange("d h t -> d (h t)"),
                              k.Rec[0:DK, bass.ds(b.t, 1), b.q * QB:b.q * QB + KW, :].rearrange("d a t e -> d (a t e)"),
                              start=(hg == 0), stop=False, skip_group_check=True)
                    mm = pe.matmul(o, sel[:, :], mask[:, :], start=False, stop=(hg == 1), skip_group_check=True)
                mm.then_inc(s_ready, 1)

            def transposes(b):
                pe.wait_ge(e_done, b.g * 2 + 2 + 4)
                pe.wait_ge(p_evac, b.g + 1)
                for hg in range(2):
                    for kt in range(2):
                        mm = pe.transpose(psP[b.q % 2][:, hg, kt, :], probs[:, b.q % 2, hg, kt * P:(kt + 1) * P], k.ident[:, :])
                mm.then_inc(p_ready, 1)

            def values(b):
                if b.q == 0:
                    pe.wait_ge(b_evac, b.t * MADE + MADE + 1)
                pe.wait_ge(p_evac, b.g + 1 + 2)
                pe.wait_ge(o_evac, b.g + 1)
                for hg in range(2):
                    for kt in range(2):
                        mm = pe.matmul(psO[:, hg, :], PT[:, b.q % 2, hg, kt, :], V[b.r][:, b.q + kt, :],
                                       start=(hg == 0 and kt == 0), stop=(hg == 1 and kt == 1), skip_group_check=True)
                mm.then_inc(o_ready, 1)

            def turn(b):
                pe.wait_ge(o_evac, b.g + 1 + 1)
                pe.wait_ge(y_evac, b.g + 1)
                pe.transpose(psY[:, :, :], Y[:, b.q % 2, :, :].rearrange("p g d -> p (g d)"),
                             k.ident[:, :]).then_inc(y_ready, 1)

            def project(b):
                u = b.q // 4
                pe.wait_ge(y_evac, b.g + 1 + 1)
                pe.wait_ge(z_added, b.t * TS + u + 1)
                for c in range(4):
                    mm = pe.matmul(psZ[:, :], YT[:, c, u * P:(u + 1) * P], wo[:, c, :], start=(c == 0), stop=(c == 3))
                mm.then_inc(z_ready, 1)

            def step(j, s, late):
                if late >= 0:
                    b = At(j, s, 0)
                    scores(b)
                if b1 := lagging(j, s, late, 1):
                    transposes(b1)
                if b2 := lagging(j, s, late, 2):
                    values(b2)
                if b3 := lagging(j, s, late, 3):
                    turn(b3)
                b4 = lagging(j, s, late, 4)
                if b4 and b4.q % 4 == 3:
                    project(b4)
                if late >= 0 and b.q in at:
                    make(b.t + 1, 1 - b.r, at[b.q])

            for n in range(MADE):
                make(0, 0, n)
            turns(pe, step, 5)

        @block.scalar
        def _(act):
            act.sem_inc(b_evac, 1)
            act.sem_inc(e_done, 4)
            act.sem_inc(y_evac, 1)

            def made(t, r, n):
                act.wait_ge(b_ready, t * MADE + n + 1)
                if n < 4:
                    for x in range(2):
                        ins = nc.scalar.copy(QT[r][:, n // 2, :, 2 * n % 4 + x, :],
                                             psB[x * DK:(x + 1) * DK, :].rearrange("d (b t) -> d b t", b=NQ))
                else:
                    g = n - 4
                    w = min(4, NQ + 1 - 4 * g)
                    ins = nc.scalar.copy(V[r][:, 4 * g:4 * g + w, :],
                                         psB[:, 0:w * P].rearrange("p (w c) -> p w c", c=P)[:, :, DK:P])
                ins.then_inc(b_evac, 1)

            def exponentials(b):
                act.wait_ge(m_ready, b.g + 1)
                act.wait_ge(p_ready, b.g + 1)
                for hg in range(2):
                    nc.scalar.activation(probs[:, b.q % 2, hg, :], psS[b.q % 2][:, hg, :], ACT.Exp,
                                         bias=nm[:, b.q % 2, hg:hg + 1], scale=scale,
                                         accum_out=sums[:, b.q % 4, hg:hg + 1]).then_inc(e_done, 1)

            def turned(b):
                act.wait_ge(y_ready, b.g + 1 + 2)
                act.wait_ge(z_ready, b.t * TS + b.q // 4 + 1)
                nc.scalar.copy(YT[:, :, b.q * QB:(b.q + 1) * QB], psY[:, :, :]).then_inc(y_evac, 1)

            def step(j, s, late):
                if late >= 0:
                    b = At(j, s, 0)
                    exponentials(b)
                if b3 := lagging(j, s, late, 3):
                    turned(b3)
                if late >= 0 and b.q in at:
                    made(b.t + 1, 1 - b.r, at[b.q])

            for n in range(MADE):
                made(0, 0, n)
            turns(act, step, 4)

        @block.vector
        def _(dve):
            dve.wait_ge(weights, 64)
            nc.vector.tensor_copy(mask[:, :], mask_f[:, :]).then_inc(casts, 1)
            nc.vector.tensor_copy(sel[:, :], sel_f[:, :]).then_inc(casts, 1)
            dve.sem_inc(p_evac, 2)
            dve.sem_inc(o_evac, 1)
            dve.sem_inc(z_added, 1)

            def maxima(b, ch):
                dve.wait_ge(s_ready, b.g + 1)
                dve.wait_ge(e_done, b.g * 2 + 2)
                ch.step(nc.vector.tensor_reduce(mx[:, b.q % 2, :], psS[b.q % 2][:, :, :], AX.X, ALU.max))
                nc.vector.tensor_scalar(nm[:, b.q % 2, :], mx[:, b.q % 2, :], -scale, None, ALU.mult).then_inc(m_ready, 1)

            def turned(b):
                dve.wait_ge(p_ready, b.g + 1 + 2)
                dve.wait_ge(o_ready, b.g + 1)
                nc.vector.tensor_copy(PT[:, b.q % 2, :, :, :], psP[b.q % 2][:, :, :, :]).then_inc(p_evac, 1)

            def divided(b, ch):
                ch.step(nc.vector.reciprocal(rs[:, b.q % 2, :], sums[:, b.q % 4, :]))
                dve.wait_ge(o_ready, b.g + 1 + 2)
                dve.wait_ge(y_ready, b.g + 1)
                nc.vector.tensor_tensor(Y[:, b.q % 2, :, :], psO[:, :, :], bc(rs[:, b.q % 2, :].unsqueeze(2), [P, 2, DK]),
                                        ALU.mult).then_inc(o_evac, 1)

            def add(b, ch):
                n = b.t * TS + b.q // 4
                dve.wait_ge(z_ready, n + 1 + 4)
                x = k.X[:, bass.ds(n, 1), :].rearrange("p a c -> p (a c)")
                ch.step(nc.vector.tensor_tensor(x, x, psZ[:, :], ALU.add))
                pass_gate(k, dve)
                nc.vector.bn_stats(k.BST[:, bass.ds(n, 1), :].rearrange("p a c -> p (a c)"), x).then_inc(z_added, 1)

            chains = {}

            def step(j, s, late):
                if s == 0:
                    done = chains[0].n if chains else 0
                    NST = SP2 * 2 + 2 * TS
                    chains[len(chains)] = Chain(dve, dstep, (j - 1) * NST + done if chains else 0)
                ch = chains[len(chains) - 1]
                if late >= 0:
                    maxima(At(j, s, 0), ch)
                if b1 := lagging(j, s, late, 1):
                    turned(b1)
                if b2 := lagging(j, s, late, 2):
                    divided(b2, ch)
                b5 = lagging(j, s, late, 5)
                if b5 and b5.q % 4 == 3:
                    add(b5, ch)
                if s == SP2 - 1 and len(chains) == 2:
                    assert ch.n == SP2 * 2 + 2 * TS

            turns(dve, step, 6)


def position_qkv(k):
    nc, a = k.nc, k.a
    with ExitStack() as ctx:
        wqkv = k.sb(ctx, "wqkv", [P, KC, QKVW])
        lnw, lnb = k.sb(ctx, "ln1w", [P, KC]), k.sb(ctx, "ln1b", [P, KC])
        bst = k.sb(ctx, "p_bst", [P, TS, 6])
        mean, var = k.sb(ctx, "p_mean", [P, TS]), k.sb(ctx, "p_var", [P, TS])
        tmp, rstd = k.sb(ctx, "p_tmp", [P, TS]), k.sb(ctx, "p_rstd", [P, TS])
        XN = k.sb(ctx, "p_XN", [P, TS, D])
        XT = k.sb(ctx, "p_XT", [P, KC, T])
        psT = [k.ps(ctx, f"p_psT{c}", [P, T]) for c in range(KC)]
        psQ = [k.ps(ctx, f"p_psQ{s}", [P, QKVW]) for s in range(4)]
        weights = k.sem(ctx, "p_weights")
        steps, var_ready, root = k.sem(ctx, "p_steps"), k.sem(ctx, "p_var_ready"), k.sem(ctx, "p_root")
        xn_ready, t_ready, t_evac = k.sem(ctx, "p_xn_ready"), k.sem(ctx, "p_t_ready"), k.sem(ctx, "p_t_evac")
        q_ready, q_evac = k.sem(ctx, "p_q_ready"), k.sem(ctx, "p_q_evac")
        rows = RowStats(k, ctx)
        block = ctx.enter_context(nc.Block())

        @block.sync
        def _(sp):
            sp.dma_start(wqkv[:, :, :], a["qkv1"].rearrange("(k p) n -> p k n", p=P)).then_inc(weights, 16)
            sp.dma_start(lnw[:, :], a["ln1w"]).then_inc(weights, 16)
            sp.dma_start(lnb[:, :], a["ln1b"]).then_inc(weights, 16)

        @block.gpsimd
        def _(pool):
            rows.roots(pool)
            with pool.Fori(0, NB) as i:
                pool.wait_ge(var_ready, i + 1)
                nc.gpsimd.tensor_tensor(rstd[:, :], var[:, :], k.mhalf[:, 0:TS], ALU.pow).then_inc(root, 1)

        @block.vector
        def _(dve):
            NST = TS * 2 + 6
            rows.sums(dve)
            rows.ready(dve, 1)
            with dve.Fori(0, NB) as i:
                ch = Chain(dve, steps, i * NST)
                for u in range(TS):
                    hs = k.HS[:, bass.ds(i * TS + u, 1), :].rearrange("p a c -> p (a c)")
                    n = ch.mark(normalise(k, hs, i * TS + u))
                    ch.after(n)
                    pass_gate(k, dve)
                    n = ch.mark(nc.vector.bn_stats(bst[:, u, :], hs))
                ch.after(n)
                stats_steps(nc, ch, bst[:, :, :], mean[:, :], var[:, :], tmp[:, :], var_ready)
                dve.wait_ge(root, i + 1)
                dve.wait_ge(t_ready, i + 1)
                for u in range(TS):
                    hs = k.HS[:, bass.ds(i * TS + u, 1), :].rearrange("p a c -> p (a c)")
                    nc.vector.tensor_scalar(XN[:, u, :], hs, mean[:, u:u + 1], rstd[:, u:u + 1],
                                            ALU.subtract, ALU.mult).then_inc(xn_ready, 1)
                assert ch.n == NST

        @block.tensor
        def _(pe):
            pe.sem_inc(t_ready, 1)
            pe.sem_inc(q_ready, 4)
            pe.wait_ge(weights, 48)
            with pe.Fori(0, NB) as i:
                pe.wait_ge(t_evac, i * 2 + 2)
                for u in range(TS):
                    pe.wait_ge(xn_ready, i * TS + u + 1)
                    for c in range(KC):
                        mm = pe.transpose(psT[c][:, u * P:(u + 1) * P], XN[:, u, c * P:(c + 1) * P], k.ident[:, :])
                mm.then_inc(t_ready, 1)
                pe.wait_ge(t_evac, i * 2 + 4)
                for u in range(TS):
                    pe.wait_ge(q_evac, i * TS + u + 1)
                    for c in range(KC):
                        mm = pe.matmul(psQ[u][:, :], XT[:, c, u * P:(u + 1) * P], wqkv[:, c, :],
                                       start=(c == 0), stop=(c == KC - 1))
                    mm.then_inc(q_ready, 1)

        @block.scalar
        def _(act):
            act.sem_inc(t_evac, 2)
            act.sem_inc(q_evac, 4)
            act.wait_ge(weights, 48)
            with act.Fori(0, NB) as i:
                act.wait_ge(t_ready, i + 2)
                act.wait_ge(q_ready, i * TS + 4)
                for c in range(KC):
                    nc.scalar.activation(XT[:, c, :], psT[c][:, :], ACT.Identity, bias=lnb[:, c:c + 1],
                                         scale=lnw[:, c:c + 1]).then_inc(t_evac, 1)
                for u in range(TS):
                    act.wait_ge(q_ready, i * TS + u + 1 + 4)
                    nc.scalar.copy(k.QKV[:, bass.ds(i * TS + u, 1), :].rearrange("p a c -> p (a c)"),
                                   psQ[u][:, :]).then_inc(q_evac, 1)


def position_attention(k):
    nc, a = k.nc, k.a
    S = NB
    G = 4

    def units(rows):
        return [(s, t, min(t + G, s + 1)) for s in rows for t in range(0, s + 1, G)]

    own_rows_s, own_rows_v = (1, 7), (2, 7)
    score_units = units([s for s in range(S) if s not in own_rows_s])
    value_units = units([s for s in range(S) if s not in own_rows_v])
    own_scores, own_values = units(own_rows_s), units(own_rows_v)
    NU = len(score_units)
    assert NU == len(value_units) == 9 and len(own_values) == 3
    with ExitStack() as ctx:
        wp = k.sb(ctx, "wp", [P, KC, D])
        wr = k.sb(ctx, "wr", [P, KC, NE])
        lnw, lnb = k.sb(ctx, "rl_w", [P, KC]), k.sb(ctx, "rl_b", [P, KC])
        sc = k.sb(ctx, "sc", [P, S, S, NH])
        PR = k.sb(ctx, "a_PR", [P, S, S, NH])
        mx = k.sb(ctx, "a_mx", [P, S, NH])
        prodS = k.sb(ctx, "prodS", [P, 3, G, D])
        prodV = k.sb(ctx, "prodV", [P, 3, G, D])
        ownS = k.sb(ctx, "ownS", [P, G, D])
        ownV = k.sb(ctx, "ownV", [P, 3, G, D])
        AT = k.sb(ctx, "o_AT", [P, 2, KC, P])
        mean, var = k.sb(ctx, "o_mean", [P, S]), k.sb(ctx, "o_var", [P, S])
        tmp, rstd = k.sb(ctx, "o_tmp", [P, S]), k.sb(ctx, "o_rstd", [P, S])
        XN = k.sb(ctx, "o_XN", [P, 4, D])
        XT = k.sb(ctx, "o_XT", [P, 2, KC, P])
        psA = [k.ps(ctx, f"o_psA{s}", [P, KC, P]) for s in range(2)]
        psH = [k.ps(ctx, f"o_psH{s}", [P, D]) for s in range(2)]
        psT = [k.ps(ctx, f"o_psT{s}", [P, KC, P]) for s in range(2)]
        psL = k.ps(ctx, "o_psL", [P, S, NE])
        weights, steps = k.sem(ctx, "a_weights"), k.sem(ctx, "a_steps")
        s_made, s_summed = k.sem(ctx, "a_s_made"), k.sem(ctx, "a_s_summed")
        sub_ready, exp_ready, p_ready = k.sem(ctx, "a_sub"), k.sem(ctx, "a_exp"), k.sem(ctx, "a_p")
        v_made, v_used = k.sem(ctx, "a_v_made"), k.sem(ctx, "a_v_used")
        own_made, own_used = k.sem(ctx, "a_own_made"), k.sem(ctx, "a_own_used")
        a_evac = k.sem(ctx, "a_a_evac")
        h_ready, h_added = k.sem(ctx, "a_h_ready"), k.sem(ctx, "a_h_added")
        var_ready, root = k.sem(ctx, "a_var_ready"), k.sem(ctx, "a_root")
        xn_ready, t_ready, t_evac = k.sem(ctx, "a_xn_ready"), k.sem(ctx, "a_t_ready"), k.sem(ctx, "a_t_evac")
        l_ready, l_copied = k.sem(ctx, "a_l_ready"), k.sem(ctx, "a_l_copied")
        block = ctx.enter_context(nc.Block())

        def turns(eng, turn):
            turn(0, True, False, False)
            turn(1, True, True, False)
            with eng.Fori(2, TS) as i:
                turn(i, True, True, True)
            turn(TS, False, True, True)
            turn(TS + 1, False, False, True)

        def row(s, bt):
            return k.QKV[:, bass.ds(bt + s * TS, 1), :].rearrange("p a (g c) -> p (a g) c", g=NKV)

        def fwd(x):
            return x.rearrange("p (g j d) -> p g j d", g=NKV, j=QG)

        def score_product(eng, dst, bt, s, t):
            q = row(s, bt)[:, :, 0:QG * HD].rearrange("p g (j d) -> p g j d", j=QG)
            kk = row(t, bt)[:, :, QG * HD:QG * HD + HD].unsqueeze(2)
            return eng.tensor_tensor(fwd(dst), q, bc(kk, [P, NKV, QG, HD]), ALU.mult)

        def value_product(eng, dst, bt, s, t):
            v = row(t, bt)[:, :, QG * HD + HD:].unsqueeze(2)
            p = PR[:, s, t, :].rearrange("p (g j) -> p g j", g=NKV).unsqueeze(3)
            return eng.tensor_tensor(fwd(dst), bc(p, [P, NKV, QG, HD]), bc(v, [P, NKV, QG, HD]), ALU.mult)

        @block.sync
        def _(sp):
            sp.dma_start(wp[:, :, :], a["proj"].rearrange("(k p) n -> p k n", p=P)).then_inc(weights, 16)
            sp.dma_start(wr[:, :, :], a["router"].rearrange("(k p) n -> p k n", p=P)).then_inc(weights, 16)
            sp.dma_start(lnw[:, :], a["ln2w"]).then_inc(weights, 16)
            sp.dma_start(lnb[:, :], a["ln2b"]).then_inc(weights, 16)

        @block.gpsimd
        def _(pool):
            def turn(i, entering, leaving, last):
                for m in range(NU + 3):
                    if entering and m < NU:
                        s, t0, t1 = score_units[m]
                        pool.wait_ge(s_summed, i * NU + m + 1)
                        pass_gate(k, pool)
                        for t in range(t0, t1):
                            ins = score_product(nc.gpsimd, prodS[:, m % 3, t - t0, :], i, s, t)
                        ins.then_inc(s_made, 1)
                    n = m - 3
                    if leaving and n >= 0:
                        s, t0, t1 = value_units[n]
                        if n == 0:
                            pool.wait_ge(p_ready, i)
                        pool.wait_ge(v_used, i * NU - NU + n + 1)
                        pass_gate(k, pool)
                        for t in range(t0, t1):
                            ins = value_product(nc.gpsimd, prodV[:, n % 3, t - t0, :], i - 1, s, t)
                        ins.then_inc(v_made, 1)

            turns(pool, turn)

        @block.tensor
        def _(pe):
            pe.sem_inc(v_used, 3)
            pe.sem_inc(own_used, 3)
            pe.wait_ge(weights, 64)

            def attended(j, s):
                pe.wait_ge(a_evac, j * S + s + 1)
                own = s in own_rows_v
                us = own_values if own else value_units
                for n, (s_, t0, t1) in enumerate(us):
                    if s_ != s:
                        continue
                    pe.wait_ge(own_made if own else v_made, j * len(us) + n + 1)
                    src = ownV[:, n, :, :] if own else prodV[:, n % 3, :, :]
                    for t in range(t0, t1):
                        for c in range(KC):
                            mm = pe.matmul(psA[s % 2][:, c, :], src[:, t - t0, c * P:(c + 1) * P], k.ident[:, :],
                                           start=(t == 0 and c == 0), stop=(t == s and c == KC - 1), skip_group_check=True)
                    mm.then_inc(own_used if own else v_used, 1)

            def project(j, s):
                pe.wait_ge(a_evac, j * S + s + 1 + 2)
                pe.wait_ge(h_added, j * S + s + 1)
                for c in range(KC):
                    mm = pe.matmul(psH[s % 2][:, :], AT[:, s % 2, c, :], wp[:, c, :], start=(c == 0), stop=(c == KC - 1))
                mm.then_inc(h_ready, 1)

            def turned(j, s):
                pe.wait_ge(xn_ready, j * S + s + 1)
                pe.wait_ge(t_evac, (j * S + s) * KC + KC)
                for c in range(KC):
                    mm = pe.transpose(psT[s % 2][:, c, :], XN[:, s % 4, c * P:(c + 1) * P], k.ident[:, :])
                mm.then_inc(t_ready, 1)

            def logits(j, s):
                pe.wait_ge(t_evac, (j * S + s) * KC + KC + 2 * KC)
                if s == 0:
                    pe.wait_ge(l_copied, j + 1)
                for c in range(KC):
                    mm = pe.matmul(psL[:, s, :], XT[:, s % 2, c, :], wr[:, c, :],
                                   start=(s == 0 and c == 0), stop=(s == S - 1 and c == KC - 1), skip_group_check=True)
                mm.then_inc(l_ready, 1)

            def turn(i, entering, leaving, last):
                for s in range(S + 4):
                    if leaving and s < S:
                        attended(i - 1, s)
                    if leaving and 1 <= s <= S:
                        project(i - 1, s - 1)
                    if last and 3 <= s < S + 3:
                        turned(i - 2, s - 3)
                    if last and s >= 4:
                        logits(i - 2, s - 4)

            turns(pe, turn)

        @block.scalar
        def _(act):
            act.sem_inc(a_evac, 2)
            act.sem_inc(t_evac, 2 * KC)
            act.sem_inc(l_copied, 1)
            act.wait_ge(weights, 64)

            def turn(i, entering, leaving, last):
                if last:
                    act.wait_ge(var_ready, i - 1)
                    nc.scalar.activation(var[:, :], var[:, :], ACT.Sqrt).then_inc(root, 1)
                for s in range(S + 3):
                    if leaving and s < S:
                        j, own = i - 1, s in own_rows_v
                        n = sum(s_ <= s for s_, _, _ in (own_values if own else value_units))
                        act.wait_ge(own_used if own else v_used, j * (3 if own else NU) + n + 3)
                        act.wait_ge(h_ready, j * S + s + 1)
                        nc.scalar.copy(AT[:, s % 2, :, :], psA[s % 2][:, :, :]).then_inc(a_evac, 1)
                    if last and s >= 3:
                        j, s2 = i - 2, s - 3
                        act.wait_ge(t_ready, j * S + s2 + 1 + 4)
                        act.wait_ge(l_ready, j * S + s2 + 1)
                        for c in range(KC):
                            nc.scalar.activation(XT[:, s2 % 2, c, :], psT[s2 % 2][:, c, :], ACT.Identity,
                                                 bias=lnb[:, c:c + 1], scale=lnw[:, c:c + 1]).then_inc(t_evac, 1)
                    if entering and s == S - 2:
                        act.wait_ge(sub_ready, i + 1)
                        nc.scalar.activation(PR[:, :, :, :], PR[:, :, :, :], ACT.Exp, scale=0.25).then_inc(exp_ready, 1)
                if last:
                    act.wait_ge(l_ready, j * S + S + 2)
                    nc.scalar.copy(k.LG[:, :, bass.ds(j, 1), :].rearrange("p s a e -> p s (a e)"),
                                   psL[:, :, :]).then_inc(l_copied, 1)

            turns(act, turn)

        @block.vector
        def _(dve):
            dve.sem_inc(s_summed, 3)
            dve.sem_inc(h_added, 2)
            dve.sem_inc(h_ready, 2)
            dve.sem_inc(t_ready, 4)
            dve.sem_inc(l_ready, 2)
            by_t = sc[:, :, :, :].rearrange("p s t h -> p s h t")
            by_t_p = PR[:, :, :, :].rearrange("p s t h -> p s h t")

            def summed(src, s, t0, t1):
                return nc.vector.tensor_reduce(sc[:, s, t0:t1, :], src[:, 0:t1 - t0, :].rearrange(
                    "p t (h d) -> p t h d", d=HD), AX.X, ALU.add)

            def own_score(i, n, ch):
                s, t0, t1 = own_scores[n]
                for t in range(t0, t1):
                    m = ch.mark(score_product(nc.vector, ownS[:, t - t0, :], i, s, t))
                ch.after(m)
                ch.step(summed(ownS, s, t0, t1))

            def own_value(j, n):
                s, t0, t1 = own_values[n]
                dve.wait_ge(own_used, j * 3 + n + 1)
                pass_gate(k, dve)
                for t in range(t0, t1):
                    ins = value_product(nc.vector, ownV[:, n, t - t0, :], j, s, t)
                ins.then_inc(own_made, 1)

            def probabilities(j, ch):
                dve.wait_ge(exp_ready, j + 1)
                ch.step(nc.vector.tensor_reduce(mx[:, :, :], by_t_p, AX.X, ALU.add))
                ch.step(nc.vector.reciprocal(mx[:, :, :], mx[:, :, :]))
                nc.vector.tensor_tensor(by_t_p, by_t_p, bc(mx[:, :, :].unsqueeze(3), [P, S, NH, S]),
                                        ALU.mult).then_inc(p_ready, 1)
                dve.wait_ge(p_ready, j + 1)

            def add(j, s, ch):
                dve.wait_ge(h_ready, j * S + s + 1 + 2)
                hs = k.HS[:, bass.ds(j + s * TS, 1), :].rearrange("p a c -> p (a c)")
                ch.step(nc.vector.tensor_tensor(hs, hs, psH[s % 2][:, :], ALU.add))
                pass_gate(k, dve)
                nc.vector.bn_stats(k.BST[:, bass.ds(j + s * TS, 1), :].rearrange("p a c -> p (a c)"), hs).then_inc(h_added, 1)

            def statistics(j, ch):
                dve.wait_ge(h_added, j * S + S + 2)
                bst = k.BST[:, :, :].rearrange("p (s t) w -> p s t w", t=TS)[:, :, bass.ds(j, 1), :].rearrange(
                    "p s a w -> p s (a w)")
                stats_steps(nc, ch, bst, mean[:, :], var[:, :], tmp[:, :], var_ready)
                dve.wait_ge(root, j + 1)
                ch.step(nc.vector.reciprocal(rstd[:, :], var[:, :]))

            def normed(j, s):
                dve.wait_ge(t_ready, j * S + s + 1)
                hs = k.HS[:, bass.ds(j + s * TS, 1), :].rearrange("p a c -> p (a c)")
                nc.vector.tensor_scalar(XN[:, s % 4, :], hs, mean[:, s:s + 1], rstd[:, s:s + 1],
                                        ALU.subtract, ALU.mult).then_inc(xn_ready, 1)

            ENTER, LEAVE, LAST = 10 + 3 + 1, S - 2 + 2, 2 + 6 + 1
            own_score_at, own_value_at = {0: 0, 2: 1, 4: 2}, {1: 0, 5: 1, 6: 2}
            add_at = {3: 0, 4: 1, 5: 2, 6: 3, 8: 4}

            def turn(i, entering, leaving, last):
                before = ENTER * min(i, TS) + LEAVE * max(i - 1, 0) if isinstance(i, int) else i * (ENTER + LEAVE) - LEAVE
                before = before + (i - 2) * LAST if last else before
                ch = Chain(dve, steps, before + 1)
                for n in range(NU):
                    if entering:
                        s, t0, t1 = score_units[n]
                        dve.wait_ge(s_made, i * NU + n + 1)
                        summed(prodS[:, n % 3, :, :], s, t0, t1).then_inc(s_summed, 1)
                        if n in own_score_at:
                            own_score(i, own_score_at[n], ch)
                    if leaving and n == 0:
                        probabilities(i - 1, ch)
                    if last and n == 1:
                        for s in (S - 2, S - 1):
                            add(i - 2, s, ch)
                    if last and n == 2:
                        statistics(i - 2, ch)
                    if leaving and n in own_value_at:
                        own_value(i - 1, own_value_at[n])
                    if last and n >= 3:
                        normed(i - 2, n - 3)
                    if leaving and n in add_at:
                        add(i - 1, add_at[n], ch)
                if entering:
                    dve.wait_ge(s_summed, i * NU + NU + 3)
                    ch.step(nc.vector.tensor_reduce(mx[:, :, :], by_t, AX.X, ALU.max))
                    if leaving:
                        dve.wait_ge(v_made, i * NU)
                        dve.wait_ge(own_made, i * 3)
                    nc.vector.tensor_tensor(by_t_p, by_t, bc(mx[:, :, :].unsqueeze(3), [P, S, NH, S]),
                                            ALU.subtract).then_inc(sub_ready, 1)
                    dve.wait_ge(sub_ready, i + 1)
                if last:
                    normed(i - 2, S - 2)
                    normed(i - 2, S - 1)
                if leaving:
                    add(i - 1, 5, ch)
                assert ch.n == ENTER * entering + LEAVE * leaving + LAST * last, ch.n

            Chain(dve, steps).step(nc.vector.memset(sc[:, :, :, :], NEG))
            turns(dve, turn)


def route(k, following):
    nc, a = k.nc, k.a
    with ExitStack() as ctx:
        before = k.sb(ctx, "before", [P, P])
        iota8 = k.sb(ctx, "iota8", [P, NE])
        best = k.sb(ctx, "best", [P, NT, 8])
        bidx = k.sb(ctx, "bidx", [P, NT, 8], U32)
        idxf = k.sb(ctx, "idxf", [P, NT, 2])
        oh = k.sb(ctx, "oh", [P, 2, NT, NE])
        both = k.sb(ctx, "both", [P, NT, NE])
        seen = k.sb(ctx, "seen", [P, NT, NE])
        pick = k.sb(ctx, "pick", [P, 2, NT, NE])
        rank = k.sb(ctx, "rank", [P, NT, 2])
        fits = k.sb(ctx, "fits", [P, NT, 2])
        ed, es = k.sb(ctx, "ed", [P, NT]), k.sb(ctx, "es", [P, NT])
        slot = k.sb(ctx, "slot", [P, NT, 2])
        sidx = k.sb(ctx, "sidx", [P, 2, TS, 2], U32)
        XN = k.sb(ctx, "s_XN", [P, 2, TS, D])
        psR = k.ps(ctx, "o_psR", [P, NT, NE])
        weights, steps = k.sem(ctx, "o_weights"), k.sem(ctx, "o_steps")
        d_ready, d_exp = k.sem(ctx, "o_d_ready"), k.sem(ctx, "o_d_exp")
        m_ready, r_ready = k.sem(ctx, "o_m_ready"), k.sem(ctx, "o_r_ready")
        row_ready, free = k.sem(ctx, "o_row_ready"), k.sem(ctx, "o_row_free")
        sent = [k.sem(ctx, f"o_sent{s}") for s in range(2)]
        rows = RowStats(k, ctx)
        block = ctx.enter_context(nc.Block())

        @block.sync
        def _(sp):
            sp.dma_start(before[:, :], a["before"]).then_inc(weights, 16)
            sp.dma_start(iota8[:, :], a["iota8"]).then_inc(weights, 16)
            following.load(sp)

        @block.gpsimd
        def _(pool):
            pool.sem_inc(free, 2)
            rows.roots(pool)
            with pool.Fori(0, NB // 2) as i:
                for x in range(2):
                    pool.wait_ge(row_ready, (i * 2 + x) * (TS + 1) + TS + 1)
                    pass_gate(k, pool)
                    for u in range(TS):
                        for j in range(2):
                            pool.indirect_dma_start(
                                k.xt_dram[:, :], bass.IndirectOffsetOnAxis(ap=sidx[:, x, u, j:j + 1], axis=0),
                                XN[:, x, u, :], None, bounds_check=SLOTS - 1, oob_is_err=False,
                            ).then_inc(sent[x], 16)
                    if x == 1:
                        for y in range(2):
                            pool.wait_ge(sent[y], i * (2 * TS * 16) + 2 * TS * 16)
                            pool.sem_inc(free, 1)

        @block.tensor
        def _(pe):
            pe.wait_ge(weights, 32)
            pe.wait_ge(m_ready, 1)
            pe.matmul(psR[:, :, :].rearrange("p t e -> p (t e)"), before[:, :],
                      both[:, :, :].rearrange("p t e -> p (t e)"), start=True, stop=False)
            pe.matmul(psR[:, :, :].rearrange("p t e -> p (t e)"), k.ones[:, :],
                      seen[:, :, :].rearrange("p t e -> p (t e)"), start=False, stop=True).then_inc(r_ready, 1)

        @block.scalar
        def _(act):
            act.wait_ge(d_ready, 1)
            nc.scalar.activation(ed[:, :], ed[:, :], ACT.Exp).then_inc(d_exp, 1)

        @block.vector
        def _(dve):
            rows.sums(dve)
            ch = Chain(dve, steps)
            LG = k.LG[:, :, :, :].rearrange("p s t e -> p (s t) e")
            for t in range(NT):
                n = ch.mark(nc.vector.max(best[:, t, :], LG[:, t, :]))
            ch.after(n)
            for t in range(NT):
                n = ch.mark(nc.vector.max_index(bidx[:, t, :], best[:, t, :], LG[:, t, :]))
            nc.vector.tensor_tensor(ed[:, :], best[:, :, 1], best[:, :, 0], ALU.subtract).then_inc(d_ready, 1)
            ch.after(n)
            ch.step(nc.vector.tensor_copy(idxf[:, :, :], bidx[:, :, 0:2]))
            dve.wait_ge(weights, 32)
            for j in range(2):
                n = ch.mark(nc.vector.tensor_tensor(oh[:, j, :, :], bc(iota8[:, :].unsqueeze(1), [P, NT, NE]),
                                                    bc(idxf[:, :, j:j + 1], [P, NT, NE]), ALU.is_equal))
            ch.after(n)
            ch.step(nc.vector.tensor_tensor(both[:, :, :], oh[:, 0, :, :], oh[:, 1, :, :], ALU.add))
            for e in range(NE):
                n = ch.mark(nc.vector.tensor_tensor_scan(seen[:, :, e], k.ones[:, 0:NT], both[:, :, e], 0.0,
                                                         ALU.mult, ALU.add))
            ch.after(n)
            nc.vector.tensor_tensor(seen[:, :, :], seen[:, :, :], both[:, :, :], ALU.subtract).then_inc(m_ready, 1)
            dve.wait_ge(d_exp, 1)
            ch.step(nc.vector.tensor_scalar(es[:, :], ed[:, :], 1.0, None, ALU.add))
            ch.step(nc.vector.reciprocal(es[:, :], es[:, :]))
            dve.wait_ge(r_ready, 1)
            for j in range(2):
                n = ch.mark(nc.vector.tensor_tensor(pick[:, j, :, :], oh[:, j, :, :], psR[:, :, :], ALU.mult))
            ch.after(n)
            for j in range(2):
                n = ch.mark(nc.vector.tensor_reduce(rank[:, :, j], pick[:, j, :, :], AX.X, ALU.add))
            ch.after(n)
            ch.step(nc.vector.tensor_scalar(fits[:, :, :], rank[:, :, :], float(CAP), None, ALU.is_lt))
            ch.step(nc.vector.scalar_tensor_tensor(slot[:, :, :], idxf[:, :, :], float(CAP), rank[:, :, :], ALU.mult, ALU.add))
            ch.step(nc.vector.scalar_tensor_tensor(slot[:, :, :], slot[:, :, :], -float(SLOTS), fits[:, :, :], ALU.add, ALU.mult))
            ch.step(nc.vector.tensor_scalar(slot[:, :, :], slot[:, :, :], float(SLOTS), None, ALU.add))
            ch.step(nc.vector.tensor_copy(k.slots[:, :, :], slot[:, :, :]))
            rows.ready(dve, 1)
            with dve.Fori(0, NB // 2) as i:
                for x in range(2):
                    dve.wait_ge(free, i * 2 + x + 1)
                    pass_gate(k, dve)
                    n = i * (2 * TS) + x * TS
                    nc.vector.tensor_copy(sidx[:, x, :, :], k.slots[:, bass.ds(n, TS), :]).then_inc(row_ready, 1)
                    for u in range(TS):
                        m = i * (2 * TS) + (x * TS + u)
                        nc.vector.tensor_scalar(XN[:, x, u, :], k.HS[:, bass.ds(m, 1), :].rearrange("p a c -> p (a c)"),
                                                k.mean[:, bass.ds(m, 1)], k.rstd[:, bass.ds(m, 1)],
                                                ALU.subtract, ALU.mult).then_inc(row_ready, 1)
            n = ch.mark(nc.vector.tensor_tensor(k.prob[:, :, 0], es[:, :], fits[:, :, 0], ALU.mult))
            ch.step(nc.vector.tensor_tensor(ed[:, :], es[:, :], ed[:, :], ALU.mult))
            ch.mark(nc.vector.tensor_tensor(k.prob[:, :, 1], ed[:, :], fits[:, :, 1], ALU.mult))


def experts(k):
    nc, a = k.nc, k.a
    CH = 2 * P
    NCH = CAP // CH
    with ExitStack() as ctx:
        w1 = k.sb(ctx, "w1", [P, 2, KC, FE])
        w2 = k.sb(ctx, "w2", [P, 2, FE // P, D])
        lnw, lnb = k.sb(ctx, "e_w", [P, KC]), k.sb(ctx, "e_b", [P, KC])
        XE = k.sb(ctx, "XE", [P, 4, 2, D])
        XT = k.sb(ctx, "e_XT", [P, 2, KC, CH])
        HT = k.sb(ctx, "e_HT", [P, 2, FE // P, CH])
        YE = k.sb(ctx, "YE", [P, 2, 2, D])
        psX = k.ps(ctx, "e_psX", [P, KC, CH])
        psH = [[k.ps(ctx, f"e_psH{s}{h}", [P, 2, CH]) for h in range(2)] for s in range(2)]
        psY = [k.ps(ctx, f"e_psY{s}", [P, 2, D]) for s in range(2)]
        consts = k.sem(ctx, "e_consts")
        w_loaded = [k.sem(ctx, f"e_w_loaded{s}") for s in range(2)]
        x_loaded = [k.sem(ctx, f"e_x_loaded{s}") for s in range(2)]
        y_stored = [k.sem(ctx, f"e_y_stored{s}") for s in range(2)]
        x_ready, x_evac = k.sem(ctx, "e_x_ready"), k.sem(ctx, "e_x_evac")
        h_ready, h_done = k.sem(ctx, "e_h_ready"), k.sem(ctx, "e_h_done")
        y_ready, y_evac = k.sem(ctx, "e_y_ready"), k.sem(ctx, "e_y_evac")
        block = ctx.enter_context(nc.Block())
        N = 2 * NCH
        assert N % 2 == 0

        @block.sync
        def _(sp):
            sp.dma_start(lnw[:, :], a["ln2w"]).then_inc(consts, 16)
            sp.dma_start(lnb[:, :], a["ln2b"]).then_inc(consts, 16)
            with sp.Fori(0, NE // 2) as i:
                for s in range(2):
                    sp.wait_ge(y_ready, i * N + (s + 1) * NCH)
                    sp.dma_start(w1[:, s, :, :], a["w1"][bass.ds(i * 2 + s, 1), :, :].rearrange("a (k p) n -> p (a k) n", p=P)).then_inc(w_loaded[s], 16)
                    sp.dma_start(w2[:, s, :, :], a["w2"][bass.ds(i * 2 + s, 1), :, :].rearrange("a (k p) n -> p (a k) n", p=P)).then_inc(w_loaded[s], 16)
                    for c in range(s * NCH, (s + 1) * NCH):
                        sp.wait_ge(x_ready, i * N + c + 1)
                        sp.dma_start(XE[:, c % 2, :, :], k.xt_dram[bass.ds((i * N + c) * CH, CH), :].rearrange(
                            "(j p) n -> p j n", p=P)).then_inc(x_loaded[c % 2], 16)

        @block.tensor
        def _(pe):
            pe.sem_inc(y_ready, N)
            pe.sem_inc(x_ready, 2)

            def turn(i, c):
                pe.wait_ge(x_loaded[c % 2], i * (16 * N // 2) + 16 * (c // 2 + 1))
                pe.wait_ge(x_evac, (i * N + c) * 2 + 2)
                for j in range(2):
                    for kc in range(KC):
                        mm = pe.transpose(psX[:, kc, j * P:(j + 1) * P], XE[:, c % 2, j, kc * P:(kc + 1) * P], k.ident[:, :])
                mm.then_inc(x_ready, 1)

            def hidden(i, c):
                s = c // NCH
                if c % NCH == 0:
                    pe.wait_ge(w_loaded[s], i * 32 + 32)
                pe.wait_ge(x_evac, (i * N + c) * 2 + 4)
                for half in range(2):
                    pe.wait_ge(h_done, (i * N + c) * 2 + half + 1)
                    for m in range(2):
                        for kc in range(KC):
                            f = (half * 2 + m) * P
                            mm = pe.matmul(psH[c % 2][half][:, m, :], w1[:, s, kc, f:f + P], XT[:, c % 2, kc, :],
                                           start=(m == 0 and kc == 0), stop=(m == 1 and kc == KC - 1), skip_group_check=True)
                    mm.then_inc(h_ready, 1)

            def rows(i, c):
                s = c // NCH
                pe.wait_ge(h_done, (i * N + c) * 2 + 2 + 4)
                pe.wait_ge(y_evac, i * N + c + 1)
                for j in range(2):
                    for m in range(FE // P):
                        mm = pe.matmul(psY[c % 2][:, j, :], HT[:, c % 2, m, j * P:(j + 1) * P], w2[:, s, m, :],
                                       start=(j == 0 and m == 0), stop=(j == 1 and m == FE // P - 1), skip_group_check=True)
                mm.then_inc(y_ready, 1)

            with pe.Fori(0, NE // 2) as i:
                turn(i, 0)
                for c in range(N):
                    if c + 1 < N:
                        turn(i, c + 1)
                    hidden(i, c)
                    if c >= 1:
                        rows(i, c - 1)
                rows(i, N - 1)

        @block.scalar
        def _(act):
            act.sem_inc(h_done, 4)
            act.sem_inc(y_stored[0], 16)
            act.sem_inc(y_stored[1], 16)

            def store(i, c):
                act.wait_ge(y_evac, i * N + c + 1 + 2)
                act.dma_start(k.y_dram[bass.ds((i * N + c) * CH, CH), :].rearrange("(j p) n -> p j n", p=P),
                              YE[:, c % 2, :, :]).then_inc(y_stored[c % 2], 16)

            with act.Fori(0, NE // 2) as i:
                for c in range(N):
                    act.wait_ge(y_ready, i * N + c + 1 + N - 2)
                    for half in range(2):
                        act.wait_ge(h_ready, (i * N + c) * 2 + half + 1)
                        nc.scalar.activation(HT[:, c % 2, 2 * half:2 * half + 2, :], psH[c % 2][half][:, :, :],
                                             ACT.Gelu_apprx_tanh).then_inc(h_done, 1)
                    if c >= 2:
                        store(i, c - 2)
                store(i, N - 2)
                store(i, N - 1)
            for s in range(2):
                act.wait_ge(y_stored[s], 16 + 16 * (NE // 2) * (N // 2))

        @block.vector
        def _(dve):
            dve.sem_inc(x_evac, 2)
            dve.sem_inc(y_evac, 2)
            dve.wait_ge(consts, 32)

            def evac_x(i, c):
                dve.wait_ge(x_ready, i * N + c + 1 + 2)
                for kc in range(KC):
                    nc.vector.tensor_scalar(XT[:, c % 2, kc, :], psX[:, kc, :], lnw[:, kc:kc + 1], lnb[:, kc:kc + 1],
                                            ALU.mult, ALU.add).then_inc(x_evac, 1)

            def evac_y(i, c):
                dve.wait_ge(y_ready, i * N + c + 1 + N)
                dve.wait_ge(y_stored[c % 2], i * (16 * N // 2) + 16 * (c // 2 + 1))
                nc.vector.tensor_copy(YE[:, c % 2, :, :], psY[c % 2][:, :, :]).then_inc(y_evac, 1)

            with dve.Fori(0, NE // 2) as i:
                evac_x(i, 0)
                for c in range(N):
                    if c >= 2:
                        evac_y(i, c - 2)
                    if c + 1 < N:
                        evac_x(i, c + 1)
                evac_y(i, N - 2)
                evac_y(i, N - 1)


class RetentionWeights:

    def __init__(self, k, ctx):
        self.wqkv = k.sb(ctx, "n_wqkv", [P, KC, 3 * D])
        self.wo = k.sb(ctx, "n_wo", [P, KC, D])
        self.gam, self.bet = k.sb(ctx, "n_gam", [P, KC]), k.sb(ctx, "n_bet", [P, KC])
        self.rotC, self.rotS = k.sb(ctx, "rotC", [P, TS, 2 * D]), k.sb(ctx, "rotS", [P, TS, 2 * D])
        self.causal = k.sb(ctx, "causal", [P, P])
        self.carry = k.sb(ctx, "carry", [P, KC, P])
        self.group = k.sb(ctx, "group", [P, P])
        self.loaded = k.sem(ctx, "n_weights")
        self.a = k.a

    def load(self, sp):
        a = self.a
        for dst, src in ((self.wqkv[:, :, :], a["wqkv1"].rearrange("(k p) n -> p k n", p=P)),
                         (self.rotC[:, :, :], a["rotC"]), (self.rotS[:, :, :], a["rotS"]),
                         (self.causal[:, :], a["causal"]), (self.carry[:, :, :], a["carry"]),
                         (self.wo[:, :, :], a["wo1"].rearrange("(k p) n -> p k n", p=P)),
                         (self.gam[:, :], a["gamma"]), (self.bet[:, :], a["beta"]), (self.group[:, :], a["group"])):
            sp.dma_start(dst, src).then_inc(self.loaded, 16)


def load_ffn_weights(k, sp):
    n1 = KC * 2 * FF
    sp.dma_start(k.ffn_raw[:, 0:n1].rearrange("p (k n) -> p k n", k=KC),
                 k.a["wgu"].rearrange("(k p) n -> p k n", p=P)).then_inc(k.ffn_loaded, 16)
    sp.dma_start(k.ffn_raw[:, n1:].rearrange("p (m n) -> p m n", m=FF // P),
                 k.a["wd"].rearrange("(m p) n -> p m n", p=P)).then_inc(k.ffn_loaded, 16)


def retention(k, w):
    nc, a = k.nc, k.a
    with ExitStack() as ctx:
        wqkv, wo, gam, bet = w.wqkv, w.wo, w.gam, w.bet
        rotC, rotS, causal, carry, group = w.rotC, w.rotS, w.causal, w.carry, w.group
        weights = w.loaded
        cidx = k.sb(ctx, "cidx", [P, 2, 2], U32)
        YG = k.sb(ctx, "YG", [P, 2, 2, D])
        bst = k.sb(ctx, "n_bst", [P, 2, 6])
        stat = k.sb(ctx, "n_stat", [P, 2, 2])
        std, rstd = k.sb(ctx, "n_std", [P, 2, 1]), k.sb(ctx, "n_rstd", [P, 2, 1])
        XN = k.sb(ctx, "n_XN", [P, 2, D])
        XT = k.sb(ctx, "n_XT", [P, KC, P])
        m1, m2 = k.sb(ctx, "rot1", [P, 2 * D]), k.sb(ctx, "rot2", [P, 2 * D])
        Qr = k.sb(ctx, "Qr", [P, D])
        Kr = k.sb(ctx, "Kr", [P, 2, D])
        Kpar = [k.sb(ctx, f"Kpar{par}", [P, KC, P]) for par in range(2)]
        V = k.sb(ctx, "n_V", [P, 2, D])
        Vpar = [k.sb(ctx, f"Vpar{par}", [P, 2, D]) for par in range(2)]
        KT = k.sb(ctx, "n_KT", [P, 2, KC, P])
        QT = k.sb(ctx, "n_QT", [P, KC, P])
        ST = k.sb(ctx, "n_ST", [P, 4, KC, 2, P])
        state = k.sb(ctx, "state", [P, KC, P])
        snew = k.sb(ctx, "snew", [P, KC, P])
        wmean = k.sb(ctx, "wmean", [P, KC, H1])
        eps = k.sb(ctx, "n_eps", [P, 1])
        R = k.sb(ctx, "n_R", [P, 2, KC, P])
        sq = k.sb(ctx, "n_sq", [P, KC, P])
        root = k.sb(ctx, "n_root", [P, KC, P])
        inv = k.sb(ctx, "n_inv", [P, KC, P])
        RN = k.sb(ctx, "n_RN", [P, KC, P])
        RT = k.sb(ctx, "n_RT", [P, KC, P])
        psT = k.ps(ctx, "n_psT", [P, 2, KC, P])
        psQK = k.ps(ctx, "n_psQK", [P, 2 * D])
        psV = k.ps(ctx, "n_psV", [P, D])
        psK = k.ps(ctx, "n_psK", [P, 2, KC, P])
        psX = k.ps(ctx, "n_psX", [P, 2, KC, P])
        psS = [k.ps(ctx, f"n_psS{s}", [P, KC, 2, P]) for s in range(2)]
        psR = k.ps(ctx, "n_psR", [P, KC, P])
        zeroed = k.sem(ctx, "n_zeroed")
        xn_ready, xt_ready, xt_evac = k.sem(ctx, "n_xn_ready"), k.sem(ctx, "n_xt_ready"), k.sem(ctx, "n_xt_evac")
        sq_ready, m_ready, m_root = k.sem(ctx, "n_sq_ready"), k.sem(ctx, "n_m_ready"), k.sem(ctx, "n_m_root")
        rn_ready, rt_ready = k.sem(ctx, "n_rn_ready"), k.sem(ctx, "n_rt_ready")
        qk_ready, v_ready, v_evac = k.sem(ctx, "n_qk_ready"), k.sem(ctx, "n_v_ready"), k.sem(ctx, "n_v_evac")
        rot_done, rot_ready = k.sem(ctx, "n_rot_done"), k.sem(ctx, "n_rot_ready")
        x_ready, x_evac = k.sem(ctx, "n_x_ready"), k.sem(ctx, "n_x_evac")
        s_ready, s_masked = k.sem(ctx, "n_s_ready"), k.sem(ctx, "n_s_masked")
        r_ready, r_read = k.sem(ctx, "n_r_ready"), k.sem(ctx, "n_r_read")
        st_ready, st_done = k.sem(ctx, "n_st_ready"), k.sem(ctx, "n_st_done")
        z_ready, z_added = k.sem(ctx, "n_z_ready"), k.sem(ctx, "n_z_added")
        centre_step, centred = k.sem(ctx, "n_centre_step"), k.sem(ctx, "n_centred")
        arrive_step, inverse_step = k.sem(ctx, "n_arrive_step"), k.sem(ctx, "n_inverse_step")
        state_step, add_step = k.sem(ctx, "n_state_step"), k.sem(ctx, "n_add_step")
        inverse_done = k.sem(ctx, "n_inverse_done")
        i_ready, rows_used = k.sem(ctx, "n_i_ready"), k.sem(ctx, "n_rows_used")
        got = [k.sem(ctx, f"n_got{x}") for x in range(2)]
        stat_ready, std_ready = k.sem(ctx, "n_stat_ready"), k.sem(ctx, "n_std_ready")
        block = ctx.enter_context(nc.Block())

        @block.sync
        def _(sp):
            load_ffn_weights(k, sp)

        def stream(eng, step):
            def peeled(g):
                step(g // TS, g % TS, lambda d: 0 <= g + d < NT)
            for g in range(-2, TS):
                peeled(g)
            with eng.Fori(1, NB - 1) as i:
                for s in range(TS):
                    step(i, s, lambda d: True)
            for g in range(NT - TS, NT + 2):
                peeled(g)

        def states(i, s):
            return i * (TS - 1) + max(s - 1, 0)

        @block.tensor
        def _(pe):
            pe.sem_inc(x_ready, 1)
            pe.wait_ge(weights, 16 * 9)
            pe.wait_ge(centred, 1)

            def turn_x(g, s):
                pe.wait_ge(xn_ready, g + 1 + 2)
                pe.wait_ge(xt_evac, g + 1)
                pe.wait_ge(st_done, g + 1)
                for c in range(KC):
                    mm = pe.transpose(psT[:, 0, c, :], XN[:, s % 2, c * P:(c + 1) * P], k.ident[:, :])
                mm.then_inc(xt_ready, 1)

            def project(g, s):
                pe.wait_ge(xt_evac, g + 2)
                pe.wait_ge(rot_done, g + 1)
                for c in range(KC):
                    mm = pe.matmul(psQK[:, :], XT[:, c, :], wqkv[:, c, 0:2 * D], start=(c == 0), stop=(c == KC - 1))
                mm.then_inc(qk_ready, 1)
                pe.wait_ge(v_evac, g + 1)
                pe.wait_ge(z_added, g + 1)
                for c in range(KC):
                    mm = pe.matmul(psV[:, :], XT[:, c, :], wqkv[:, c, 2 * D:], start=(c == 0), stop=(c == KC - 1))
                mm.then_inc(v_ready, 1)

            def turn_qk(g, s):
                pe.wait_ge(rot_ready, g + 2)
                pe.wait_ge(x_evac, g * 2 + 2)
                pe.wait_ge(m_root, g + 1)
                for par in range(2):
                    for c in range(KC):
                        pe.transpose(psK[:, par, c, :], Kpar[par][:, c, :], k.ident[:, :])
                for c in range(KC):
                    mm = pe.transpose(psX[:, 0, c, :], Qr[:, c * P:(c + 1) * P], k.ident[:, :])
                mm.then_inc(x_ready, 1)

            def scores(g, half):
                if half == 0:
                    pe.wait_ge(x_evac, g * 2 + 4)
                pe.wait_ge(s_masked, g * 4 + 2 * half + 2)
                for c in range(KC):
                    for par in range(2):
                        for b in range(2):
                            r = 32 * (2 * half + b)
                            mm = pe.matmul(psS[b][:, c, par, :], KT[r:r + 32, par, c, :], QT[r:r + 32, c, :],
                                           start=(c == 0 and par == 0), stop=(c == 1 and par == 1), skip_group_check=True)
                mm.then_inc(s_ready, 1)

            def from_state(g):
                pe.wait_ge(r_read, g + 1)
                pe.wait_ge(st_done, g + 2)
                for c in range(KC):
                    pe.matmul(psR[:, c, :], state[:, c, :], QT[:, c, :], start=(c == 0), stop=False,
                              skip_group_check=True)

            def from_chunk(g, s, half):
                u = (s - 1) % TS
                pe.wait_ge(s_masked, g * 4 + 2 * half + 2 + 2)
                for r in (2 * half, 2 * half + 1):
                    for c in range(KC):
                        for par in range(2):
                            h = (c * 4 + r) * 2
                            mm = pe.matmul(psR[32 * r:32 * r + 32, c, :], Vpar[par][:, u % 2, h * DH:(h + 2) * DH],
                                           ST[:, r, c, par, :], start=False, stop=(r == 3 and c == 1 and par == 1),
                                           skip_group_check=True)
                if half == 1:
                    mm.then_inc(r_ready, 1)

            def to_state(s):
                u = (s - 1) % TS
                for c in range(KC):
                    mm = pe.matmul(psT[:, 1, c, :], Kr[:, u % 2, c * P:(c + 1) * P], V[:, u % 2, c * P:(c + 1) * P],
                                   start=(c == 0), stop=(c == KC - 1), skip_group_check=True)
                mm.then_inc(st_ready, 1)

            def variances(g):
                pe.wait_ge(sq_ready, g + 1)
                pe.matmul(psX[:, 1, :, :], group[:, :], sq[:, :, :], start=True, stop=True).then_inc(m_ready, 1)

            def out(g, entering):
                pe.wait_ge(rt_ready, g + 1 + 1)
                pe.wait_ge(v_evac, g + 4 if entering else NT + 1)
                pe.wait_ge(z_added, g + 3)
                for c in range(KC):
                    mm = pe.matmul(psV[:, :], RT[:, c, :], wo[:, c, :], start=(c == 0), stop=(c == KC - 1))
                mm.then_inc(z_ready, 1)

            def step(i, s, has):
                g, entering, attending, leaving = i * TS + s, has(0), has(-1), has(-2)
                if attending:
                    scores(g - 1, 0)
                if leaving:
                    variances(g - 2)
                if entering:
                    turn_x(g, s)
                if attending:
                    from_state(g - 1)
                if entering:
                    project(g, s)
                if attending:
                    scores(g - 1, 1)
                    from_chunk(g - 1, s, 0)
                    from_chunk(g - 1, s, 1)
                if entering:
                    turn_qk(g, s)
                if leaving:
                    out(g - 2, entering)
                if attending and s != 0:
                    to_state(s)

            stream(pe, step)

        @block.scalar
        def _(act):
            act.sem_inc(xt_evac, 1)
            act.sem_inc(std_ready, 2)
            act.sem_inc(m_root, 2)
            act.sem_inc(r_read, 1)
            act.sem_inc(rt_ready, 1)
            act.sem_inc(v_evac, 1)
            act.sem_inc(x_evac, 2)
            act.wait_ge(weights, 16 * 9)
            act.wait_ge(zeroed, 5)

            def deviation(g, x):
                act.wait_ge(stat_ready, g + 1)
                act.wait_ge(xn_ready, g + 1)
                nc.scalar.activation(std[:, x, :], stat[:, x, 1:2], ACT.Sqrt, bias=eps[:, 0:1]).then_inc(std_ready, 1)

            def x_turned(g):
                act.wait_ge(xt_ready, g + 1)
                nc.scalar.copy(XT[:, :, :], psT[:, 0, :, :]).then_inc(xt_evac, 1)

            def values(g, s):
                act.wait_ge(v_ready, g + 1)
                nc.scalar.copy(V[:, s % 2, :], psV[:, :])
                for par in range(2):
                    def side(x):
                        return x.rearrange("p (g h d) -> p g h d", h=2, d=DH)[:, :, par, :]
                    ins = nc.scalar.copy(side(Vpar[par][:, s % 2, :]), side(psV[:, :]))
                ins.then_inc(v_evac, 1)

            def result_read(g, s):
                act.wait_ge(r_ready, g + 1)
                act.wait_ge(rn_ready, g + 1)
                nc.scalar.copy(R[:, (s - 1) % 2, :, :], psR[:, :, :]).then_inc(r_read, 1)

            def root_of(g):
                act.wait_ge(m_ready, g + 1)
                act.wait_ge(rn_ready, g + 2)
                nc.scalar.activation(root[:, :, :], psX[:, 1, :, :], ACT.Sqrt, bias=eps[:, 0:1]).then_inc(m_root, 1)

            def scaled(g):
                act.wait_ge(rn_ready, g + 1 + 2)
                for c in range(KC):
                    ins = nc.scalar.activation(RT[:, c, :], RN[:, c, :], ACT.Identity, bias=bet[:, c:c + 1],
                                               scale=gam[:, c:c + 1])
                ins.then_inc(rt_ready, 1)

            def qk_turned(g):
                act.wait_ge(x_ready, g + 2)
                nc.scalar.copy(KT[:, :, :, :], psK[:, :, :, :]).then_inc(x_evac, 1)
                nc.scalar.copy(QT[:, :, :], psX[:, 0, :, :]).then_inc(x_evac, 1)

            def step(i, s, has):
                g, entering, attending, leaving = i * TS + s, has(0), has(-1), has(-2)
                if leaving:
                    root_of(g - 2)
                if entering:
                    x_turned(g)
                    values(g, s)
                if leaving:
                    scaled(g - 2)
                if attending:
                    result_read(g - 1, s)
                if entering:
                    qk_turned(g)
                if has(1):
                    deviation(g + 1, (s + 1) % 2)

            stream(act, step)

        @block.gpsimd
        def _(pool):
            pool.sem_inc(rot_ready, 1)
            for par in range(2):
                nc.gpsimd.memset(Kpar[par][:, :, :], 0.0).then_inc(zeroed, 1)
                nc.gpsimd.memset(Vpar[par][:, :, :], 0.0).then_inc(zeroed, 1)
            nc.gpsimd.memset(eps[:, :], EPS).then_inc(zeroed, 1)
            pool.wait_ge(zeroed, 5)

            def gathered(g, x, i):
                pool.wait_ge(rows_used, g + 1)
                nc.gpsimd.tensor_copy(cidx[:, x, :], k.slots[:, bass.ds(g, 1), :].rearrange("p a j -> p (a j)")).then_inc(i_ready, 1)
                pool.wait_ge(i_ready, g + 1)
                pass_gate(k, pool)
                for j in range(2):
                    pool.indirect_dma_start(YG[:, x, j, :], None, k.y_dram[:, :],
                                            bass.IndirectOffsetOnAxis(ap=cidx[:, x, j:j + 1], axis=0)).then_inc(got[x], 16)

            def squared(g, s):
                pool.wait_ge(r_read, g + 2)
                pool.wait_ge(m_ready, g) if not isinstance(g, int) or g else None
                x = R[:, (s - 1) % 2, :, :]
                nc.gpsimd.tensor_tensor(sq[:, :, :], x, x, ALU.mult).then_inc(sq_ready, 1)

            def rotated(g, s):
                pool.wait_ge(rot_done, g + 2)
                pool.wait_ge(x_ready, g + 1)
                nc.gpsimd.tensor_tensor(Qr[:, :], m1[:, 0:D], m2[:, 0:D], ALU.add)
                nc.gpsimd.tensor_tensor(Kr[:, s % 2, :], m1[:, D:], m2[:, D:], ALU.add)
                for par in range(2):
                    def side(x):
                        return x.rearrange("p (g h d) -> p g h d", h=2, d=DH)[:, :, par, :]
                    dst = Kpar[par][:, :, :].rearrange("p c (g h d) -> p (c g) h d", h=2, d=DH)[:, :, par, :]
                    ins = nc.gpsimd.tensor_tensor(dst, side(m1[:, D:]), side(m2[:, D:]), ALU.add)
                ins.then_inc(rot_ready, 1)

            def step(i, s, has):
                g, entering, attending, leaving = i * TS + s, has(0), has(-1), has(-2)
                if has(2):
                    gathered(g + 2, s % 2, i)
                if entering:
                    rotated(g, s)
                if attending:
                    squared(g - 1, s)

            stream(pool, step)

        @block.vector
        def _(dve):
            dve.sem_inc(rot_done, 1)
            dve.sem_inc(s_masked, 2)
            dve.sem_inc(st_done, 1)
            nc.vector.memset(state[:, :, :], 0.0).then_inc(st_done, 1)
            dve.sem_inc(rn_ready, 2)
            dve.sem_inc(xn_ready, 2)
            dve.sem_inc(rows_used, 2)
            dve.sem_inc(z_added, 3)
            dve.wait_ge(weights, 16 * 9)

            wv = wqkv[:, :, 2 * D:].rearrange("p c (h d) -> p c h d", d=DH)
            first = Chain(dve, centre_step)
            for c in range(KC):
                n = first.mark(nc.vector.tensor_reduce(wmean[:, c, :], wv[:, c, :, :], AX.X, ALU.add))
            first.after(n)
            first.step(nc.vector.tensor_scalar(wmean[:, :, :], wmean[:, :, :], 1.0 / DH, None, ALU.mult))
            for c in range(KC):
                n = first.mark(nc.vector.tensor_tensor(wv[:, c, :, :], wv[:, c, :, :],
                                                       bc(wmean[:, c, :].unsqueeze(2), [P, H1, DH]), ALU.subtract))
            first.after(n)
            dve.sem_inc(centred, 1)

            def arrived(g, x, pair):
                ch = Chain(dve, arrive_step, g * 3)
                X = k.X[:, bass.ds(g, 1), :].rearrange("p a c -> p (a c)")
                h = k.HS[:, bass.ds(g, 1), :].rearrange("p a c -> p (a c)")
                pr = k.prob[:, bass.ds(g, 1), :].rearrange("p a j -> p (a j)")
                ch.step(nc.vector.tensor_tensor(X, X, h, ALU.add))
                dve.wait_ge(got[x], pair * 32 + 32)
                ch.step(nc.vector.scalar_tensor_tensor(X, YG[:, x, 0, :], pr[:, 0:1], X, ALU.mult, ALU.add))
                nc.vector.scalar_tensor_tensor(X, YG[:, x, 1, :], pr[:, 1:2], X, ALU.mult, ALU.add).then_inc(rows_used, 1)
                dve.wait_ge(rows_used, g + 1 + 2)
                pass_gate(k, dve)
                ch.step(nc.vector.bn_stats(bst[:, x, :], X))
                dve.wait_ge(std_ready, g + 1)
                pass_gate(k, dve)
                nc.vector.bn_aggr(stat[:, x, :], bst[:, x:x + 1, :]).then_inc(stat_ready, 1)

            def norm(g, x):
                dve.wait_ge(std_ready, g + 1 + 2)
                nc.vector.reciprocal(rstd[:, x, :], std[:, x, :]).then_inc(inverse_step, 1)
                dve.wait_ge(inverse_step, g + 1)
                nc.vector.tensor_scalar(XN[:, x, :], k.X[:, bass.ds(g, 1), :], stat[:, x, 0:1], rstd[:, x, :],
                                        ALU.subtract, ALU.mult).then_inc(xn_ready, 1)

            def rotate(g, s):
                dve.wait_ge(qk_ready, g + 1)
                dve.wait_ge(rot_ready, g + 1)
                nc.vector.tensor_tensor(m1[:, :], psQK[:, :], rotC[:, s, :], ALU.mult)
                for x in range(2):
                    def lane(y, z):
                        return y.rearrange("p (n two) -> p n two", two=2)[:, :, z]
                    ins = nc.vector.tensor_tensor(lane(m2[:, :], x), lane(psQK[:, :], 1 - x), lane(rotS[:, s, :], x), ALU.mult)
                ins.then_inc(rot_done, 1)

            def mask(g, half):
                dve.wait_ge(s_ready, g * 2 + half + 1)
                for r in (2 * half, 2 * half + 1):
                    nc.vector.tensor_tensor(ST[:, r, :, :, :].rearrange("p c a t -> p (c a) t"),
                                            psS[r % 2][:, :, :, :].rearrange("p c a t -> p (c a) t"),
                                            bc(causal[:, :].unsqueeze(1), [P, 4, P]), ALU.mult).then_inc(s_masked, 1)

            def carry_on(g, i, s, old):
                ch = Chain(dve, state_step, i * (TS - 2) + max(s - 2, 0))
                if s == 0:
                    dve.wait_ge(r_ready, g + 1)
                    nc.vector.memset(state[:, :, :], 0.0).then_inc(st_done, 1)
                    return
                dve.wait_ge(st_ready, old + 1)
                new = psT[:, 1, :, :]
                if (s - 1) % TS > 0:
                    ch.step(nc.vector.tensor_tensor(snew[:, :, :], psT[:, 1, :, :], state[:, :, :], ALU.add))
                    new = snew[:, :, :]
                nc.vector.tensor_tensor(state[:, :, :], new, carry[:, :, :], ALU.mult).then_inc(st_done, 1)

            def result(g, s):
                dve.wait_ge(m_root, g + 1 + 2)
                nc.vector.reciprocal(inv[:, :, :], root[:, :, :]).then_inc(inverse_done, 1)
                dve.wait_ge(inverse_done, g + 1)
                dve.wait_ge(rt_ready, g + 1)
                nc.vector.tensor_tensor(RN[:, :, :], R[:, (s - 2) % 2, :, :], inv[:, :, :], ALU.mult).then_inc(rn_ready, 1)

            def add(g):
                ch = Chain(dve, add_step, g)
                dve.wait_ge(z_ready, g + 1)
                x = k.X[:, bass.ds(g, 1), :].rearrange("p a c -> p (a c)")
                bst = k.BST[:, bass.ds(g, 1), :].rearrange("p a c -> p (a c)")
                ch.step(nc.vector.tensor_tensor(x, x, psV[:, :], ALU.add))
                pass_gate(k, dve)
                nc.vector.bn_stats(bst, x).then_inc(z_added, 1)

            def step(i, s, has):
                g, entering, attending, leaving = i * TS + s, has(0), has(-1), has(-2)
                if attending:
                    mask(g - 1, 0)
                if leaving:
                    result(g - 2, s)
                if entering:
                    rotate(g, s)
                if attending:
                    mask(g - 1, 1)
                if has(1):
                    arrived(g + 1, (s + 1) % 2, i * 2 + (s + 1) // 2)
                if attending:
                    carry_on(g - 1, i, s, states(i, s))
                if has(1):
                    norm(g + 1, (s + 1) % 2)
                if leaving:
                    add(g - 2)

            stream(dve, step)


def swiglu(k):
    nc, a = k.nc, k.a
    M = FF // P
    with ExitStack() as ctx:
        wgu = k.sb(ctx, "wgu", [P, KC, 2 * FF])
        wd = k.sb(ctx, "wd", [P, M, D])
        XN = k.sb(ctx, "f_XN", [P, TS, D])
        XT = k.sb(ctx, "f_XT", [P, KC, T])
        SG = k.sb(ctx, "f_SG", [P, 2, T])
        HT = k.sb(ctx, "f_HT", [P, M, T])
        psT = [k.ps(ctx, f"f_psT{c}", [P, T]) for c in range(KC)]
        psG = [k.ps(ctx, f"f_psG{s}", [P, T]) for s in range(2)]
        psU = [k.ps(ctx, f"f_psU{s}", [P, T]) for s in range(2)]
        psY = [k.ps(ctx, f"f_psY{s}", [P, D]) for s in range(2)]
        casts = k.sem(ctx, "f_casts")
        xn_ready, t_ready, t_evac = k.sem(ctx, "f_xn_ready"), k.sem(ctx, "f_t_ready"), k.sem(ctx, "f_t_evac")
        g_ready, g_done, u_done = k.sem(ctx, "f_g_ready"), k.sem(ctx, "f_g_done"), k.sem(ctx, "f_u_done")
        y_ready, y_added = k.sem(ctx, "f_y_ready"), k.sem(ctx, "f_y_added")
        rows = RowStats(k, ctx)
        n1 = KC * 2 * FF
        block = ctx.enter_context(nc.Block())

        @block.tensor
        def _(pe):
            pe.sem_inc(t_ready, 1)
            pe.sem_inc(y_ready, 4)
            def turn(i):
                pe.wait_ge(t_evac, i * 2 + 2)
                for u in range(TS):
                    pe.wait_ge(xn_ready, i * TS + u + 1)
                    for c in range(KC):
                        mm = pe.transpose(psT[c][:, u * P:(u + 1) * P], XN[:, u, c * P:(c + 1) * P], k.ident[:, :])
                mm.then_inc(t_ready, 1)

            def gate_up(i):
                pe.wait_ge(casts, 1)
                pe.wait_ge(t_evac, i * 2 + 4)
                for m in range(M):
                    pe.wait_ge(g_done, i * M + m + 1)
                    for c in range(KC):
                        mm = pe.matmul(psG[m % 2][:, :], wgu[:, c, m * P:(m + 1) * P], XT[:, c, :], start=(c == 0), stop=(c == KC - 1))
                    mm.then_inc(g_ready, 1)
                    pe.wait_ge(u_done, i * M + m + 1)
                    for c in range(KC):
                        mm = pe.matmul(psU[m % 2][:, :], wgu[:, c, FF + m * P:FF + (m + 1) * P], XT[:, c, :], start=(c == 0), stop=(c == KC - 1))
                    mm.then_inc(g_ready, 1)

            def down(i):
                pe.wait_ge(casts, 2)
                pe.wait_ge(u_done, i * M + M + 2)
                for u in range(TS):
                    pe.wait_ge(y_added, i * TS + u + 1)
                    for m in range(M):
                        mm = pe.matmul(psY[u % 2][:, :], HT[:, m, u * P:(u + 1) * P], wd[:, m, :], start=(m == 0), stop=(m == M - 1))
                    mm.then_inc(y_ready, 1)

            turn(0)
            with pe.Fori(1, NB) as i:
                gate_up(i - 1)
                turn(i)
                down(i - 1)
            gate_up(NB - 1)
            down(NB - 1)

        @block.scalar
        def _(act):
            act.sem_inc(t_evac, 2)
            act.sem_inc(g_done, 2)

            def turned(i):
                act.wait_ge(t_ready, i + 2)
                for c in range(KC):
                    nc.scalar.copy(XT[:, c, :], psT[c][:, :]).then_inc(t_evac, 1)

            def gates(i):
                for m in range(M):
                    act.wait_ge(g_ready, (i * M + m) * 2 + 1)
                    act.wait_ge(u_done, i * M + m + 1)
                    nc.scalar.activation(SG[:, m % 2, :], psG[m % 2][:, :], ACT.Silu, scale=QSCALE).then_inc(g_done, 1)

            turned(0)
            with act.Fori(1, NB) as i:
                gates(i - 1)
                turned(i)
            gates(NB - 1)

        @block.sync
        def _(sp):
            with sp.Fori(0, NB) as i:
                sp.wait_ge(y_added, i * TS + TS + 2)
                sp.dma_start(k.out[bass.ds(i * T, T), :].rearrange("(j p) c -> p j c", p=P),
                             k.X[:, bass.ds(i * TS, TS), :]).then_inc(k.stored, 16)
            sp.wait_ge(k.stored, 16 * NB)

        @block.vector
        def _(dve):
            dve.sem_inc(u_done, 2)
            dve.sem_inc(y_added, 2)
            rows.sums(dve)
            dve.wait_ge(k.ffn_loaded, 32)
            nc.vector.tensor_copy(wgu[:, :, :].rearrange("p k n -> p (k n)"), k.ffn_raw[:, 0:n1]).then_inc(casts, 1)

            def normed(i):
                dve.wait_ge(t_ready, i + 1)
                for u in range(TS):
                    normalise(k, XN[:, u, :], i * TS + u).then_inc(xn_ready, 1)

            def hidden(i):
                for m in range(M):
                    dve.wait_ge(g_ready, (i * M + m) * 2 + 2)
                    dve.wait_ge(g_done, i * M + m + 1 + 2)
                    dve.wait_ge(y_ready, i * TS + TS)
                    nc.vector.scalar_tensor_tensor(HT[:, m, :], psU[m % 2][:, :], QSCALE, SG[:, m % 2, :],
                                                   ALU.mult, ALU.mult).then_inc(u_done, 1)

            def add(i):
                for u in range(TS):
                    dve.wait_ge(y_ready, i * TS + u + 1 + 4)
                    x = k.X[:, bass.ds(i * TS + u, 1), :].rearrange("p a c -> p (a c)")
                    nc.vector.scalar_tensor_tensor(x, psY[u % 2][:, :], QSCALE, x, ALU.mult, ALU.add).then_inc(y_added, 1)

            rows.ready(dve, 0)
            normed(0)
            nc.vector.tensor_copy(wd[:, :, :].rearrange("p m n -> p (m n)"), k.ffn_raw[:, n1:]).then_inc(casts, 1)
            rows.ready(dve, 1)
            with dve.Fori(1, NB) as i:
                normed(i)
                hidden(i - 1)
                add(i - 1)
            hidden(NB - 1)
            add(NB - 1)

        @block.gpsimd
        def _(pool):
            rows.roots(pool)


def lay_out(x):
    f = np.ascontiguousarray
    c = {}
    c["x"] = f(x["L0_attn_X"]).reshape(NB * T, D)
    c["wg"] = f(x["L0_attn_w_G"].reshape(H0 * E0, D).T)
    c["bg"] = f(x["L0_attn_b_G"].reshape(1, H0 * E0))
    c["wkv"] = f(np.concatenate([x["L0_attn_w_K"], x["L0_attn_w_V"]], axis=1).reshape(H0 * P, D).T)
    c["wq"] = f(x["L0_attn_w_Q"].reshape(H0 * DK, D).T)
    c["wo"] = f(x["L0_attn_w_O"].reshape(2, 4, DK, D).transpose(1, 0, 2, 3)).reshape(H0 * DK, D)
    c["ikv"] = f(np.concatenate([x["L0_attn_init_K_rec"], x["L0_attn_init_V_rec"]], axis=2).transpose(2, 0, 1))
    c["ident"] = np.eye(P, dtype=np.float32)
    q, s = np.arange(32)[:, None], np.arange(64)[None, :]
    seen = (s > q) & (s <= q + L0)
    c["mask"] = f(np.repeat(np.where(seen, 0.0, NEG).astype(np.float32), E0, axis=1))
    c["sel"] = f(np.tile(np.eye(32, dtype=np.float32), (1, 4)))
    col = lambda v: f(v.reshape(KC, P).T)
    c["qkv1"] = f(x["L0_ffn_qkv_weight"].T)
    c["proj"] = f(x["L0_ffn_proj_weight"].T)
    c["router"] = f(x["L0_ffn_router_weight"])
    c["ln1w"], c["ln1b"] = col(x["L0_ffn_ln1_weight"]), col(x["L0_ffn_ln1_bias"])
    c["ln2w"], c["ln2b"] = col(x["L0_ffn_ln2_weight"]), col(x["L0_ffn_ln2_bias"])
    c["w1"], c["w2"] = f(x["L0_ffn_moe_w1"]), f(x["L0_ffn_moe_w2"])
    c["before"] = np.triu(np.ones((P, P), np.float32), 1)
    c["iota8"] = f(np.tile(np.arange(NE, dtype=np.float32), (P, 1)))
    flat = lambda w: w.reshape(D, D)
    c["wqkv1"] = f(np.concatenate([flat(x["L1_attn_WQ"]), flat(x["L1_attn_WK"]), flat(x["L1_attn_WV"])]).T)
    c["wo1"] = f(x["L1_attn_WO"])
    c["gamma"], c["beta"] = col(x["L1_attn_gamma"]), col(x["L1_attn_beta"])
    c["rotC"], c["rotS"], c["carry"] = decay_tables()
    c["group"] = np.kron(np.eye(P // DH), np.full((DH, DH), 1.0 / DH)).astype(np.float32)
    c["causal"] = np.triu(np.ones((P, P), np.float32))
    c["wgu"] = f(np.concatenate([x["L1_ffn_w_gate"], x["L1_ffn_w_up"]]).T)
    c["wd"] = f(x["L1_ffn_w_down"].T)
    return c


def decay_tables():
    freq = (10.0 ** (-4.0 * (np.arange(0, DH, 2, dtype=np.float32) / np.float32(DH)))).astype(np.float32)
    angle = (np.arange(T, dtype=np.float32)[:, None] * freq[None, :]).astype(np.float64)
    gamma = 1.0 - 2.0 ** (-5.0 - np.arange(H1, dtype=np.float64))
    i = np.arange(P, dtype=np.float64)
    both = np.stack([gamma[None, :] ** i[:, None], gamma[None, :] ** -i[:, None]], axis=1)
    def spread(t):
        t = t.reshape(TS, P, 1, 1, DH).transpose(1, 0, 2, 3, 4) * both[:, None, :, :, None]
        return np.ascontiguousarray(t.reshape(P, TS, 2 * D).astype(np.float32))
    cos = np.repeat(np.cos(angle), 2, axis=1)
    sin = np.stack([-np.sin(angle), np.sin(angle)], axis=2).reshape(T, DH)
    carry = np.zeros((P, KC, P))
    for h in range(H1):
        r = slice(h % 8 * DH, h % 8 * DH + DH)
        carry[r, h // 8, r] = gamma[h] ** P
    return spread(cos), spread(sin), carry.astype(np.float32)


_SHAPE = (NB, T, D)


def kernel(**inputs):
    import numpy as _np
    import concourse.bacc as _bacc
    from concourse import mybir as _mybir
    from concourse.bass_utils import run_bass_kernel_spmd as _run

    arrays = lay_out(inputs)
    nc = _bacc.Bacc("TRN2", target_bir_lowering=False, num_devices=1)
    args = {}
    for name, v in arrays.items():
        args[name] = nc.dram_tensor("in_" + name, v.shape, _mybir.dt.from_np(v.dtype), kind="ExternalInput").ap()
    out = nc.dram_tensor("out_x", (NB * T, D), F32, kind="ExternalOutput").ap()
    build(nc, args, out)
    r = _run(nc, [{"in_" + n: v for n, v in arrays.items()}], core_ids=[0])
    return r.results[0]["out_x"].reshape(_SHAPE)
```
